# Optimizing a Trainium2 kernel written in Bass

```python
import numpy as np
import jax
import jax.numpy as jnp

def _softmax(x, axis=-1):
    return jax.nn.softmax(x, axis=axis)

def _gelu(x):
    return jax.nn.gelu(x, approximate=True)

def _silu(x):
    return jax.nn.silu(x)

def _sigmoid(x):
    return jax.nn.sigmoid(x)

def _layernorm(x, axis=-1, eps=1e-05):
    m = jnp.mean(x, axis=axis, keepdims=True)
    v = jnp.var(x, axis=axis, keepdims=True)
    return (x - m) / jnp.sqrt(v + eps)

def _scatter_add(tgt, idx, src, axis=0):
    return tgt.at[idx].add(src)

def _segment_sum(src, seg, n):
    return jax.ops.segment_sum(src, seg, n)
kernel_name = 'mk_gnn_preln_d4_gnn_r32_6f862b'

def setup_inputs(seed: int=0):
    np.random.seed(seed)
    _w = jnp.asarray

    def _rec_inputs():
        import jax
        import jax.numpy as jnp
        _gk = jax.random.key(seed)
        x = -0.0002117 + 1 * jax.random.normal(jax.random.fold_in(_gk, 1), (3125, 256), jnp.float32)
        src = jax.random.randint(jax.random.fold_in(_gk, 2), (50000,), 0, 3125, jnp.int32)
        dst = jnp.minimum((3125 * jax.random.uniform(jax.random.fold_in(_gk, 3), (50000,)) ** 2.0).astype(jnp.int32), 99999)
        _o = jnp.argsort(dst, stable=True)
        src = src[_o]
        dst = dst[_o]
        edge_type_2 = jax.random.randint(jax.random.fold_in(_gk, 13), (50000,), 0, 2, jnp.int32)
        edge_type_8 = jax.random.randint(jax.random.fold_in(_gk, 14), (50000,), 0, 8, jnp.int32)
        return (x, src, dst, edge_type_2, edge_type_8)
    x, src, dst, edge_type_2, edge_type_8 = _rec_inputs()

    def _L0_gnn_setup():
        import jax, jax.numpy as jnp
        import numpy as np
        N = 3125
        E = 25000
        EMB = 256
        HID = 256
        EPS = 1e-05

        def _pool_max(h, edge_src, edge_dst):
            pooled = jax.ops.segment_max(h[edge_src], edge_dst, num_segments=N)
            cnt = jax.ops.segment_sum(jnp.ones((edge_dst.shape[0],), h.dtype), edge_dst, num_segments=N)
            return jnp.where((cnt > 0)[:, None], pooled, jnp.zeros((), h.dtype))

        def _layernorm(x, g, b):
            mu = jnp.mean(x, axis=-1, keepdims=True)
            var = jnp.mean(jnp.square(x - mu), axis=-1, keepdims=True)
            return (x - mu) * jax.lax.rsqrt(var + EPS) * g + b
        key = jax.random.key(seed)
        ks = jax.random.split(key, 12)
        s = 0.05
        return {'embeddings': jax.random.normal(ks[0], (N, EMB), jnp.float32), 'edge_src': jax.random.randint(ks[1], (E,), 0, N, jnp.int32), 'edge_dst': jax.random.randint(ks[2], (E,), 0, N, jnp.int32), 'Wp1': jax.random.normal(ks[3], (HID, EMB), jnp.float32) * s, 'bp1': jnp.zeros((HID,), jnp.float32), 'Wm1': jax.random.normal(ks[4], (HID, EMB + HID), jnp.float32) * s, 'bm1': jnp.zeros((HID,), jnp.float32), 'Wm2': jax.random.normal(ks[5], (HID, 2 * HID), jnp.float32) * s, 'bm2': jnp.zeros((HID,), jnp.float32), 'Wm3': jax.random.normal(ks[6], (HID, 2 * HID), jnp.float32) * s, 'bm3': jnp.zeros((HID,), jnp.float32), 'ln2_g': jnp.ones((HID,), jnp.float32), 'ln2_b': jnp.zeros((HID,), jnp.float32), 'ln3_g': jnp.ones((HID,), jnp.float32), 'ln3_b': jnp.zeros((HID,), jnp.float32)}
    _L0_gnn_all = _L0_gnn_setup()
    _L0_gnn_in = {k: v for k, v in _L0_gnn_all.items() if k in ('Wp1', 'bp1', 'Wm1', 'bm1', 'Wm2', 'bm2', 'Wm3', 'bm3', 'ln2_g', 'ln2_b', 'ln3_g', 'ln3_b')}
    del _L0_gnn_all

    def _L1_gnn_setup():
        import jax, jax.numpy as jnp
        import numpy as np
        N = 10000
        E = 10000
        D = 256
        L = 3
        key = jax.random.key(seed)
        ks = jax.random.split(key, 10)
        s = 1.0 / np.sqrt(D)
        x = jax.random.normal(ks[0], (N, D), dtype=jnp.float32)
        edges = jax.random.randint(ks[1], (2, E), 0, N, dtype=jnp.int32)
        w_in = jax.random.uniform(ks[2], (D, D), jnp.float32, -s, s)
        b_in = jax.random.uniform(ks[3], (D,), jnp.float32, -s, s)
        wq = jax.random.uniform(ks[4], (L, D, D), jnp.float32, -s, s)
        wk = jax.random.uniform(ks[5], (L, D, D), jnp.float32, -s, s)
        wv = jax.random.uniform(ks[6], (L, D, D), jnp.float32, -s, s)
        wp = jax.random.uniform(ks[7], (L, D, D), jnp.float32, -s, s)
        bp = jax.random.uniform(ks[8], (L, D), jnp.float32, -s, s)
        return {'x': x, 'edges': edges, 'w_in': w_in, 'b_in': b_in, 'wq': wq, 'wk': wk, 'wv': wv, 'wp': wp, 'bp': bp}
    _L1_gnn_all = _L1_gnn_setup()
    _L1_gnn_in = {k: v for k, v in _L1_gnn_all.items() if k in ('w_in', 'b_in', 'wq', 'wk', 'wv', 'wp', 'bp')}
    del _L1_gnn_all

    def _L2_gnn_setup():
        import jax, jax.numpy as jnp
        import numpy as np
        N_NODES = 10000
        N_EDGES = 10000
        D = 256
        D_OUT = 256
        NUM_REL = 2
        key = jax.random.key(seed)
        ks = jax.random.split(key, 16)
        s = 1.0 / np.sqrt(D)
        inp = {}
        inp['feat'] = jax.random.normal(ks[0], (N_NODES, D), dtype=jnp.float32)
        inp['src'] = jax.random.randint(ks[1], (N_EDGES,), 0, N_NODES, dtype=jnp.int32)
        inp['dst'] = jax.random.randint(ks[2], (N_EDGES,), 0, N_NODES, dtype=jnp.int32)
        inp['rel'] = jax.random.randint(ks[3], (N_EDGES,), 0, NUM_REL, dtype=jnp.int32)
        inp['W_rel'] = jax.random.normal(ks[4], (NUM_REL, D, D), dtype=jnp.float32) * s
        inp['b_rel'] = jax.random.normal(ks[5], (NUM_REL, D), dtype=jnp.float32) * s
        inp['W_ih'] = jax.random.normal(ks[6], (4 * D, D), dtype=jnp.float32) * s
        inp['b_ih'] = jax.random.normal(ks[7], (4 * D,), dtype=jnp.float32) * s
        inp['b_hh'] = jax.random.normal(ks[8], (4 * D,), dtype=jnp.float32) * s
        h = D // 2
        inp['W1'] = jax.random.normal(ks[9], (h, D), dtype=jnp.float32) * s
        inp['b1'] = jax.random.normal(ks[10], (h,), dtype=jnp.float32) * s
        inp['W2'] = jax.random.normal(ks[11], (h, h), dtype=jnp.float32) * (1.0 / np.sqrt(h))
        inp['b2'] = jax.random.normal(ks[12], (h,), dtype=jnp.float32) * (1.0 / np.sqrt(h))
        inp['W3'] = jax.random.normal(ks[13], (D_OUT, h), dtype=jnp.float32) * (1.0 / np.sqrt(h))
        inp['b3'] = jax.random.normal(ks[14], (D_OUT,), dtype=jnp.float32) * (1.0 / np.sqrt(h))
        return inp
    _L2_gnn_all = _L2_gnn_setup()
    _L2_gnn_in = {k: v for k, v in _L2_gnn_all.items() if k in ('W_rel', 'b_rel', 'W_ih', 'b_ih', 'b_hh', 'W1', 'b1', 'W2', 'b2', 'W3', 'b3')}
    del _L2_gnn_all

    def _L3_gnn_setup():
        import jax, jax.numpy as jnp
        import numpy as np
        N = 50000
        E = 25000
        DIN = 256
        DOUT = 256
        R = 8
        key = jax.random.key(seed)
        k1, k2, k3, k4, k5, k6 = jax.random.split(key, 6)
        h = jax.random.normal(k1, (N, DIN), dtype=jnp.float32)
        weight = jax.random.normal(k2, (R, DIN, DOUT), dtype=jnp.float32) * (1.0 / np.sqrt(DIN))
        sl_w = jax.random.normal(k3, (DOUT, DIN), dtype=jnp.float32) * (1.0 / np.sqrt(DIN))
        sl_b = jax.random.normal(k4, (DOUT,), dtype=jnp.float32) * 0.01
        edge_index = jax.random.randint(k5, (2, E), 0, N, dtype=jnp.int32)
        edge_type = jax.random.randint(k6, (E,), 0, R, dtype=jnp.int32)
        return {'h': h, 'weight': weight, 'sl_w': sl_w, 'sl_b': sl_b, 'edge_index': edge_index, 'edge_type': edge_type, 'num_nodes': N}
    _L3_gnn_all = _L3_gnn_setup()
    _L3_gnn_in = {k: v for k, v in _L3_gnn_all.items() if k in ('weight', 'sl_w', 'sl_b')}
    del _L3_gnn_all
    return {'x': x, 'src': src, 'dst': dst, 'edge_type_2': edge_type_2, 'edge_type_8': edge_type_8, 'L0_gnn_Wp1': _L0_gnn_in['Wp1'], 'L0_gnn_bp1': _L0_gnn_in['bp1'], 'L0_gnn_Wm1': _L0_gnn_in['Wm1'], 'L0_gnn_bm1': _L0_gnn_in['bm1'], 'L0_gnn_Wm2': _L0_gnn_in['Wm2'], 'L0_gnn_bm2': _L0_gnn_in['bm2'], 'L0_gnn_Wm3': _L0_gnn_in['Wm3'], 'L0_gnn_bm3': _L0_gnn_in['bm3'], 'L0_gnn_ln2_g': _L0_gnn_in['ln2_g'], 'L0_gnn_ln2_b': _L0_gnn_in['ln2_b'], 'L0_gnn_ln3_g': _L0_gnn_in['ln3_g'], 'L0_gnn_ln3_b': _L0_gnn_in['ln3_b'], 'L1_gnn_w_in': _L1_gnn_in['w_in'], 'L1_gnn_b_in': _L1_gnn_in['b_in'], 'L1_gnn_wq': _L1_gnn_in['wq'], 'L1_gnn_wk': _L1_gnn_in['wk'], 'L1_gnn_wv': _L1_gnn_in['wv'], 'L1_gnn_wp': _L1_gnn_in['wp'], 'L1_gnn_bp': _L1_gnn_in['bp'], 'L2_gnn_W_rel': _L2_gnn_in['W_rel'], 'L2_gnn_b_rel': _L2_gnn_in['b_rel'], 'L2_gnn_W_ih': _L2_gnn_in['W_ih'], 'L2_gnn_b_ih': _L2_gnn_in['b_ih'], 'L2_gnn_b_hh': _L2_gnn_in['b_hh'], 'L2_gnn_W1': _L2_gnn_in['W1'], 'L2_gnn_b1': _L2_gnn_in['b1'], 'L2_gnn_W2': _L2_gnn_in['W2'], 'L2_gnn_b2': _L2_gnn_in['b2'], 'L2_gnn_W3': _L2_gnn_in['W3'], 'L2_gnn_b3': _L2_gnn_in['b3'], 'L3_gnn_weight': _L3_gnn_in['weight'], 'L3_gnn_sl_w': _L3_gnn_in['sl_w'], 'L3_gnn_sl_b': _L3_gnn_in['sl_b']}

def reference(x, src, dst, edge_type_2, edge_type_8, L0_gnn_Wp1, L0_gnn_bp1, L0_gnn_Wm1, L0_gnn_bm1, L0_gnn_Wm2, L0_gnn_bm2, L0_gnn_Wm3, L0_gnn_bm3, L0_gnn_ln2_g, L0_gnn_ln2_b, L0_gnn_ln3_g, L0_gnn_ln3_b, L1_gnn_w_in, L1_gnn_b_in, L1_gnn_wq, L1_gnn_wk, L1_gnn_wv, L1_gnn_wp, L1_gnn_bp, L2_gnn_W_rel, L2_gnn_b_rel, L2_gnn_W_ih, L2_gnn_b_ih, L2_gnn_b_hh, L2_gnn_W1, L2_gnn_b1, L2_gnn_W2, L2_gnn_b2, L2_gnn_W3, L2_gnn_b3, L3_gnn_weight, L3_gnn_sl_w, L3_gnn_sl_b):
    import jax
    import jax.numpy as jnp

    def _L0_gnn_ref(embeddings, edge_src, edge_dst, Wp1, bp1, Wm1, bm1, Wm2, bm2, Wm3, bm3, ln2_g, ln2_b, ln3_g, ln3_b):
        import jax, jax.numpy as jnp
        import numpy as np
        N = 3125
        E = 25000
        EMB = 256
        HID = 256
        EPS = 1e-05

        def _pool_max(h, edge_src, edge_dst):
            pooled = jax.ops.segment_max(h[edge_src], edge_dst, num_segments=N)
            cnt = jax.ops.segment_sum(jnp.ones((edge_dst.shape[0],), h.dtype), edge_dst, num_segments=N)
            return jnp.where((cnt > 0)[:, None], pooled, jnp.zeros((), h.dtype))

        def _layernorm(x, g, b):
            mu = jnp.mean(x, axis=-1, keepdims=True)
            var = jnp.mean(jnp.square(x - mu), axis=-1, keepdims=True)
            return (x - mu) * jax.lax.rsqrt(var + EPS) * g + b
        h1 = jax.nn.relu(embeddings @ Wp1.T + bp1)
        p1 = _pool_max(h1, edge_src, edge_dst)
        x = jax.nn.relu(jnp.concatenate([embeddings, p1], axis=1) @ Wm1.T + bm1)
        p2 = _pool_max(x, edge_src, edge_dst)
        y2 = jax.nn.relu(jnp.concatenate([x, p2], axis=1) @ Wm2.T + bm2)
        x = _layernorm(y2 + x, ln2_g, ln2_b)
        p3 = _pool_max(x, edge_src, edge_dst)
        y3 = jax.nn.relu(jnp.concatenate([x, p3], axis=1) @ Wm3.T + bm3)
        x = _layernorm(y3 + x, ln3_g, ln3_b)
        return x

    def _L1_gnn_ref(x, edges, w_in, b_in, wq, wk, wv, wp, bp):
        import jax, jax.numpy as jnp
        import numpy as np
        N = 10000
        E = 10000
        D = 256
        L = 3
        n, d = x.shape
        src, dst = (edges[0], edges[1])
        scale = 1.0 / jnp.sqrt(jnp.asarray(d, x.dtype))
        h = jax.nn.relu(x @ w_in + b_in)
        for l in range(wq.shape[0]):
            q = h @ wq[l]
            k = h @ wk[l]
            v = h @ wv[l]
            scores = jnp.sum(q[dst] * k[src], axis=1) * scale
            mx = jax.ops.segment_max(scores, dst, num_segments=n)
            exp = jnp.exp(jnp.clip(scores - mx[dst], -50.0, 50.0))
            ssum = jax.ops.segment_sum(exp, dst, num_segments=n)
            alpha = exp / (ssum[dst] + 1e-09)
            alpha = jnp.nan_to_num(alpha, nan=0.0, posinf=0.0, neginf=0.0)
            msg = v[src] * alpha[:, None]
            agg = jax.ops.segment_sum(msg, dst, num_segments=n)
            h = jax.nn.relu(agg @ wp[l] + bp[l] + h)
        return h

    def _L2_gnn_ref(feat, src, dst, rel, W_rel, b_rel, W_ih, b_ih, b_hh, W1, b1, W2, b2, W3, b3):
        import jax, jax.numpy as jnp
        import numpy as np
        N_NODES = 10000
        N_EDGES = 10000
        D = 256
        D_OUT = 256
        NUM_REL = 2
        n_nodes = feat.shape[0]
        S = feat[src]

        def edge_nn(x, W, b):
            h = jax.nn.relu(x @ W.T + b)
            return jax.nn.relu(h @ W.T + b)
        msgs = jnp.zeros_like(S)
        for r in range(W_rel.shape[0]):
            msgs = jnp.where((rel == r)[:, None], edge_nn(S, W_rel[r], b_rel[r]), msgs)
        agg = jax.ops.segment_sum(msgs, dst, num_segments=n_nodes)
        gates = agg @ W_ih.T + b_ih + b_hh
        i, f, g, o = jnp.split(gates, 4, axis=-1)
        c = jax.nn.sigmoid(i) * jnp.tanh(g)
        hn = jax.nn.sigmoid(o) * jnp.tanh(c)
        x = jax.nn.relu(hn @ W1.T + b1)
        x = jax.nn.relu(x @ W2.T + b2)
        return x @ W3.T + b3

    def _L3_gnn_ref(h, weight, sl_w, sl_b, edge_index, edge_type, num_nodes):
        import jax, jax.numpy as jnp
        import numpy as np
        N = 50000
        E = 25000
        DIN = 256
        DOUT = 256
        R = 8
        src, dst = (edge_index[0], edge_index[1])
        hW = jnp.einsum('nd,rde->rne', h, weight)
        msg = hW[edge_type, src]
        m = jax.ops.segment_sum(msg, dst, num_segments=num_nodes)
        deg = jax.ops.segment_sum(jnp.ones_like(dst, dtype=h.dtype), dst, num_segments=num_nodes)
        deg = jnp.maximum(deg, 1.0)[:, None]
        return h @ sl_w.T + sl_b + m / deg
    edge_index = jnp.stack([src, dst])
    h = jnp.maximum(_layernorm(x, axis=-1), 0.0)
    x = x + _L0_gnn_ref(h, src, dst, L0_gnn_Wp1, L0_gnn_bp1, L0_gnn_Wm1, L0_gnn_bm1, L0_gnn_Wm2, L0_gnn_bm2, L0_gnn_Wm3, L0_gnn_bm3, L0_gnn_ln2_g, L0_gnn_ln2_b, L0_gnn_ln3_g, L0_gnn_ln3_b)
    h = jnp.maximum(_layernorm(x, axis=-1), 0.0)
    x = x + _L1_gnn_ref(h, edge_index, L1_gnn_w_in, L1_gnn_b_in, L1_gnn_wq, L1_gnn_wk, L1_gnn_wv, L1_gnn_wp, L1_gnn_bp)
    h = jnp.maximum(_layernorm(x, axis=-1), 0.0)
    x = x + _L2_gnn_ref(h, src, dst, edge_type_2, L2_gnn_W_rel, L2_gnn_b_rel, L2_gnn_W_ih, L2_gnn_b_ih, L2_gnn_b_hh, L2_gnn_W1, L2_gnn_b1, L2_gnn_W2, L2_gnn_b2, L2_gnn_W3, L2_gnn_b3)
    h = jnp.maximum(_layernorm(x, axis=-1), 0.0)
    x = x + _L3_gnn_ref(h, L3_gnn_weight, L3_gnn_sl_w, L3_gnn_sl_b, edge_index, edge_type_8, 3125)
    return x

_drawn_inputs = setup_inputs


def setup_inputs(seed=0):
    import zlib

    import numpy as np

    out = dict(_drawn_inputs(seed))
    spreads = {'L0_gnn_bp1': (0.0, 0.1),
     'L0_gnn_bm1': (0.0, 0.1),
     'L0_gnn_bm2': (0.0, 0.1),
     'L0_gnn_bm3': (0.0, 0.1),
     'L0_gnn_ln2_g': (1.0, 0.2),
     'L0_gnn_ln2_b': (0.0, 0.1),
     'L0_gnn_ln3_g': (1.0, 0.2),
     'L0_gnn_ln3_b': (0.0, 0.1)}
    factors = {'L1_gnn_b_in': 3.83,
     'L1_gnn_wq': 28.344,
     'L1_gnn_wk': 27.923,
     'L2_gnn_b_rel': 2.941,
     'L2_gnn_b_ih': 24.986,
     'L2_gnn_b_hh': 8.0,
     'L2_gnn_b1': 3.089,
     'L3_gnn_sl_b': 8.0}
    for name, (base, spread) in spreads.items():
        noise = np.random.default_rng([zlib.crc32(name.encode()), seed]).standard_normal(out[name].shape)
        drawn = base * np.exp(spread * noise) if base else spread * noise
        out[name] = jnp.asarray(drawn.astype(out[name].dtype))
    for name, factor in factors.items():
        out[name] = (out[name] * factor).astype(out[name].dtype)
    return out
```

```python
from contextlib import ExitStack

import concourse.bass as bass
from concourse import mybir

F32 = mybir.dt.float32
BF16 = mybir.dt.bfloat16
I32 = mybir.dt.int32
ALU = mybir.AluOpType
ACT = mybir.ActivationFunctionType
AX_X = mybir.AxisListType.X

P = 128
N = 3125
E = 50000
D = 256
K2 = D // P
TILES = -(-E // P)
BLOCKS = -(-N // P)
NODES = BLOCKS * P
RING = 8
UNROLL = 2 * RING
STEPS = -(-(TILES + BLOCKS - 1) // UNROLL) * UNROLL
SPAD = 512
CHUNKS = SPAD // P
assert TILES <= SPAD and STEPS <= SPAD
NCOL = 400
NGROUP = NODES // NCOL
TRS = 5
ROW = D + 1
EPS = 1e-5
RESET = -2e38
LOW = -1e30
SM_EPS = 1e-9
LAYERS = 3
FAR = 1e6
FUNCS = {"Relu": ACT.Relu, "Copy": ACT.Copy, "Sqrt": ACT.Sqrt, "Identity": ACT.Identity,
         "Sigmoid": ACT.Sigmoid, "Tanh": ACT.Tanh}
REL2, REL8 = 2, 8

GROUPS = [
    [("Wp1", 2, 256), ("Wm1", 4, 256), ("Wm2", 4, 256), ("Wm3", 4, 256)],
    [("w_in", 2, 256)],
    [("wq", 2, 256), ("wk", 2, 256), ("wv", 2, 256), ("wp", 2, 256)],
    [("rel0", 2, 256), ("rel1", 2, 256), ("ih_i", 2, 256), ("ih_g", 2, 256), ("ih_o", 2, 256),
     ("W1", 2, 128), ("W2", 1, 128), ("W3", 1, 256)],
    [("typ", 2, REL8 * 256), ("self", 2, 256)],
]
BIASES = ["bp1", "bm1", "bm2", "bm3", "ln2_g", "ln2_b", "ln3_g", "ln3_b", "b_in", "bp_0", "bp_1", "bp_2",
          "br_0", "br_1", "bi", "bg", "bo", "hi", "hg", "ho", "b1", "b2", "b3", "slb"]


def plan():
    s = [("steps",), ("load", 0, 0)]
    s += ln("X", "B", "C") + [("relu_mul", "H", "B")]
    s += [("dense", "Wp1", ["H"], "B", "Relu", "bp1"), ("table", "B")]
    s += [("maxpool",), ("untranspose", None, "C"), ("dense", "Wm1", ["H", "C"], "B", "Relu", "bm1"), ("table", "B")]
    s += [("maxpool",), ("untranspose", None, "C"), ("dense", "Wm2", ["B", "C"], "H", "Relu", "bm2"), ("add", "H", "B")]
    s += ln("H", "B", "C") + [("affine", "B", "ln2_g", "ln2_b"), ("table", "B")]
    s += [("maxpool",), ("untranspose", None, "C"), ("dense", "Wm3", ["B", "C"], "H", "Relu", "bm3"), ("add", "H", "B")]
    s += ln("H", "B", "C") + [("affine", "B", "ln3_g", "ln3_b"), ("add", "X", "B"), ("load", 1, 0)]
    s += ln("X", "B", "C") + [("relu_mul", "H", "B")]
    s += [("dense", "w_in", ["H"], "B", "Relu", "b_in"), ("table", "B")]
    for layer in range(LAYERS):
        s += [("load", 2, layer), ("fold",), ("dense", "Wqk", ["B"], "C", "Scale", None), ("split", "C")]
        s += [("score",), ("softmax",), ("attend",), ("untranspose", "ssum", "C")]
        s += [("dense", "Wvp", ["C"], "H", "Identity", f"bp_{layer}"), ("add_relu", "B", "H")]
        if layer < LAYERS - 1:
            s += [("table", "B")]
    s += [("add", "X", "B"), ("load", 3, 0)]
    s += ln("X", "B", "C") + [("relu_mul", "H", "B")]
    for r in range(REL2):
        s += [("dense", f"rel{r}", ["H"], "B", "Relu", f"br_{r}"), ("dense", f"rel{r}", ["B"], "C", "Relu", f"br_{r}"),
              ("table", "C", "rel", r)]
    s += [("sum", "rel"), ("untranspose", None, "C")]
    s += [("dense", "ih_i", ["C"], "B", "Sigmoid", "bi"), ("dense", "ih_g", ["C"], "H", "Tanh", "bg"), ("mul", "B", "H")]
    s += [("tanh", "B"), ("dense", "ih_o", ["C"], "H", "Sigmoid", "bo"), ("mul", "H", "B")]
    s += [("dense", "W1", ["H"], "B", "Relu", "b1"), ("dense", "W2", ["B"], "C", "Relu", "b2"),
          ("dense", "W3", ["C"], "B", "Identity", "b3"), ("add", "X", "B"), ("load", 4, 0)]
    s += ln("X", "B", "C") + [("relu_mul", "H", "B")]
    s += [("table8", "H"), ("dense", "self", ["H"], "B", "Identity", "slb"), ("add", "X", "B")]
    s += [("sum", "typ"), ("untranspose", "deg", "C"), ("add", "X", "C"), ("store",)]
    return s


def ln(src, centred, squares):
    return [("dense", "mean", [src], "M", "Copy", None), ("centre", src, centred, squares),
            ("dense", "mean", [squares], "M", "Sqrt", None), ("recip",)]


def gnn_kernel(nc, edges, xT, weights, biases, out, table, table_rel, table_typ, spill, resets):
    PLAN = plan()
    FIRST = {kind: [n for n, s in enumerate(PLAN) if s[0] == kind][0] for kind in {s[0] for s in PLAN}}
    with ExitStack() as ctx:
        def sb(name, shape, dt=F32):
            return ctx.enter_context(nc.sbuf_tensor(name, shape, dt))

        def sem(name):
            return ctx.enter_context(nc.semaphore(name))

        X = sb("X", [P, K2, NODES])
        H = sb("H", [P, K2, NODES])
        B = sb("B", [P, K2, NODES])
        C = sb("C", [P, K2, NODES])
        AM = sb("AM", [P, BLOCKS * ROW + NODES])
        A = AM[:, 0:BLOCKS * ROW].rearrange("p (b r) -> p b r", r=ROW)
        M = AM[:, BLOCKS * ROW:].rearrange("p (o n) -> p o n", o=1)
        G = AM[:, 0:BLOCKS * 3 * D // 2].bitcast(BF16).rearrange("p (b s d) -> p b s d", s=3, d=D)
        BIG = {"X": X, "H": H, "B": B, "C": C, "M": M}
        def window(h, c):
            return C[:, c, h * 4 * P:(h + 1) * 4 * P]

        W = sb("W", [P, max(sum(k * m for _, k, m in g) for g in GROUPS)])
        Wfold = sb("Wfold", [P, 2, K2, D])
        bias = sb("bias", [P, len(BIASES), K2])
        ring = sb("ring", [P, RING, ROW])
        work = sb("work", [P, 2 * TRS * D])
        stage_in = work[:, 0:TRS * D].rearrange("p (k d) -> p k d", d=D)
        stage_out = work[:, TRS * D:].rearrange("p (k d) -> p k d", d=D)
        ohot = work[:, 0:RING * P].rearrange("p (k e) -> p k e", e=P)
        ohot_bf = work[:, 0:RING * P // 2].bitcast(BF16).rearrange("p (k e) -> p k e", e=P)
        back = work[:, 1024:1536].rearrange("p (k d) -> p k d", d=D)
        junk = work[:, 1536:1792]
        resetw = work[:, 1792:2304].bitcast(BF16).rearrange("p (h e) -> p h e", h=2)
        ohT = work[:, 2304:2432].bitcast(BF16).rearrange("p (k e) -> p k e", e=P)
        ident = sb("ident", [P, P])
        identb = sb("identb", [P, P], BF16)
        ones = sb("ones", [P, P])
        meanw = sb("meanw", [P, K2, P])
        epsc = sb("epsc", [P, 1])
        iota_row = sb("iota_row", [P, P])
        idx = {n: sb(f"idx_{n}", [P, SPAD], I32) for n in ("src", "rel", "typ")}
        idx_now = sb("idx_now", [P, 2, RING], I32)
        dloc = sb("dloc", [P, SPAD])
        eloc = sb("eloc", [P, SPAD])
        score = sb("score", [P, SPAD])
        score8 = sb("score8", [P, RING])
        rst_row = sb("rst_row", [P, CHUNKS, P])
        end_row = sb("end_row", [P, CHUNKS, P])
        val_row = sb("val_row", [P, CHUNKS, P])
        blk = sb("blk", [1, SPAD], I32)
        rowhas = sb("rowhas", [1, 2, SPAD])
        carry = sb("carry", [1, SPAD + 2])
        carry_col = sb("carry_col", [P, CHUNKS])
        tail = sb("tail", [P, CHUNKS])
        rcol = sb("rcol", [P, BLOCKS])
        sm_a = stage_in[:, 0:2, :].rearrange("p a d -> p (a d)").rearrange("p (c e) -> p c e", e=P)
        sm_b = stage_in[:, 2:4, :].rearrange("p a d -> p (a d)").rearrange("p (c e) -> p c e", e=P)
        sm_c = stage_out[:, 0:2, :].rearrange("p a d -> p (a d)").rearrange("p (c e) -> p c e", e=P)
        PS = ctx.enter_context(nc.psum_tensor("PS", [P, 8, 512], F32))
        PSB = PS[:].rearrange("p b e -> p (b e)").bitcast(BF16).rearrange("p (b e) -> p b e", b=8)


        flatB = B[:].rearrange("p c n -> p (c n)")
        flatC = C[:].rearrange("p c n -> p (c n)")
        flatH = H[:].rearrange("p c n -> p (c n)")
        edge_int = flatB[:, 0:6 * SPAD].bitcast(I32).rearrange("p (a c e) -> p a c e", a=6, e=P)
        scratch = flatB[:, 6 * SPAD:7 * SPAD]
        counts = flatB[:, 7 * SPAD:7 * SPAD + 32]
        small = flatB[:, 7 * SPAD + 32:7 * SPAD + 224].rearrange("p (j b) -> p j b", b=32)
        bound = flatB[:, 7 * SPAD + 224:7 * SPAD + 224 + BLOCKS + 1]
        ge2 = flatB[:, 7 * SPAD + 256:7 * SPAD + 256 + BLOCKS]
        bound_i = flatB[:, 7 * SPAD + 288:7 * SPAD + 288 + 2 * (BLOCKS + 1)].bitcast(I32).rearrange("p (a b) -> p a b", a=2)
        where = flatB[:, 7 * SPAD + 352:7 * SPAD + 352 + 2 * CHUNKS].rearrange("p (a c) -> p a c", a=2)
        has_col = flatB[:, 7 * SPAD + 368:7 * SPAD + 368 + 2 * CHUNKS].rearrange("p (a c) -> p a c", a=2)
        attr = flatC[:, 0:7 * SPAD].rearrange("p (a s) -> p a s", a=7)
        diag = flatH[:, 0:2 * SPAD].rearrange("p (a s) -> p a s", a=2)
        row128 = flatH[:, 2 * SPAD:3 * SPAD]
        pick = flatH[:, 3 * SPAD:7 * SPAD].rearrange("p (c s) -> p c s", c=CHUNKS)
        reset_flat = flatH[:, 7 * SPAD:7 * SPAD + SPAD // 2].bitcast(BF16)
        reset_bf = reset_flat.rearrange("p (c e) -> p c e", e=P)

        def flat_of(rows):
            return (rows if isinstance(rows, bass.AP) else rows[:]).rearrange("p c e -> p (c e)")

        def wide(k):
            base, at = (flatB, k) if k < 3 else (flatC, k - 3)
            return base[:, at * REL8 * D:(at + 1) * REL8 * D]

        wview = {}
        for g in GROUPS:
            at = 0
            for name, k, m in g:
                wview[name] = W[:, at:at + k * m].rearrange("p (k m) -> p k m", k=k)
                at += k * m
        wview["Wqk"] = Wfold[:, 0]
        wview["Wvp"] = Wfold[:, 1]
        wview["mean"] = meanw

        def bias_of(name, c):
            return bias[:, BIASES.index(name), c:c + 1]

        stage_done = sem("stage_done")
        consts = sem("consts")
        vec = sem("vec")
        loaded = sem("loaded")
        to_pe = sem("to_pe")
        from_pe = sem("from_pe")
        rows_ready = sem("rows_ready")
        arg_ready = sem("arg_ready")
        exp_done = sem("exp_done")
        half_ready = sem("half_ready")
        mm_done = sem("mm_done")
        mm_out = sem("mm_out")
        tr_in = sem("tr_in")
        tr_done = sem("tr_done")
        tr_out = sem("tr_out")
        tabled = [sem(f"tabled{k}") for k in range(TRS)]
        gathered = [sem(f"gathered{k}") for k in range(RING)]
        reloaded = [sem(f"reloaded{k}") for k in range(RING)]
        slot_free = sem("slot_free")
        spilled = [sem(f"spilled{k}") for k in range(RING)]
        passed = sem("passed")
        staged = sem("staged")
        reset_in = [sem(f"reset_in{h}") for h in range(2)]
        win_max = sem("win_max")
        back_tr = sem("back_tr")
        back_in = sem("back_in")
        oh_made = sem("oh_made")
        oh_tr = sem("oh_tr")
        oht_in = sem("oht_in")
        expanded = sem("expanded")
        summed = sem("summed")
        added = sem("added")
        moved = sem("moved")
        stored = sem("stored")

        block = ctx.enter_context(nc.Block())

        def before(n, kinds):
            return sum(1 for s in PLAN[:n] if s[0] in kinds)

        def groups_before(n):
            return (sum(NGROUP * halves_out(s) for s in PLAN[:n] if s[0] == "dense")
                    + 4 * BLOCKS * before(n, ("table8",)))

        def halves_out(s):
            return 1 if s[1] in ("mean", "W1", "W2") else 2

        TR = ("table", "untranspose", "split")
        TR8 = TR + ("table8",)
        EDGE = ("maxpool", "score", "attend", "sum")
        GATHERS = ("maxpool", "score", "sum")
        SUMS = ("maxpool", "attend", "sum")
        split_step = sem("split_step")

        def pe_hands(n):
            return 4 * before(n, ("steps",)) + before(n, ("fold",)) + 6 * before(n, ("softmax",))

        def dve_hands(n):
            return 4 * before(n, ("steps",)) + 5 * before(n, ("softmax",))

        def one(rows, at):
            return rows[bass.ds(at, 1)].rearrange("o p d -> (o p) d")

        def begin(eng, n):
            if n:
                eng.wait_ge(stage_done, n)

        def block_regs(eng, s, count=4):
            regs = nc.values_load_multi_w_load_instructions(
                blk[0:1, bass.ds(s, count)], engines=(eng.engine,), min_val=0, max_val=BLOCKS - 1,
                skip_runtime_bounds_check_because="the table is cut to the last block")[1]
            return regs

        @block.gpsimd
        def _(pool):
            pool.memset(ones[:], 1.0)
            pool.memset(meanw[:], 1.0 / D)
            pool.memset(epsc[:], EPS)
            pool.memset(score[:], 0.0)
            pool.memset(carry[:], LOW)
            pool.memset(ident[:], 0.0).then_inc(consts, 1)
            pool.iota(iota_row[:], pattern=[[1, P]], base=0, channel_multiplier=0,
                      allow_small_or_imprecise_dtypes=True)
            pool.iota(tail[:], pattern=[[P, CHUNKS]], base=0, channel_multiplier=1,
                      allow_small_or_imprecise_dtypes=True)
            pool.wait_ge(consts, 1)
            pool.affine_select(out=ident[:], in_=ident[:], compare_op=ALU.not_equal, fill=1.0, base=0,
                               pattern=[[-1, P]], channel_multiplier=1).then_inc(consts, 1)
            pool.wait_ge(consts, 2)
            pool.tensor_copy(identb[:], ident[:]).then_inc(consts, 1)
            for n, s in enumerate(PLAN):
                if s[0] not in ("maxpool", "score", "sum"):
                    continue
                begin(pool, n)
                gathers = before(n, ("maxpool", "score", "sum")) * STEPS
                uses = before(n, EDGE) * STEPS
                spills = 1 + before(n, ("score",)) * (STEPS // RING)
                src = {"rel": table_rel, "typ": table_typ}.get(s[-1], table)
                ids = idx[s[-1]] if s[0] == "sum" else idx["src"]
                with pool.Fori(0, STEPS // UNROLL) as i:
                    for h in range(2):
                        pool.wait_ge(slot_free, i * UNROLL + (uses + h * RING + 1))
                        pool.tensor_copy(idx_now[:, h, :], ids[:, bass.ds(i * UNROLL + h * RING, RING)]).then_inc(staged, 1)
                        pool.wait_ge(staged, i * 2 + (gathers // RING + h + 1))
                        for k in range(RING):
                            pool.wait_ge(slot_free, i * UNROLL + (uses + h * RING + k + 1))
                            if s[0] == "score":
                                pool.wait_ge(spilled[k], i * 32 + 16 * (spills + h))
                            pool.sem_inc(passed, 1)
                            pool.indirect_dma_start(
                                ring[:, k, 0:D], None, src,
                                bass.IndirectOffsetOnAxis(ap=idx_now[:, h, k:k + 1], axis=0)).then_inc(gathered[k], 16)


        @block.sync
        def _(sp):
            for n, s in enumerate(PLAN):
                if s[0] == "steps":
                    for a in range(6):
                        sp.dma_start(edge_int[:, a], edges[a].rearrange("(c p e) -> p c e", c=CHUNKS, e=P)).then_inc(loaded, 16)
                    sp.dma_start(bias[:], biases).then_inc(loaded, 16)
                    sp.dma_start(X[:], xT).then_inc(loaded, 16)
                    for k in range(TRS):
                        sp.dma_start(spill[0, k:k + 1, 0:1], biases[0:1, 0, 0:1]).then_inc(tabled[k], 16)
                    for k in range(RING):
                        sp.dma_start(spill[1, k:k + 1, 0:1], biases[0:1, 0, 0:1]).then_inc(spilled[k], 16)
                    for credit in tabled + spilled:
                        sp.wait_ge(credit, 16)
                    sp.wait_ge(rows_ready, 1)
                    sp.dma_start(resets.rearrange("(c q) e -> q c e", q=P), reset_bf).then_inc(stored, 16)
                    sp.wait_ge(stored, 16)
                    sp.wait_ge(rows_ready, 2)
                    sp.wait_ge(loaded, 16 * 8)
                    sp.sem_inc(stage_done, 1)
                elif s[0] == "load":
                    begin(sp, n)
                    at = 16 * (8 + before(n, ("load",)))
                    width = sum(k * m for _, k, m in GROUPS[s[1]])
                    sp.dma_start(W[:, 0:width], weights[s[1]][s[2]]).then_inc(loaded, 16)
                    sp.wait_ge(loaded, at + 16)
                    sp.sem_inc(stage_done, 1)
                elif s[0] == "table":
                    begin(sp, n)
                    u = before(n, TR) * BLOCKS
                    t = before(n, ("table",))
                    to = table if len(s) == 2 else table_rel[s[3] * NODES:(s[3] + 1) * NODES, :]
                    rows = to.rearrange("(b p) d -> b p d", p=P)
                    with sp.Fori(0, BLOCKS // TRS) as i:
                        for k in range(TRS):
                            sp.wait_ge(tr_out, i * TRS + (u + k + 1 + TRS))
                            sp.dma_start(one(rows, i * TRS + k), stage_out[:, k, :]).then_inc(tabled[k], 16)
                    for k in range(TRS):
                        sp.wait_ge(tabled[k], 16 * (1 + (t + 1) * (BLOCKS // TRS)))
                    sp.sem_inc(stage_done, 1)
                elif s[0] == "table8":
                    begin(sp, n)
                    g0 = groups_before(n)
                    t = before(n, ("table",)) * (BLOCKS // TRS)
                    rows = table_typ.rearrange("(b p r) d -> b p (r d)", p=P, r=REL8)
                    with sp.Fori(0, BLOCKS // TRS) as i:
                        for k in range(TRS):
                            sp.wait_ge(mm_out, i * (4 * TRS) + (g0 + 4 * k + 4 + 4))
                            sp.dma_start(one(rows, i * TRS + k), wide(k)).then_inc(tabled[k], 16)
                    for k in range(TRS):
                        sp.wait_ge(tabled[k], 16 * (1 + t + BLOCKS // TRS))
                    sp.sem_inc(stage_done, 1)
                elif s[0] == "maxpool":
                    begin(sp, n)
                    m = before(n, ("maxpool",)) * (STEPS // 4)
                    rows = resets.rearrange("(g a) e -> g (a e)", a=4)
                    with sp.Fori(0, STEPS // 8) as i:
                        for h in range(2):
                            sp.wait_ge(win_max, i * 2 + (m + h + 1))
                            sp.dma_start(resetw[:, h, :], rows[bass.ds(i * 2 + h, 1), :].to_broadcast([P, 4 * P]))\
                              .then_inc(reset_in[h], 16)
                elif s[0] == "score":
                    begin(sp, n)
                    g0 = before(n, GATHERS) * (STEPS // RING)
                    with sp.Fori(0, STEPS // RING) as i:
                        for k in range(RING):
                            sp.wait_ge(gathered[k], i * 16 + 16 * (g0 + 1))
                            sp.dma_start(one(spill, i * RING + k), ring[:, k, 0:D]).then_inc(spilled[k], 16)
                    for k in range(RING):
                        sp.wait_ge(spilled[k], 16 * (1 + (before(n, ("score",)) + 1) * (STEPS // RING)))
                    sp.wait_ge(moved, (before(n, ("score",)) + 1) * (STEPS // RING) + 1)
                    sp.sem_inc(stage_done, 1)
                elif s[0] == "attend":
                    begin(sp, n)
                    u = before(n, EDGE) * STEPS
                    with sp.Fori(0, STEPS // RING) as i:
                        for k in range(RING):
                            sp.wait_ge(slot_free, i * RING + (u + k + 1))
                            sp.dma_start(ring[:, k, 0:D], one(spill, i * RING + k)).then_inc(reloaded[k], 16)
                elif s[0] == "store":
                    begin(sp, n)
                    sp.dma_start(out, X[:, :, 0:N]).then_inc(stored, 16)
                    sp.wait_ge(stored, 32)

        @block.scalar
        def _(act):
            for n, s in enumerate(PLAN):
                if s[0] == "dense":
                    _, w, ins, to, func, b = s
                    halves = halves_out(s)
                    g0 = groups_before(n)
                    dst = BIG[to]
                    with act.Fori(0, NGROUP // 2) as i:
                        for j in range(2 * halves):
                            cols = bass.ds(i * (2 * NCOL) + (j // halves) * NCOL, NCOL)
                            bank = (j if halves == 2 else j)
                            act.wait_ge(mm_done, i * (2 * halves) + (g0 + j + 1))
                            more = {}
                            if func == "Scale":
                                more["scale"] = float(D) ** -0.5
                            elif func == "Sqrt":
                                more["bias"] = epsc[:]
                            elif b:
                                more["bias"] = bias_of(b, j % halves)
                            fn = ACT.Copy if func == "Scale" else FUNCS[func]
                            nc.scalar.activation(dst[:, j % halves, cols], PS[:, bank, 0:NCOL], fn, **more).then_inc(mm_out, 1)
                    act.wait_ge(mm_out, g0 + NGROUP * halves + 4)
                    act.sem_inc(stage_done, 1)
                elif s[0] in TR:
                    begin(act, n)
                    u = before(n, TR8) * BLOCKS
                    with act.Fori(0, BLOCKS // TRS) as i:
                        for k in range(TRS):
                            act.wait_ge(tr_done, i * TRS + (u + k + 1))
                            dst = stage_in[:, k, :]
                            if s[0] == "untranspose":
                                src = A[:, bass.ds(i * TRS + k, 1), 0:D].rearrange("p o d -> p (o d)")
                                if s[1]:
                                    nc.scalar.activation(dst, src, ACT.Copy, scale=rcol[:, bass.ds(i * TRS + k, 1)]).then_inc(tr_in, 1)
                                else:
                                    nc.scalar.activation(dst, src, ACT.Copy).then_inc(tr_in, 1)
                            else:
                                src = BIG[s[1]][:, :, bass.ds(i * (TRS * P) + k * P, P)]
                                nc.scalar.activation(dst.rearrange("p (c e) -> p c e", c=K2), src, ACT.Copy).then_inc(tr_in, 1)
                elif s[0] == "centre":
                    h0 = 2 * before(n, ("centre",))
                    for c in range(K2):
                        act.wait_ge(half_ready, h0 + c + 1)
                        last = nc.scalar.activation(BIG[s[3]][:, c, :], BIG[s[2]][:, c, :], ACT.Square)
                    last.then_inc(stage_done, 1)
                elif s[0] == "tanh":
                    begin(act, n)
                    nc.scalar.activation(BIG[s[1]][:], BIG[s[1]][:], ACT.Tanh).then_inc(stage_done, 1)
                elif s[0] == "table8":
                    g0 = groups_before(n)
                    with act.Fori(0, BLOCKS // TRS) as i:
                        for k in range(TRS):
                            act.wait_ge(tabled[k], i * 16 + 16 * (1 + before(n, ("table",)) * (BLOCKS // TRS)))
                            for q in range(4):
                                act.wait_ge(mm_done, i * (4 * TRS) + (g0 + 4 * k + q + 1))
                                nc.scalar.activation(wide(k)[:, q * 512:(q + 1) * 512], PS[:, (4 * k + q) % 8, :],
                                                     ACT.Copy).then_inc(mm_out, 1)
                elif s[0] == "fold":
                    act.wait_ge(from_pe, pe_hands(n) + 1)
                    for f in range(2):
                        for c in range(K2):
                            last = nc.scalar.activation(Wfold[:, f, c, :], PS[:, 2 * f + c, 0:D], ACT.Copy)
                    last.then_inc(stage_done, 1)
                elif s[0] == "maxpool":
                    m = before(n, ("maxpool",)) * STEPS
                    with act.Fori(0, STEPS // RING) as i:
                        for k in range(RING):
                            act.wait_ge(back_tr, i * RING + (m + k + 1 + 8))
                            act.wait_ge(summed, i * RING + (m + k + 1 - 2 + RING))
                            nc.scalar.activation(back[:, k % 2, :], PS[:, 4 + k % 2, 0:D], ACT.Copy).then_inc(back_in, 1)
                elif s[0] == "score":
                    q = before(n, ("score",)) * STEPS
                    with act.Fori(0, STEPS // RING) as i:
                        for k in range(RING):
                            act.wait_ge(oh_tr, i * RING + (q + k + 1 + RING))
                            act.wait_ge(expanded, i * RING + (q + k + 1))
                            nc.scalar.activation(ohT[:, k % 2, :], PSB[:, k % 2, 0:P], ACT.Copy).then_inc(oht_in, 1)
                elif s[0] == "softmax":
                    act.wait_ge(arg_ready, before(n, ("softmax",)) + 1)
                    nc.scalar.activation(sm_a, sm_c, ACT.Exp).then_inc(exp_done, 1)

        @block.tensor
        def _(pe):
            pe.wait_ge(consts, 3)
            for n, s in enumerate(PLAN):
                if s[0] == "dense":
                    _, w, ins, to, func, b = s
                    begin(pe, n)
                    halves = halves_out(s)
                    g0 = groups_before(n)
                    wt = wview[w]
                    ks = [(BIG[x], c) for x in ins for c in range(K2)][:wt.shape[1]]
                    with pe.Fori(0, NGROUP // 2) as i:
                        for j in range(2 * halves):
                            cols = bass.ds(i * (2 * NCOL) + (j // halves) * NCOL, NCOL)
                            c = j % halves
                            pe.wait_ge(mm_out, i * (2 * halves) + (g0 + j + 1 + (4 - 2 * halves)))
                            for q, (x, xc) in enumerate(ks):
                                last = nc.tensor.matmul(PS[:, j, 0:NCOL], wt[:, q, c * P:(c + 1) * P], x[:, xc, cols],
                                                        start=(q == 0), stop=(q == len(ks) - 1))
                            last.then_inc(mm_done, 1)
                elif s[0] in TR:
                    u = before(n, TR8) * BLOCKS
                    v = before(n, TR) * BLOCKS
                    with pe.Fori(0, BLOCKS // TRS) as i:
                        for k in range(TRS):
                            pe.wait_ge(tr_in, i * TRS + (u + k + 1))
                            pe.wait_ge(tr_out, i * TRS + (v + k + 1))
                            for c in range(K2):
                                last = nc.tensor.transpose(PS[:, k, c * P:(c + 1) * P], stage_in[:, k, c * P:(c + 1) * P], ident[:])
                            last.then_inc(tr_done, 1)
                elif s[0] == "table8":
                    u = before(n, TR8) * BLOCKS
                    g0 = groups_before(n)
                    with pe.Fori(0, BLOCKS // TRS) as i:
                        for k in range(TRS):
                            pe.wait_ge(tr_in, i * TRS + (u + k + 1))
                            for q in range(4):
                                pe.wait_ge(mm_out, i * (4 * TRS) + (g0 + 4 * k + q + 1))
                                for c in range(K2):
                                    last = nc.tensor.matmul(PS[:, (4 * k + q) % 8, :], stage_in[:, k, c * P:(c + 1) * P],
                                                            wview["typ"][:, c, q * 512:(q + 1) * 512],
                                                            start=(c == 0), stop=(c == K2 - 1))
                                last.then_inc(mm_done, 1)
                            pe.wait_ge(mm_done, i * (4 * TRS) + (g0 + 4 * k + 4))
                            pe.sem_inc(tr_done, 1)
                elif s[0] == "fold":
                    begin(pe, n)
                    for f, (a, b) in enumerate((("wq", "wk"), ("wv", "wp"))):
                        for c in range(K2):
                            for d in range(K2):
                                last = nc.tensor.matmul(PS[:, 2 * f + c, 0:D], wview[a][:, d, c * P:(c + 1) * P],
                                                        wview[b][:, d, :], start=(d == 0), stop=(d == K2 - 1))
                    last.then_inc(from_pe, 1)
                elif s[0] == "steps":
                    pe.wait_ge(to_pe, 1)
                    nc.tensor.matmul(PS[:, 0, 0:BLOCKS - 1], ones[:], counts[:, 0:BLOCKS - 1], start=True, stop=True).then_inc(from_pe, 1)
                    pe.wait_ge(to_pe, 2)
                    for a in range(2):
                        for c in range(CHUNKS):
                            last = nc.tensor.matmul(PS[:, 1 + a, c * P:(c + 1) * P], ones[:], diag[:, a, c * P:(c + 1) * P],
                                                    start=True, stop=True)
                    last.then_inc(from_pe, 1)
                    pe.wait_ge(to_pe, 3)
                    for bank, a in enumerate((0, 1, 4, 5, 6)):
                        for c in range(CHUNKS):
                            last = nc.tensor.matmul(PS[:, bank, :], attr[:, a, c * P:(c + 1) * P], pick[:, c, :],
                                                    start=(c == 0), stop=(c == CHUNKS - 1))
                    for bank, a in ((5, 2), (6, 3), (7, 0)):
                        for j in range(CHUNKS):
                            for c in range(CHUNKS):
                                last = nc.tensor.matmul(PS[:, bank, j * P:(j + 1) * P], pick[:, c, j * P:(j + 1) * P],
                                                        attr[:, a, c * P:(c + 1) * P], start=(c == 0), stop=(c == CHUNKS - 1))
                    last.then_inc(from_pe, 1)
                    pe.wait_ge(to_pe, 4)
                    for a in range(2):
                        for c in range(CHUNKS):
                            last = nc.tensor.transpose(PS[0:1, a, c * P:(c + 1) * P], has_col[:, a, c:c + 1], ident[:])
                    last.then_inc(from_pe, 1)
                elif s[0] == "softmax":
                    begin(pe, n)
                    t0, f0 = dve_hands(n), pe_hands(n)
                    for c in range(CHUNKS):
                        last = nc.tensor.transpose(PS[:, 0, c * P:(c + 1) * P], score[:, c * P:(c + 1) * P], ident[:])
                    last.then_inc(from_pe, 1)
                    for direction in range(2):
                        pe.wait_ge(to_pe, t0 + 2 * direction + 1)
                        for c in range(CHUNKS):
                            last = nc.tensor.transpose(PS[0:1, 1, c * P:(c + 1) * P], tail[:, c:c + 1], ident[:])
                        last.then_inc(from_pe, 1)
                        pe.wait_ge(to_pe, t0 + 2 * direction + 2)
                        for c in range(CHUNKS):
                            at = 2 * direction + c * P
                            last = nc.tensor.matmul(PS[:, 2, c:c + 1], carry[0:1, at:at + P], ones[0:1, 0:1], start=True, stop=True)
                        last.then_inc(from_pe, 1)
                    pe.wait_ge(to_pe, t0 + 5)
                    for c in range(CHUNKS):
                        last = nc.tensor.transpose(PS[:, 3, c * P:(c + 1) * P], sm_b[:, c, :], ident[:])
                    last.then_inc(from_pe, 1)
                elif s[0] == "maxpool":
                    begin(pe, n)
                    u = before(n, EDGE) * STEPS
                    g0 = before(n, GATHERS) * (STEPS // RING)
                    oh0 = before(n, EDGE) * (STEPS // 4)
                    m = before(n, ("maxpool",)) * STEPS
                    a0 = before(n, SUMS) * STEPS

                    def to_features(i, h):
                        pe.wait_ge(win_max, i * 2 + (m // 4 + h + 1))
                        for k4 in range(4):
                            k = 4 * h + k4
                            pe.wait_ge(gathered[k], i * 16 + 16 * (g0 + 1))
                            for c in range(K2):
                                last = nc.tensor.transpose(PS[:, 2 * h + c, k4 * P:(k4 + 1) * P],
                                                           ring[:, k, c * P:(c + 1) * P], ident[:])
                            last.then_inc(slot_free, 1)

                    def to_edges(i, k):
                        pe.wait_ge(back_in, i * RING + (m + k + 1))
                        for c in range(K2):
                            last = nc.tensor.transpose(PS[:, 4 + k % 2, c * P:(c + 1) * P],
                                                       window(k // 4, c)[:, (k % 4) * P:(k % 4 + 1) * P], ident[:])
                        last.then_inc(back_tr, 1)

                    def to_nodes(i, k):
                        pe.wait_ge(back_in, i * RING + (m + k + 1 + 2))
                        pe.wait_ge(added, i * RING + (a0 + k + 1))
                        nc.tensor.matmul(PS[:, 6 + k % 2, 0:D], ohot[:, k, :], back[:, k % 2, :],
                                         start=True, stop=True).then_inc(summed, 1)

                    def body(i, final):
                        for h in range(2):
                            if h == 0:
                                to_features(i, 1)
                            elif not final:
                                to_features(i + 1, 0)
                            pe.wait_ge(win_max, i * 2 + (m // 4 + h + 1 + 2))
                            pe.wait_ge(oh_made, i * 2 + (oh0 + h + 1))
                            to_edges(i, 4 * h)
                            for k in range(4 * h, 4 * h + 4):
                                if k % 4 < 3:
                                    to_edges(i, k + 1)
                                to_nodes(i, k)

                    to_features(0, 0)
                    with pe.Fori(0, STEPS // RING - 1) as i:
                        body(i, False)
                    body(STEPS // RING - 1, True)
                elif s[0] == "score":
                    begin(pe, n)
                    u = before(n, EDGE) * STEPS
                    oh0 = before(n, EDGE) * (STEPS // 4)
                    q = before(n, ("score",)) * STEPS

                    def turn(i, k):
                        if k % 4 == 0:
                            pe.wait_ge(oh_made, i * 2 + (oh0 + k // 4 + 1))
                        pe.wait_ge(oht_in, i * RING + (q + k + 1))
                        nc.tensor.transpose(PSB[:, k % 2, 0:P], ohot_bf[:, k, :], identb[:]).then_inc(oh_tr, 1)

                    def body(i, final):
                        for k in range(RING):
                            if k % 4 == 0:
                                blocks = block_regs(pe, i * RING + k)
                            if k < RING - 1:
                                turn(i, k + 1)
                            elif not final:
                                turn(i + 1, 0)
                            pe.wait_ge(oht_in, i * RING + (q + k + 1 + 2))
                            pe.wait_ge(slot_free, i * RING + (u + k + 1 + 4))
                            for part in range(3):
                                rows = G[:, bass.ds(blocks[k % 4], 1), part, :].rearrange("p o d -> p (o d)")
                                last = nc.tensor.matmul(PS[:, 2 + k % 4, 0:D], ohT[:, k % 2, :], rhs=rows,
                                                        start=(part == 0), stop=(part == 2))
                            last.then_inc(expanded, 1)

                    turn(0, 0)
                    with pe.Fori(0, STEPS // RING - 1) as i:
                        body(i, False)
                    body(STEPS // RING - 1, True)
                elif s[0] in ("sum", "attend"):
                    begin(pe, n)
                    landed = reloaded if s[0] == "attend" else gathered
                    g0 = before(n, ("attend",) if s[0] == "attend" else GATHERS) * (STEPS // RING)
                    oh0 = before(n, EDGE) * (STEPS // 4)
                    a0 = before(n, SUMS) * STEPS
                    with pe.Fori(0, STEPS // RING) as i:
                        for k in range(RING):
                            if k % 4 == 0:
                                pe.wait_ge(oh_made, i * 2 + (oh0 + k // 4 + 1))
                            pe.wait_ge(landed[k], i * 16 + 16 * (g0 + 1))
                            pe.wait_ge(added, i * RING + (a0 + k + 1 - 4 + 2))
                            nc.tensor.matmul(PS[:, k % 4, 0:ROW], ohot[:, k, :], ring[:, k, :],
                                             start=True, stop=True).then_inc(slot_free, 1)

        @block.vector
        def _(dve):
            done = [0]

            def link(ins):
                done[0] += 1
                ins.then_inc(vec, 1)
                dve.wait_ge(vec, done[0])

            V = nc.vector
            V.memset(ring[:, :, D:ROW], 1.0).then_inc(slot_free, RING)
            V.memset(rcol[:], 0.0).then_inc(mm_out, 4)
            for s_, c_ in ((tr_done, TRS), (tr_out, TRS), (win_max, 2), (back_tr, 8), (back_in, 2), (oh_tr, RING),
                           (oht_in, 2), (expanded, 2), (summed, RING), (added, 2), (moved, 1)):
                dve.sem_inc(s_, c_)

            def one_hots(i, h, loc, scale=None, bf=False):
                if scale is None:
                    to = (ohot_bf if bf else ohot)[:, 4 * h:4 * h + 4, :]
                    at = loc[:, bass.ds(i * RING + 4 * h, 4)].rearrange("p (k o) -> p k o", o=1).to_broadcast([P, 4, P])
                    row = iota_row[:].rearrange("p (o e) -> p o e", o=1).to_broadcast([P, 4, P])
                    V.tensor_tensor(to, row, at, ALU.is_equal).then_inc(oh_made, 1)
                else:
                    for k in range(4 * h, 4 * h + 4):
                        last = V.tensor_scalar(ohot[:, k, :], iota_row[:], loc[:, bass.ds(i * RING + k, 1)],
                                               scale[:, bass.ds(i * RING + k, 1)], ALU.is_equal, ALU.mult)
                    last.then_inc(oh_made, 1)

            for n, s in enumerate(PLAN):
                if s[0] == "steps":
                    dve.wait_ge(consts, 3)
                    dve.wait_ge(loaded, 16 * 8)
                    bi, hi = BIASES.index("bi"), BIASES.index("hi")
                    link(V.tensor_tensor(bias[:, bi:bi + 3, :], bias[:, bi:bi + 3, :], bias[:, hi:hi + 3, :], ALU.add))
                    flat = [edge_int[:, a].rearrange("p c e -> p (c e)") for a in range(6)]
                    link(V.tensor_copy(attr[:, 0, :], flat[0]))
                    link(V.tensor_tensor(attr[:, 2, :], flat[0], flat[1], ALU.not_equal))
                    link(V.tensor_tensor(attr[:, 3, :], flat[0], flat[2], ALU.not_equal))
                    link(V.scalar_tensor_tensor(attr[:, 1, :], attr[:, 0, :], FAR, attr[:, 3, :], ALU.add, ALU.mult))
                    link(V.tensor_scalar(attr[:, 1, :], attr[:, 1, :], -FAR, None, ALU.add))
                    link(V.tensor_copy(attr[:, 4, :], flat[3]))
                    link(V.scalar_tensor_tensor(attr[:, 5, :], flat[4], float(NODES), flat[3], ALU.mult, ALU.add))
                    link(V.scalar_tensor_tensor(attr[:, 6, :], flat[3], float(REL8), flat[5], ALU.mult, ALU.add))
                    for b in range(1, BLOCKS):
                        link(V.tensor_scalar(scratch, attr[:, 0, :], float(b * P), 0.0, ALU.is_lt, ALU.add,
                                             accum_out=counts[:, b - 1:b]))
                    dve.sem_inc(to_pe, 1)
                    link(V.memset(bound[:, 0:1], 0.0))
                    link(V.memset(bound[:, BLOCKS:BLOCKS + 1], float(E)))
                    dve.wait_ge(from_pe, 1)
                    link(V.tensor_copy(bound[:, 1:BLOCKS], PS[:, 0, 0:BLOCKS - 1]))
                    link(V.tensor_copy(bound_i[:, 0, :], bound))
                    link(V.tensor_scalar(bound_i[:, 1, 0:BLOCKS], bound_i[:, 0, 1:BLOCKS + 1], -1.0, None, ALU.add))
                    link(V.tensor_scalar(bound_i[:, 0, :], bound_i[:, 0, :], 7, None, ALU.arith_shift_right))
                    link(V.tensor_scalar(bound_i[:, 1, 0:BLOCKS], bound_i[:, 1, 0:BLOCKS], 7, None, ALU.arith_shift_right))
                    first, cnt, cum, shift, step_d, ge = (small[:, j, 0:BLOCKS] for j in range(6))
                    link(V.tensor_copy(first, bound_i[:, 0, 0:BLOCKS]))
                    link(V.tensor_copy(cnt, bound_i[:, 1, 0:BLOCKS]))
                    link(V.scalar_tensor_tensor(cnt, cnt, 1.0, first, ALU.add, ALU.subtract))
                    link(V.tensor_tensor(ge, bound[:, 1:BLOCKS + 1], bound[:, 0:BLOCKS], ALU.is_gt))
                    link(V.tensor_tensor(cnt, cnt, ge, ALU.mult))
                    link(V.memset(ge, 1.0))
                    link(V.tensor_tensor_scan(cum, ge, cnt, 0.0, ALU.mult, ALU.add))
                    link(V.tensor_tensor(shift, first, cum, ALU.subtract))
                    link(V.tensor_tensor(shift, shift, cnt, ALU.add))
                    link(V.memset(step_d, 0.0))
                    link(V.tensor_tensor(step_d[:, 0:BLOCKS - 1], shift[:, 1:BLOCKS], shift[:, 0:BLOCKS - 1], ALU.subtract))
                    for c in range(CHUNKS):
                        link(V.tensor_scalar(ge, cum, tail[:, c:c + 1], 0.0, ALU.is_le, ALU.add, accum_out=where[:, 1, c:c + 1]))
                        link(V.tensor_tensor_reduce(ge2, ge, step_d, 1.0, 0.0, ALU.mult, ALU.add, where[:, 0, c:c + 1]))
                    link(V.tensor_tensor(where[:, 0, :], where[:, 0, :], tail[:], ALU.add))
                    link(V.tensor_scalar(where[:, 0, :], where[:, 0, :], float(TILES - 1), None, ALU.min))
                    for a in range(2):
                        for c in range(CHUNKS):
                            last = V.tensor_scalar(diag[:, a, c * P:(c + 1) * P], ident[:], where[:, a, c:c + 1], None, ALU.mult)
                    last.then_inc(to_pe, 1)
                    dve.wait_ge(from_pe, 2)
                    link(V.tensor_scalar(row128, PS[:, 2, :], float(P), None, ALU.mult))
                    link(V.tensor_scalar(blk[0:1, :], PS[0:1, 2, :], float(BLOCKS - 1), None, ALU.min))
                    for c in range(CHUNKS):
                        last = V.tensor_scalar(pick[:, c, :], PS[:, 1, :], tail[:, c:c + 1], None, ALU.is_equal)
                    last.then_inc(to_pe, 1)
                    dve.wait_ge(from_pe, 3)
                    link(V.tensor_tensor(dloc[:], PS[:, 0, :], row128, ALU.subtract))
                    link(V.tensor_tensor(eloc[:], PS[:, 1, :], row128, ALU.subtract))
                    for bank, name in ((2, "src"), (3, "rel"), (4, "typ")):
                        link(V.tensor_copy(idx[name][:], PS[:, bank, :]))
                    link(V.tensor_scalar(flat_of(rst_row), PS[:, 5, :], RESET, None, ALU.mult))
                    link(V.tensor_scalar(flat_of(end_row), PS[:, 6, :], RESET, None, ALU.mult))
                    link(V.tensor_scalar(where[:, 1, :], where[:, 1, :], float(P), None, ALU.mult))
                    link(V.tensor_scalar(reset_flat, PS[:, 5, :], RESET, None, ALU.mult))
                    dve.sem_inc(rows_ready, 1)
                    for c in range(CHUNKS):
                        last = V.tensor_scalar(val_row[:, c, :], PS[:, 7, c * P:(c + 1) * P], where[:, 1, c:c + 1], None, ALU.subtract)
                    link(last)
                    link(V.tensor_scalar(flat_of(sm_c), flat_of(val_row), 0.0, None, ALU.is_ge))
                    link(V.scalar_tensor_tensor(flat_of(val_row), flat_of(val_row), float(P), flat_of(sm_c), ALU.is_lt, ALU.mult))
                    link(V.tensor_reduce(has_col[:, 0, :], rst_row[:], AX_X, ALU.min))
                    V.tensor_reduce(has_col[:, 1, :], end_row[:], AX_X, ALU.min).then_inc(to_pe, 1)
                    dve.wait_ge(from_pe, 4)
                    V.tensor_copy(rowhas[0:1, :, :], PS[0:1, 0:2, :]).then_inc(rows_ready, 1)
                elif s[0] == "centre":
                    begin(dve, n)
                    for c in range(K2):
                        V.tensor_tensor(BIG[s[2]][:, c, :], BIG[s[1]][:, c, :], M[:, 0, :], ALU.subtract).then_inc(half_ready, 1)
                elif s[0] == "recip":
                    begin(dve, n)
                    V.reciprocal(M[:, 0, :], M[:, 0, :]).then_inc(stage_done, 1)
                elif s[0] == "relu_mul":
                    begin(dve, n)
                    for c in range(K2):
                        last = V.scalar_tensor_tensor(BIG[s[1]][:, c, :], BIG[s[2]][:, c, :], 0.0, M[:, 0, :], ALU.max, ALU.mult)
                    last.then_inc(stage_done, 1)
                elif s[0] == "affine":
                    begin(dve, n)
                    x = BIG[s[1]]
                    for c in range(K2):
                        last = V.scalar_tensor_tensor(x[:, c, :], x[:, c, :], bias_of(s[2], c), M[:, 0, :], ALU.mult, ALU.mult)
                    link(last)
                    for c in range(K2):
                        last = V.tensor_scalar(x[:, c, :], x[:, c, :], bias_of(s[3], c), None, ALU.add)
                    last.then_inc(stage_done, 1)
                elif s[0] in ("add", "mul"):
                    begin(dve, n)
                    V.tensor_tensor(BIG[s[1]][:], BIG[s[1]][:], BIG[s[2]][:], ALU.add if s[0] == "add" else ALU.mult)\
                     .then_inc(stage_done, 1)
                elif s[0] == "add_relu":
                    begin(dve, n)
                    link(V.tensor_tensor(BIG[s[1]][:], BIG[s[1]][:], BIG[s[2]][:], ALU.add))
                    V.tensor_scalar(BIG[s[1]][:], BIG[s[1]][:], 0.0, None, ALU.max).then_inc(stage_done, 1)
                elif s[0] in TR:
                    u = before(n, TR8) * BLOCKS
                    v = before(n, TR) * BLOCKS
                    t = before(n, ("table",)) * (BLOCKS // TRS)
                    with dve.Fori(0, BLOCKS // TRS) as i:
                        for k in range(TRS):
                            if s[0] == "table":
                                dve.wait_ge(tabled[k], i * 16 + 16 * (1 + t))
                            dve.wait_ge(tr_done, i * TRS + (u + k + 1 + TRS))
                            if s[0] == "table":
                                V.tensor_copy(stage_out[:, k, :], PS[:, k, 0:D]).then_inc(tr_out, 1)
                            elif s[0] == "untranspose":
                                V.tensor_copy(BIG[s[2]][:, :, bass.ds(i * (TRS * P) + k * P, P)],
                                              PS[:, k, 0:D].rearrange("p (c e) -> p c e", c=K2)).then_inc(tr_out, 1)
                            else:
                                parts = [G[:, bass.ds(i * TRS + k, 1), a, :].rearrange("p o d -> p (o d)") for a in range(3)]
                                rest = stage_out[:, k, :]
                                b0 = before(n, ("split",)) * 4 * BLOCKS
                                for a in range(2):
                                    V.tensor_copy(parts[a], PS[:, k, 0:D] if a == 0 else rest).then_inc(split_step, 1)
                                    dve.wait_ge(split_step, i * (4 * TRS) + (b0 + 4 * k + 2 * a + 1))
                                    V.tensor_tensor(rest, PS[:, k, 0:D] if a == 0 else rest, parts[a], ALU.subtract)\
                                     .then_inc(split_step, 1)
                                    dve.wait_ge(split_step, i * (4 * TRS) + (b0 + 4 * k + 2 * a + 2))
                                V.tensor_copy(parts[2], rest).then_inc(tr_out, 1)
                    if s[0] != "table":
                        dve.wait_ge(tr_out, v + BLOCKS + TRS)
                        dve.sem_inc(stage_done, 1)
                elif s[0] == "table8":
                    begin(dve, n)
                    u = before(n, TR8) * BLOCKS
                    with dve.Fori(0, BLOCKS // TRS) as i:
                        for k in range(TRS):
                            dve.wait_ge(tr_done, i * TRS + (u + k + 1))
                            V.tensor_copy(stage_in[:, k, :].rearrange("p (c e) -> p c e", c=K2),
                                          H[:, :, bass.ds(i * (TRS * P) + k * P, P)]).then_inc(tr_in, 1)
                elif s[0] == "maxpool":
                    begin(dve, n)
                    u = before(n, EDGE) * STEPS
                    m = before(n, ("maxpool",)) * STEPS
                    a0 = before(n, SUMS) * STEPS
                    link(V.memset(A, 0.0))

                    def scans(i, h):
                        dve.wait_ge(win_max, i * 2 + (m // 4 + h + 2))
                        dve.wait_ge(back_tr, i * RING + (m + 4 * h + 4))
                        dve.wait_ge(slot_free, i * RING + (u + 4 * h + 4 + RING))
                        dve.wait_ge(reset_in[h], i * 16 + 16 * (m // RING + 1))
                        for c in range(K2):
                            last = V.tensor_tensor_scan(window(h, c), resetw[:, h, :], PS[:, 2 * h + c, :],
                                                        window(1 - h, c)[:, 4 * P - 1:4 * P], ALU.add, ALU.max)
                        last.then_inc(win_max, 1)
                        one_hots(i, h, eloc)

                    def body(i, final):
                        for h in range(2):
                            if h == 0:
                                scans(i, 1)
                            elif not final:
                                scans(i + 1, 0)
                            blocks = block_regs(dve, i * RING + 4 * h)
                            for k in range(4 * h, 4 * h + 4):
                                dve.wait_ge(summed, i * RING + (m + k + 1 + RING))
                                dve.wait_ge(added, i * RING + (a0 + k + 2))
                                to = A[:, bass.ds(blocks[k % 4], 1), 0:D].rearrange("p o d -> p (o d)")
                                V.tensor_tensor(to, to, PS[:, 6 + k % 2, 0:D], ALU.add).then_inc(added, 1)

                    scans(0, 0)
                    with dve.Fori(0, STEPS // RING - 1) as i:
                        body(i, False)
                    body(STEPS // RING - 1, True)
                    dve.wait_ge(added, a0 + STEPS + 2)
                    dve.sem_inc(stage_done, 1)
                elif s[0] == "score":
                    begin(dve, n)
                    u = before(n, EDGE) * STEPS
                    g0 = before(n, GATHERS) * (STEPS // RING)
                    q = before(n, ("score",)) * STEPS

                    def body(i, final):
                        dve.wait_ge(moved, i + (q // RING + 1))
                        for h in range(2):
                            for k in range(4 * h, 4 * h + 4):
                                dve.wait_ge(expanded, i * RING + (q + k + 1 + 2))
                                dve.wait_ge(gathered[k], i * 16 + 16 * (g0 + 1))
                                dve.wait_ge(slot_free, i * RING + (u + k + RING))
                                V.tensor_tensor_reduce(junk, PS[:, 2 + k % 4, 0:D], ring[:, k, 0:D], 1.0, 0.0,
                                                       ALU.mult, ALU.add, score8[:, k:k + 1]).then_inc(slot_free, 1)
                            if not final:
                                one_hots(i + 1, h, dloc, bf=True)
                        dve.wait_ge(slot_free, i * RING + (u + RING + RING))
                        V.tensor_copy(score[:, bass.ds(i * RING, RING)], score8[:]).then_inc(moved, 1)

                    for h in range(2):
                        one_hots(0, h, dloc, bf=True)
                    with dve.Fori(0, STEPS // RING - 1) as i:
                        body(i, False)
                    body(STEPS // RING - 1, True)
                elif s[0] in ("sum", "attend"):
                    begin(dve, n)
                    u = before(n, EDGE) * STEPS
                    a0 = before(n, SUMS) * STEPS
                    link(V.memset(A, 0.0))
                    scale = score if s[0] == "attend" else None

                    def body(i, final):
                        for h in range(2):
                            blocks = block_regs(dve, i * RING + 4 * h)
                            for k in range(4 * h, 4 * h + 4):
                                dve.wait_ge(slot_free, i * RING + (u + k + 1 + RING))
                                dve.wait_ge(added, i * RING + (a0 + k + 2))
                                to = A[:, bass.ds(blocks[k % 4], 1), :].rearrange("p o d -> p (o d)")
                                V.tensor_tensor(to, to, PS[:, k % 4, 0:ROW], ALU.add).then_inc(added, 1)
                            if not final:
                                one_hots(i + 1, h, dloc, scale)

                    for h in range(2):
                        one_hots(0, h, dloc, scale)
                    with dve.Fori(0, STEPS // RING - 1) as i:
                        body(i, False)
                    body(STEPS // RING - 1, True)
                    dve.wait_ge(added, a0 + STEPS + 2)
                    total = A[:, :, D:ROW].rearrange("p b o -> p (b o)")
                    if s[0] == "attend":
                        link(V.tensor_scalar(rcol[:], total, SM_EPS, None, ALU.add))
                    else:
                        link(V.tensor_scalar(rcol[:], total, 1.0, None, ALU.max))
                    V.reciprocal(rcol[:], rcol[:]).then_inc(stage_done, 1)
                elif s[0] == "softmax":
                    f0 = pe_hands(n)
                    dve.wait_ge(from_pe, f0 + 1)
                    link(V.tensor_scalar(flat_of(sm_c), flat_of(val_row), -1.0, -LOW, ALU.add, ALU.mult))
                    link(V.tensor_tensor(flat_of(sm_b), PS[:, 0, :], flat_of(sm_c), ALU.add))
                    for c in range(CHUNKS):
                        last = V.tensor_tensor_scan(sm_a[:, c, :], rst_row[:, c, :], sm_b[:, c, :], LOW, ALU.add, ALU.max)
                    link(last)
                    V.tensor_copy(tail[:], sm_a[:, :, P - 1]).then_inc(to_pe, 1)
                    dve.wait_ge(from_pe, f0 + 2)
                    V.tensor_tensor_scan(carry[0:1, 1:SPAD + 1], rowhas[0:1, 0, :], PS[0:1, 1, :], LOW, ALU.add, ALU.max).then_inc(to_pe, 1)
                    dve.wait_ge(from_pe, f0 + 3)
                    link(V.tensor_copy(carry_col[:], PS[:, 2, 0:CHUNKS]))
                    for c in range(CHUNKS):
                        last = V.tensor_tensor_scan(sm_a[:, c, :], rst_row[:, c, :], sm_b[:, c, :], carry_col[:, c:c + 1], ALU.add, ALU.max)
                    link(last)
                    for c in range(CHUNKS):
                        last = V.tensor_tensor_scan(sm_c[:, c, ::-1], end_row[:, c, ::-1], sm_a[:, c, ::-1], LOW, ALU.add, ALU.max)
                    link(last)
                    V.tensor_copy(tail[:], sm_c[:, :, 0]).then_inc(to_pe, 1)
                    dve.wait_ge(from_pe, f0 + 4)
                    V.tensor_tensor_scan(carry[0:1, SPAD:0:-1], rowhas[0:1, 1, ::-1], PS[0:1, 1, ::-1], LOW, ALU.add, ALU.max).then_inc(to_pe, 1)
                    dve.wait_ge(from_pe, f0 + 5)
                    link(V.tensor_copy(carry_col[:], PS[:, 2, 0:CHUNKS]))
                    for c in range(CHUNKS):
                        last = V.tensor_tensor_scan(sm_c[:, c, ::-1], end_row[:, c, ::-1], sm_a[:, c, ::-1], carry_col[:, c:c + 1], ALU.add, ALU.max)
                    link(last)
                    link(V.tensor_tensor(flat_of(sm_c), flat_of(sm_b), flat_of(sm_c), ALU.subtract))
                    V.tensor_scalar(flat_of(sm_c), flat_of(sm_c), 50.0, -50.0, ALU.min, ALU.max).then_inc(arg_ready, 1)
                    dve.wait_ge(exp_done, before(n, ("softmax",)) + 1)
                    link(V.tensor_tensor(flat_of(sm_b), flat_of(sm_a), flat_of(val_row), ALU.mult))
                    V.tensor_scalar(flat_of(sm_b), flat_of(sm_b), 0.0, None, ALU.max).then_inc(to_pe, 1)
                    dve.wait_ge(from_pe, f0 + 6)
                    V.tensor_copy(score[:], PS[:, 3, :]).then_inc(stage_done, 1)


def edge_rows(src, dst, type2, type8):
    import numpy as np

    pad = SPAD * P - E
    d = np.concatenate([np.full(1, -1, np.int32), dst, np.full(pad + 1, 9999, np.int32)])
    zero = np.zeros(pad, np.int32)
    rest = [np.concatenate([a, zero]) for a in (src, type2, type8)]
    return np.stack([d[1:-1], d[:-2], d[2:], *rest])


def kernel(**inputs):
    import numpy as np
    import concourse.bacc as bacc
    from concourse.bass_utils import run_bass_kernel_spmd

    a = {k: np.asarray(v) for k, v in inputs.items()}

    def halves(w):
        return w.reshape(w.shape[0] // P, P, w.shape[1]).transpose(1, 0, 2)

    def group(ws):
        return np.concatenate([halves(w).reshape(P, -1) for w in ws], axis=1)

    x = a["x"]
    xT = np.zeros((D, NODES), x.dtype)
    xT[:, :N] = x.T
    xT = np.ascontiguousarray(halves(xT))
    ih = a["L2_gnn_W_ih"]
    w = [
        group([a["L0_gnn_Wp1"].T, a["L0_gnn_Wm1"].T, a["L0_gnn_Wm2"].T, a["L0_gnn_Wm3"].T])[None],
        group([a["L1_gnn_w_in"]])[None],
        np.stack([group([a["L1_gnn_wq"][i].T, a["L1_gnn_wk"][i].T, a["L1_gnn_wv"][i].T, a["L1_gnn_wp"][i]]) for i in range(LAYERS)]),
        group([a["L2_gnn_W_rel"][0].T, a["L2_gnn_W_rel"][1].T, ih[0:D].T, ih[2 * D:3 * D].T, ih[3 * D:4 * D].T,
               a["L2_gnn_W1"].T, a["L2_gnn_W2"].T, a["L2_gnn_W3"].T])[None],
        group([a["L3_gnn_weight"].transpose(1, 0, 2).reshape(D, REL8 * D), a["L3_gnn_sl_w"].T])[None],
    ]
    bih, bhh = a["L2_gnn_b_ih"], a["L2_gnn_b_hh"]
    b = [a["L0_gnn_bp1"], a["L0_gnn_bm1"], a["L0_gnn_bm2"], a["L0_gnn_bm3"], a["L0_gnn_ln2_g"], a["L0_gnn_ln2_b"],
         a["L0_gnn_ln3_g"], a["L0_gnn_ln3_b"], a["L1_gnn_b_in"], *a["L1_gnn_bp"], *a["L2_gnn_b_rel"],
         bih[0:D], bih[2 * D:3 * D], bih[3 * D:], bhh[0:D], bhh[2 * D:3 * D], bhh[3 * D:],
         a["L2_gnn_b1"], a["L2_gnn_b2"], a["L2_gnn_b3"], a["L3_gnn_sl_b"]]
    bias = np.zeros((len(b), D), x.dtype)
    for i, v in enumerate(b):
        bias[i, :len(v)] = v
    bias = np.ascontiguousarray(bias.reshape(len(b), K2, P).transpose(2, 0, 1))

    nc = bacc.Bacc("TRN2", target_bir_lowering=False, num_devices=1)
    arrays = {}

    def put(name, v):
        arrays[name] = np.ascontiguousarray(v)
        return nc.dram_tensor(name, v.shape, mybir.dt.from_np(v.dtype), kind="ExternalInput").ap()

    e = put("edges", edge_rows(a["src"], a["dst"], a["edge_type_2"], a["edge_type_8"]))
    args = [e, put("xT", xT), [put(f"w{i}", v) for i, v in enumerate(w)], put("bias_in", bias)]
    args.append(nc.dram_tensor("outT", (P, K2, N), F32, kind="ExternalOutput").ap())
    for name, shape, dt in (("table", (NODES, D), F32), ("table_rel", (REL2 * NODES, D), F32),
                            ("table_typ", (REL8 * NODES, D), F32), ("spill", (STEPS, P, D), F32), ("resets", (SPAD, P), BF16)):
        args.append(nc.dram_tensor(name, shape, dt, kind="Internal").ap())
    gnn_kernel(nc, *args)
    r = run_bass_kernel_spmd(nc, [arrays], core_ids=[0])
    got = r.results[0]["outT"]
    return np.ascontiguousarray(got.transpose(2, 1, 0).reshape(N, D))
```

```python
from contextlib import ExitStack

import concourse.bass as bass
from concourse import mybir

F32 = mybir.dt.float32
BF16 = mybir.dt.bfloat16
I32 = mybir.dt.int32
ALU = mybir.AluOpType
ACT = mybir.ActivationFunctionType
AX_X = mybir.AxisListType.X

P = 128
N = 3125
E = 50000
D = 256
K2 = D // P
TILES = -(-E // P)
BLOCKS = -(-N // P)
NODES = BLOCKS * P
RING = 16
HALF = RING // 2
QUADS = RING // 4
UNROLL = 2 * RING
OHS = 8
STEPS = -(-(TILES + BLOCKS - 1) // UNROLL) * UNROLL
SPAD = 512
CHUNKS = SPAD // P
assert TILES <= SPAD and STEPS <= SPAD
NCOL = 400
NGROUP = NODES // NCOL
TRS = 5
ROW = D + 1
EPS = 1e-5
RESET = -2e38
LOW = -1e30
SM_EPS = 1e-9
LAYERS = 3
FAR = 1e6
FUNCS = {"Relu": ACT.Relu, "Identity": ACT.Identity,
         "Sigmoid": ACT.Sigmoid, "Tanh": ACT.Tanh}
REL2, REL8 = 2, 8

GROUPS = [
    [("Wp1", 2, 256), ("Wm1", 4, 256), ("Wm2", 4, 256), ("Wm3", 4, 256), ("w_in", 2, 256)],
    [("wq", 2, 256), ("wk", 2, 256), ("wv", 2, 256), ("wp", 2, 256)],
    [("rel0", 2, 256), ("rel1", 2, 256), ("ih_i", 2, 256), ("ih_g", 2, 256), ("ih_o", 2, 256),
     ("W1", 2, 128), ("W2", 1, 128), ("W3", 1, 256)],
    [("typ", 2, REL8 * 256), ("self", 2, 256)],
]
BIASES = ["bp1", "bm1", "bm2", "bm3", "ln2_g", "ln2_b", "ln3_g", "ln3_b", "b_in", "bp_0", "bp_1", "bp_2",
          "br_0", "br_1", "bi", "bg", "bo", "hi", "hg", "ho", "b1", "b2", "b3", "slb"]


def plan():
    pool_layer = [("maxpool",), ("untranspose", None, "C")]
    s = [("steps",), ("norm", "X", "B", "C", "H", "relu")]
    s += [("dense", "Wp1", ["H"], "B", "Relu", "bp1"), ("table", "B"), *pool_layer]
    s += [("dense", "Wm1", ["H", "C"], "B", "Relu", "bm1"), ("table", "B"), *pool_layer]
    s += [("dense", "Wm2", ["B", "C"], "H", "Relu", "bm2"), ("add", "H", "B")]
    s += [("norm", "H", "B", "C", "B", "ln2"), ("table", "B"), *pool_layer]
    s += [("dense", "Wm3", ["B", "C"], "H", "Relu", "bm3"), ("add", "H", "B"), ("load", 1, 0)]
    s += [("norm", "H", "B", "C", "B", "ln3"), ("add", "X", "B"), ("norm", "X", "B", "C", "H", "relu")]
    s += [("dense", "w_in", ["H"], "B", "Relu", "b_in"), ("table", "B")]
    for layer in range(LAYERS):
        s += [("fold",), ("load", 1, layer + 1) if layer < LAYERS - 1 else ("load", 2, 0)]
        s += [("project", "B"), ("score",), ("softmax",), ("attend",), ("untranspose", "ssum", "C")]
        s += [("dense", "Wvp", ["C"], "H", "Identity", f"bp_{layer}"), ("add_relu", "B", "H")]
        if layer < LAYERS - 1:
            s += [("table", "B")]
    s += [("add", "X", "B"), ("norm", "X", "B", "C", "H", "relu")]
    for r in range(REL2):
        s += [("dense", f"rel{r}", ["H"], "B", "Relu", f"br_{r}"), ("dense", f"rel{r}", ["B"], "C", "Relu", f"br_{r}"),
              ("table", "C", "rel", r)]
    s += [("sum", "rel"), ("untranspose", None, "C")]
    s += [("dense", "ih_i", ["C"], "B", "Sigmoid", "bi"), ("dense", "ih_g", ["C"], "H", "Tanh", "bg"), ("mul", "B", "H")]
    s += [("tanh", "B"), ("dense", "ih_o", ["C"], "H", "Sigmoid", "bo"), ("mul", "H", "B")]
    s += [("dense", "W1", ["H"], "B", "Relu", "b1"), ("dense", "W2", ["B"], "C", "Relu", "b2"),
          ("dense", "W3", ["C"], "B", "Identity", "b3"), ("load", 3, 0), ("add", "X", "B")]
    s += [("norm", "X", "B", "C", "H", "relu"), ("table8", "H"), ("dense", "self", ["H"], "B", "Identity", "slb"), ("add", "X", "B")]
    s += [("sum", "typ"), ("untranspose", "deg", "C"), ("add", "X", "C"), ("store",)]
    return s


def gnn_kernel(nc, edges, xT, weights, biases, out, table, table_rel, table_typ, spill, resets):
    PLAN = plan()
    FIRST = {kind: [n for n, s in enumerate(PLAN) if s[0] == kind][0] for kind in {s[0] for s in PLAN}}
    with ExitStack() as ctx:
        def sb(name, shape, dt=F32):
            return ctx.enter_context(nc.sbuf_tensor(name, shape, dt))

        def sem(name):
            return ctx.enter_context(nc.semaphore(name))

        X = sb("X", [P, K2, NODES])
        HC = sb("HC", [P, 2 * K2 * NODES])
        H = HC[:, 0:K2 * NODES].rearrange("p (c n) -> p c n", c=K2)
        C = HC[:, K2 * NODES:].rearrange("p (c n) -> p c n", c=K2)
        B = sb("B", [P, K2, NODES])
        AM = sb("AM", [P, BLOCKS * ROW + NODES])
        A = AM[:, 0:BLOCKS * ROW].rearrange("p (b r) -> p b r", r=ROW)
        A2 = HC[:, 2 * K2 * NODES - BLOCKS * ROW:].rearrange("p (b r) -> p b r", r=ROW)
        M = AM[:, BLOCKS * ROW:].rearrange("p (o n) -> p o n", o=1)
        G = AM[:, 0:BLOCKS * 3 * D // 2].bitcast(BF16).rearrange("p (b s d) -> p b s d", s=3, d=D)
        BIG = {"X": X, "H": H, "B": B, "C": C, "M": M}
        def window(h, c):
            return C[:, c, h * 4 * P:(h + 1) * 4 * P]

        W = sb("W", [P, max(sum(k * m for _, k, m in g) for g in GROUPS)])
        Wfold = sb("Wfold", [P, 2, K2, D])
        bias = sb("bias", [P, len(BIASES), K2])
        ring = sb("ring", [P, HALF, ROW])
        ring_c = C[:, 0, 8 * P:8 * P + HALF * ROW].rearrange("p (k r) -> p k r", r=ROW)
        ring_h = HC[:, 0:RING * ROW].rearrange("p (k r) -> p k r", r=ROW)

        def slot(k):
            return ring[:, k, :] if k < HALF else ring_c[:, k - HALF, :]

        work = sb("work", [P, 2 * TRS * D])
        stage_in = work[:, 0:TRS * D].rearrange("p (k d) -> p k d", d=D)
        stage_out = work[:, TRS * D:].rearrange("p (k d) -> p k d", d=D)
        ohot = work[:, 0:OHS * P].rearrange("p (k e) -> p k e", e=P)
        ohot_bf = work[:, 0:OHS * P // 2].bitcast(BF16).rearrange("p (k e) -> p k e", e=P)
        back = work[:, 1024:1536].rearrange("p (k d) -> p k d", d=D)
        junk = work[:, 1536:1792]
        odd_rows = work[:, 1024:1024 + 2 * ROW].rearrange("p (k r) -> p k r", r=ROW)
        resetw = work[:, 1792:2304].bitcast(BF16).rearrange("p (h e) -> p h e", h=2)
        ohT = work[:, 2304:2432].bitcast(BF16).rearrange("p (k e) -> p k e", e=P)
        ident = sb("ident", [P, P])
        identb = sb("identb", [P, P], BF16)
        ones = sb("ones", [P, P])
        meanw = sb("meanw", [P, K2, P])
        epsc = sb("epsc", [P, 1])
        iota_row = sb("iota_row", [P, P])
        idx = {n: sb(f"idx_{n}", [P, SPAD], I32) for n in ("src", "rel", "typ")}
        idx_now = sb("idx_now", [P, 2, RING], I32)
        dloc = sb("dloc", [P, SPAD])
        eloc = sb("eloc", [P, SPAD])
        score = sb("score", [P, SPAD])
        score8 = sb("score8", [P, RING])
        rst_row = sb("rst_row", [P, CHUNKS, P])
        end_row = sb("end_row", [P, CHUNKS, P])
        val_row = sb("val_row", [P, CHUNKS, P])
        blk = sb("blk", [1, SPAD], I32)
        rowhas = sb("rowhas", [1, 2, SPAD])
        carry = sb("carry", [1, SPAD + 2])
        carry_col = sb("carry_col", [P, CHUNKS])
        tail = sb("tail", [P, CHUNKS])
        rcol = sb("rcol", [P, BLOCKS])
        sm_a = stage_in[:, 0:2, :].rearrange("p a d -> p (a d)").rearrange("p (c e) -> p c e", e=P)
        sm_b = stage_in[:, 2:4, :].rearrange("p a d -> p (a d)").rearrange("p (c e) -> p c e", e=P)
        sm_c = stage_out[:, 0:2, :].rearrange("p a d -> p (a d)").rearrange("p (c e) -> p c e", e=P)
        PS = ctx.enter_context(nc.psum_tensor("PS", [P, 8, 512], F32))
        PSB = PS[:].rearrange("p b e -> p (b e)").bitcast(BF16).rearrange("p (b e) -> p b e", b=8)


        flatB = B[:].rearrange("p c n -> p (c n)")
        flatC = HC[:, K2 * NODES:]
        flatH = HC[:, 0:K2 * NODES]
        edge_int = flatB[:, 0:6 * SPAD].bitcast(I32).rearrange("p (a c e) -> p a c e", a=6, e=P)
        scratch = flatB[:, 6 * SPAD:7 * SPAD]
        counts = flatB[:, 7 * SPAD:7 * SPAD + 32]
        small = flatB[:, 7 * SPAD + 32:7 * SPAD + 224].rearrange("p (j b) -> p j b", b=32)
        bound = flatB[:, 7 * SPAD + 224:7 * SPAD + 224 + BLOCKS + 1]
        ge2 = flatB[:, 7 * SPAD + 256:7 * SPAD + 256 + BLOCKS]
        bound_i = flatB[:, 7 * SPAD + 288:7 * SPAD + 288 + 2 * (BLOCKS + 1)].bitcast(I32).rearrange("p (a b) -> p a b", a=2)
        where = flatB[:, 7 * SPAD + 352:7 * SPAD + 352 + 2 * CHUNKS].rearrange("p (a c) -> p a c", a=2)
        has_col = flatB[:, 7 * SPAD + 368:7 * SPAD + 368 + 2 * CHUNKS].rearrange("p (a c) -> p a c", a=2)
        attr = flatC[:, 0:7 * SPAD].rearrange("p (a s) -> p a s", a=7)
        diag = flatH[:, 0:2 * SPAD].rearrange("p (a s) -> p a s", a=2)
        row128 = flatH[:, 2 * SPAD:3 * SPAD]
        pick = flatH[:, 3 * SPAD:7 * SPAD].rearrange("p (c s) -> p c s", c=CHUNKS)
        reset_flat = flatH[:, 7 * SPAD:7 * SPAD + SPAD // 2].bitcast(BF16)
        reset_bf = reset_flat.rearrange("p (c e) -> p c e", e=P)

        def flat_of(rows):
            return rows[:, :, :].rearrange("p c e -> p (c e)")

        def wide(k):
            base, at = (flatB, k) if k < 3 else (flatC, k - 3)
            return base[:, at * REL8 * D:(at + 1) * REL8 * D]

        wview = {}
        for g in GROUPS:
            at = 0
            for name, k, m in g:
                wview[name] = W[:, at:at + k * m].rearrange("p (k m) -> p k m", k=k)
                at += k * m
        wview["Wqk"] = Wfold[:, 0]
        wview["Wvp"] = Wfold[:, 1]
        wview["mean"] = meanw

        def bias_of(name, c):
            return bias[:, BIASES.index(name), c:c + 1]

        stage_done = sem("stage_done")
        consts = sem("consts")
        vec = sem("vec")
        loaded = sem("loaded")
        weighted = sem("weighted")
        to_pe = sem("to_pe")
        from_pe = sem("from_pe")
        rows_ready = sem("rows_ready")
        arg_ready = sem("arg_ready")
        exp_done = sem("exp_done")
        half_ready = sem("half_ready")
        mm_done = sem("mm_done")
        mm_out = sem("mm_out")
        tr_in = sem("tr_in")
        tr_done = sem("tr_done")
        tr_out = sem("tr_out")
        tabled = sem("tabled")
        wided = [sem(f"wided{k}") for k in range(TRS)]
        mean_in = sem("mean_in")
        centred = sem("centred")
        squared = sem("squared")
        var_in = sem("var_in")
        std_out = sem("std_out")
        inverted = sem("inverted")
        scaled = sem("scaled")
        high_made = sem("high_made")
        mid_made = sem("mid_made")
        low_made = sem("low_made")
        gathered = [sem(f"gathered{k}") for k in range(RING)]
        reloaded = [sem(f"reloaded{k}") for k in range(HALF)]
        slot_free = sem("slot_free")
        spilled = [sem(f"spilled{k}") for k in range(RING)]
        passed = sem("passed")
        staged = sem("staged")
        reset_in = [sem(f"reset_in{h}") for h in range(2)]
        win_max = sem("win_max")
        back_tr = sem("back_tr")
        back_in = sem("back_in")
        oh_made = sem("oh_made")
        oh_tr = sem("oh_tr")
        oht_in = sem("oht_in")
        expanded = sem("expanded")
        summed = sem("summed")
        added = sem("added")
        even_added = sem("even_added")
        odd_out = sem("odd_out")
        odd_added = sem("odd_added")
        cleared = sem("cleared")
        moved = sem("moved")
        stored = sem("stored")

        block = ctx.enter_context(nc.Block())

        def before(n, kinds):
            return sum(1 for s in PLAN[:n] if s[0] in kinds)

        def groups_before(n):
            return (sum(NGROUP * halves_out(s) for s in PLAN[:n] if s[0] == "dense")
                    + 4 * BLOCKS * before(n, ("table8",)))

        def halves_out(s):
            return 1 if s[1] in ("mean", "W1", "W2") else 2

        TR = ("table", "untranspose", "project")
        TR8 = TR + ("table8",)
        EDGE = ("maxpool", "score", "attend", "sum")
        GATHERS = ("maxpool", "score", "sum")

        def pe_hands(n):
            return 4 * before(n, ("steps",)) + before(n, ("fold",)) + 6 * before(n, ("softmax",))

        def dve_hands(n):
            return 4 * before(n, ("steps",)) + 5 * before(n, ("softmax",))

        def one(rows, at):
            return rows[bass.ds(at, 1)].rearrange("o p d -> (o p) d")

        def begin(eng, n):
            ended = sum(1 for s in PLAN[:n] if s[0] != "load")
            if ended:
                eng.wait_ge(stage_done, ended)

        def weights_in(eng, n):
            eng.wait_ge(weighted, 16 * (1 + before(n, ("load",))))

        def part(b, a):
            return G[:, bass.ds(b, 1), a, :].rearrange("p o d -> p (o d)")

        def block_regs(eng, s, count=RING):
            regs = nc.values_load_multi_w_load_instructions(
                blk[0:1, bass.ds(s, count)], engines=(eng.engine,), min_val=0, max_val=BLOCKS - 1,
                skip_runtime_bounds_check_because="the table is cut to the last block")[1]
            return regs

        @block.gpsimd
        def _(pool):
            pool.memset(ones[:], 1.0)
            pool.memset(meanw[:], 1.0 / D)
            pool.memset(epsc[:], EPS)
            pool.memset(score[:], 0.0)
            pool.memset(carry[:], LOW)
            pool.memset(ident[:], 0.0).then_inc(consts, 1)
            pool.iota(iota_row[:], pattern=[[1, P]], base=0, channel_multiplier=0,
                      allow_small_or_imprecise_dtypes=True)
            pool.iota(tail[:], pattern=[[P, CHUNKS]], base=0, channel_multiplier=1,
                      allow_small_or_imprecise_dtypes=True)
            pool.wait_ge(consts, 1)
            pool.affine_select(out=ident[:], in_=ident[:], compare_op=ALU.not_equal, fill=1.0, base=0,
                               pattern=[[-1, P]], channel_multiplier=1).then_inc(consts, 1)
            pool.wait_ge(consts, 2)
            pool.tensor_copy(identb[:], ident[:]).then_inc(consts, 1)
            for n, s in enumerate(PLAN):
                if s[0] == "project":
                    p0 = before(n, ("project",)) * BLOCKS
                    with pool.Fori(0, BLOCKS // TRS) as i:
                        for k in range(TRS):
                            pool.wait_ge(tr_out, i * TRS + (before(n, TR) * BLOCKS + k + 1 + TRS))
                            pool.sem_inc(passed, 1)
                            pool.tensor_copy(part(i * TRS + k, 1), stage_out[:, k, :]).then_inc(mid_made, 1)
                if s[0] == "attend":
                    begin(pool, n)
                    e0 = before(n, ("attend",)) * (STEPS // 2)
                    pool.memset(A2, 0.0).then_inc(cleared, 1)
                    pool.wait_ge(cleared, before(n, ("attend",)) + 1)
                    with pool.Fori(0, STEPS // RING) as i:
                        blocks = block_regs(pool, i * RING)
                        for k in range(1, RING, 2):
                            pool.wait_ge(odd_out, i * (RING // 2) + (e0 + k // 2 + 1 + 2))
                            pool.wait_ge(odd_added, i * (RING // 2) + (e0 + k // 2 + 2))
                            pool.sem_inc(passed, 1)
                            to = A2[:, bass.ds(blocks[k], 1), :].rearrange("p o d -> p (o d)")
                            pool.tensor_tensor(to, to, odd_rows[:, k // 2 % 2, :], ALU.add).then_inc(odd_added, 1)
                if s[0] not in ("maxpool", "score", "sum"):
                    continue
                begin(pool, n)
                gathers = before(n, ("maxpool", "score", "sum")) * STEPS
                uses = before(n, EDGE) * STEPS
                spills = 1 + before(n, ("score",)) * (STEPS // RING)
                src = {"rel": table_rel, "typ": table_typ}.get(s[-1], table)
                ids = idx[s[-1]] if s[0] == "sum" else idx["src"]
                with pool.Fori(0, STEPS // UNROLL) as i:
                    for h in range(2):
                        pool.wait_ge(slot_free, i * UNROLL + (uses + h * RING + 1))
                        pool.tensor_copy(idx_now[:, h, :], ids[:, bass.ds(i * UNROLL + h * RING, RING)]).then_inc(staged, 1)
                        pool.wait_ge(staged, i * 2 + (gathers // RING + h + 1))
                        for k in range(RING):
                            pool.wait_ge(slot_free, i * UNROLL + (uses + h * RING + k + 1))
                            if s[0] == "score":
                                pool.wait_ge(spilled[k], i * 32 + 16 * (spills + h))
                            pool.sem_inc(passed, 1)
                            pool.indirect_dma_start(
                                slot(k)[:, 0:D], None, src,
                                bass.IndirectOffsetOnAxis(ap=idx_now[:, h, k:k + 1], axis=0)).then_inc(gathered[k], 16)

        @block.sync
        def _(sp):
            for n, s in enumerate(PLAN):
                if s[0] == "steps":
                    for a in range(6):
                        sp.dma_start(edge_int[:, a], edges[a].rearrange("(c p e) -> p c e", c=CHUNKS, e=P)).then_inc(loaded, 16)
                    sp.dma_start(bias[:], biases).then_inc(loaded, 16)
                    sp.dma_start(X[:], xT).then_inc(loaded, 16)
                    sp.dma_start(W[:, 0:sum(k * m for _, k, m in GROUPS[0])], weights[0][0]).then_inc(weighted, 16)
                    for k in range(TRS):
                        sp.dma_start(spill[0, k:k + 1, 0:1], biases[0:1, 0, 0:1]).then_inc(wided[k], 16)
                    for k in range(RING):
                        sp.dma_start(spill[1, k:k + 1, 0:1], biases[0:1, 0, 0:1]).then_inc(spilled[k], 16)
                    for credit in wided + spilled:
                        sp.wait_ge(credit, 16)
                    sp.wait_ge(loaded, 16 * 8)
                    sp.wait_ge(rows_ready, 1)
                    sp.dma_start(resets.rearrange("(c q) e -> q c e", q=P), reset_bf).then_inc(stored, 16)
                    sp.wait_ge(stored, 16)
                    sp.wait_ge(rows_ready, 2)
                    sp.sem_inc(stage_done, 1)
                elif s[0] == "load":
                    begin(sp, n)
                    width = sum(k * m for _, k, m in GROUPS[s[1]])
                    sp.dma_start(W[:, 0:width], weights[s[1]][s[2]]).then_inc(weighted, 16)
                elif s[0] == "table":
                    begin(sp, n)
                    u = before(n, TR) * BLOCKS
                    t = before(n, ("table",))
                    to = table if len(s) == 2 else table_rel[s[3] * NODES:(s[3] + 1) * NODES, :]
                    rows = to.rearrange("(b p) d -> p b d", p=P)
                    with sp.Fori(0, BLOCKS // TRS) as i:
                        sp.wait_ge(tr_out, i * TRS + (u + TRS + TRS))
                        sp.dma_start(rows[:, bass.ds(i * TRS, TRS), :], A[:, bass.ds(i * TRS, TRS), 0:D]).then_inc(tabled, 16)
                    sp.wait_ge(tabled, 16 * (t + 1) * (BLOCKS // TRS))
                    sp.sem_inc(stage_done, 1)
                elif s[0] == "table8":
                    begin(sp, n)
                    g0 = groups_before(n)
                    rows = table_typ.rearrange("(b p r) d -> b p (r d)", p=P, r=REL8)
                    with sp.Fori(0, BLOCKS // TRS) as i:
                        for k in range(TRS):
                            sp.wait_ge(mm_out, i * (4 * TRS) + (g0 + 4 * k + 4 + 4))
                            sp.dma_start(one(rows, i * TRS + k), wide(k)).then_inc(wided[k], 16)
                    for k in range(TRS):
                        sp.wait_ge(wided[k], 16 * (1 + BLOCKS // TRS))
                    sp.sem_inc(stage_done, 1)
                elif s[0] == "maxpool":
                    begin(sp, n)
                    m = before(n, ("maxpool",)) * (STEPS // 4)
                    rows = resets.rearrange("(g a) e -> g (a e)", a=4)
                    with sp.Fori(0, STEPS // 8) as i:
                        for h in range(2):
                            sp.wait_ge(win_max, i * 2 + (m + h + 1))
                            sp.dma_start(resetw[:, h, :], rows[bass.ds(i * 2 + h, 1), :].to_broadcast([P, 4 * P]))\
                              .then_inc(reset_in[h], 16)
                elif s[0] == "score":
                    begin(sp, n)
                    g0 = before(n, GATHERS) * (STEPS // RING)
                    with sp.Fori(0, STEPS // RING) as i:
                        for k in range(RING):
                            sp.wait_ge(gathered[k], i * 16 + 16 * (g0 + 1))
                            sp.dma_start(one(spill, i * RING + k), slot(k)[:, 0:D]).then_inc(spilled[k], 16)
                    for k in range(RING):
                        sp.wait_ge(spilled[k], 16 * (1 + (before(n, ("score",)) + 1) * (STEPS // RING)))
                    sp.wait_ge(moved, (before(n, ("score",)) + 1) * (STEPS // RING) + 1)
                    sp.sem_inc(stage_done, 1)
                elif s[0] == "attend":
                    begin(sp, n)
                    u = before(n, EDGE) * STEPS
                    rows = spill.rearrange("s p d -> p s d")
                    with sp.Fori(0, STEPS // RING) as i:
                        for k in range(0, RING, 2):
                            sp.wait_ge(slot_free, i * RING + (u + k + 2))
                            sp.dma_start(ring_h[:, k:k + 2, 0:D], rows[:, bass.ds(i * RING + k, 2), :]).then_inc(reloaded[k // 2], 16)
                elif s[0] == "store":
                    begin(sp, n)
                    sp.dma_start(out, X[:, :, 0:N]).then_inc(stored, 16)
                    sp.wait_ge(stored, 32)

        @block.scalar
        def _(act):
            for n, s in enumerate(PLAN):
                if s[0] == "dense":
                    _, w, ins, to, func, b = s
                    halves = halves_out(s)
                    g0 = groups_before(n)
                    dst = BIG[to]
                    with act.Fori(0, NGROUP // 2) as i:
                        for j in range(2 * halves):
                            cols = bass.ds(i * (2 * NCOL) + (j // halves) * NCOL, NCOL)
                            act.wait_ge(mm_done, i * (2 * halves) + (g0 + j + 1))
                            more = {}
                            if b:
                                more["bias"] = bias_of(b, j % halves)
                            fn = FUNCS[func]
                            nc.scalar.activation(dst[:, j % halves, cols], PS[:, j, 0:NCOL], fn, **more).then_inc(mm_out, 1)
                    act.wait_ge(mm_out, g0 + NGROUP * halves + 4)
                    act.sem_inc(stage_done, 1)
                elif s[0] in TR:
                    begin(act, n)
                    u = before(n, TR8) * BLOCKS
                    p0 = before(n, ("project",)) * BLOCKS

                    def copy_in(i, k):
                        act.wait_ge(tr_done, i * TRS + (u + k + 1))
                        dst = stage_in[:, k, :]
                        if s[0] == "untranspose":
                            src = A[:, bass.ds(i * TRS + k, 1), 0:D].rearrange("p o d -> p (o d)")
                            more = {"scale": rcol[:, bass.ds(i * TRS + k, 1)]} if s[1] else {}
                            nc.scalar.activation(dst, src, ACT.Copy, **more).then_inc(tr_in, 1)
                        else:
                            src = BIG[s[1]][:, :, bass.ds(i * (TRS * P) + k * P, P)]
                            nc.scalar.activation(dst.rearrange("p (c e) -> p c e", c=K2), src, ACT.Copy).then_inc(tr_in, 1)

                    with act.Fori(0, BLOCKS // TRS) as i:
                        for k in range(TRS):
                            if k == 0 or s[0] != "project":
                                copy_in(i, k)
                            if s[0] == "project":
                                if k < TRS - 1:
                                    copy_in(i, k + 1)
                                act.wait_ge(tr_done, i * TRS + (u + k + 1 + TRS))
                                nc.scalar.activation(part(i * TRS + k, 0), PS[:, k, 0:D], ACT.Copy).then_inc(high_made, 1)
                elif s[0] == "norm":
                    c0 = before(n, ("norm",)) * NGROUP

                    def square(i, j):
                        act.wait_ge(centred, i * 2 + (c0 + j + 1))
                        cols = bass.ds(i * (2 * NCOL) + j * NCOL, NCOL)
                        nc.scalar.activation(BIG[s[3]][:, :, cols], BIG[s[2]][:, :, cols], ACT.Square).then_inc(squared, 1)

                    def root(i, j):
                        act.wait_ge(var_in, i * 2 + (c0 + j + 1))
                        nc.scalar.activation(M[:, 0, bass.ds(i * (2 * NCOL) + j * NCOL, NCOL)], PS[:, 2 + j, 0:NCOL],
                                             ACT.Sqrt, bias=epsc[:]).then_inc(std_out, 1)

                    def body(i, final):
                        square(i, 1)
                        root(i, 0)
                        if not final:
                            square(i + 1, 0)
                        root(i, 1)

                    square(0, 0)
                    with act.Fori(0, NGROUP // 2 - 1) as i:
                        body(i, False)
                    body(NGROUP // 2 - 1, True)
                elif s[0] == "tanh":
                    begin(act, n)
                    nc.scalar.activation(BIG[s[1]][:, :, :], BIG[s[1]][:, :, :], ACT.Tanh).then_inc(stage_done, 1)
                elif s[0] == "table8":
                    g0 = groups_before(n)
                    with act.Fori(0, BLOCKS // TRS) as i:
                        for k in range(TRS):
                            act.wait_ge(wided[k], i * 16 + 16)
                            for q in range(4):
                                act.wait_ge(mm_done, i * (4 * TRS) + (g0 + 4 * k + q + 1))
                                nc.scalar.activation(wide(k)[:, q * 512:(q + 1) * 512], PS[:, (4 * k + q) % 8, :],
                                                     ACT.Copy).then_inc(mm_out, 1)
                elif s[0] == "fold":
                    act.wait_ge(from_pe, pe_hands(n) + 1)
                    for f in range(2):
                        for c in range(K2):
                            last = nc.scalar.activation(Wfold[:, f, c, :], PS[:, 2 * f + c, 0:D], ACT.Copy,
                                                        scale=float(D) ** -0.5 if f == 0 else 1.0)
                    last.then_inc(stage_done, 1)
                elif s[0] == "maxpool":
                    m = before(n, ("maxpool",)) * STEPS
                    with act.Fori(0, STEPS // RING) as i:
                        for k in range(RING):
                            act.wait_ge(back_tr, i * RING + (m + k + 1 + 8))
                            act.wait_ge(summed, i * RING + (m + k + 1 - 2 + OHS))
                            nc.scalar.activation(back[:, k % 2, :], PS[:, 4 + k % 2, 0:D], ACT.Copy).then_inc(back_in, 1)
                elif s[0] == "score":
                    q = before(n, ("score",)) * STEPS
                    with act.Fori(0, STEPS // RING) as i:
                        for k in range(RING):
                            act.wait_ge(oh_tr, i * RING + (q + k + 1 + OHS))
                            act.wait_ge(expanded, i * RING + (q + k + 1))
                            nc.scalar.activation(ohT[:, k % 2, :], PSB[:, k % 2, 0:P], ACT.Copy).then_inc(oht_in, 1)
                elif s[0] == "attend":
                    begin(act, n)
                    u = before(n, EDGE) * STEPS
                    e0 = before(n, ("attend",)) * (STEPS // 2)
                    with act.Fori(0, STEPS // RING) as i:
                        for k in range(1, RING, 2):
                            act.wait_ge(slot_free, i * RING + (u + k + 1 + RING))
                            act.wait_ge(odd_added, i * (RING // 2) + (e0 + k // 2 + 1))
                            nc.scalar.activation(odd_rows[:, k // 2 % 2, :], PS[:, k % 4, 0:ROW], ACT.Copy).then_inc(odd_out, 1)
                elif s[0] == "softmax":
                    act.wait_ge(arg_ready, before(n, ("softmax",)) + 1)
                    nc.scalar.activation(sm_a, sm_c, ACT.Exp).then_inc(exp_done, 1)

        @block.tensor
        def _(pe):
            pe.wait_ge(consts, 3)
            for n, s in enumerate(PLAN):
                if s[0] == "dense":
                    _, w, ins, to, func, b = s
                    begin(pe, n)
                    weights_in(pe, n)
                    halves = halves_out(s)
                    g0 = groups_before(n)
                    wt = wview[w]
                    ks = [(BIG[x], c) for x in ins for c in range(K2)][:wt.shape[1]]
                    with pe.Fori(0, NGROUP // 2) as i:
                        for j in range(2 * halves):
                            cols = bass.ds(i * (2 * NCOL) + (j // halves) * NCOL, NCOL)
                            c = j % halves
                            pe.wait_ge(mm_out, i * (2 * halves) + (g0 + j + 1 + (4 - 2 * halves)))
                            for q, (x, xc) in enumerate(ks):
                                last = nc.tensor.matmul(PS[:, j, 0:NCOL], wt[:, q, c * P:(c + 1) * P], x[:, xc, cols],
                                                        start=(q == 0), stop=(q == len(ks) - 1))
                            last.then_inc(mm_done, 1)
                elif s[0] in TR:
                    u = before(n, TR8) * BLOCKS
                    v = before(n, TR) * BLOCKS
                    if s[0] == "project":
                        begin(pe, n)
                    with pe.Fori(0, BLOCKS // TRS) as i:
                        for k in range(TRS):
                            pe.wait_ge(tr_in, i * TRS + (u + k + 1))
                            pe.wait_ge(tr_out, i * TRS + (v + k + 1))
                            for c in range(K2):
                                half = stage_in[:, k, c * P:(c + 1) * P]
                                if s[0] == "project":
                                    last = nc.tensor.matmul(PS[:, k, 0:D], half, wview["Wqk"][:, c, :], start=(c == 0), stop=(c == K2 - 1))
                                else:
                                    last = nc.tensor.transpose(PS[:, k, c * P:(c + 1) * P], half, ident[:])
                            last.then_inc(tr_done, 1)
                elif s[0] == "norm":
                    begin(pe, n)
                    c0 = before(n, ("norm",)) * NGROUP

                    def mean(i, j):
                        if not (isinstance(i, int) and i == 0):
                            pe.wait_ge(centred, i * 2 + (c0 + j - 1))
                        cols = bass.ds(i * (2 * NCOL) + j * NCOL, NCOL)
                        for c in range(K2):
                            last = nc.tensor.matmul(PS[:, j, 0:NCOL], meanw[:, c, :], BIG[s[1]][:, c, cols], start=(c == 0), stop=(c == K2 - 1))
                        last.then_inc(mean_in, 1)

                    def variance(i, j):
                        pe.wait_ge(squared, i * 2 + (c0 + j + 1))
                        pe.wait_ge(std_out, i * 2 + (c0 + j + 1))
                        cols = bass.ds(i * (2 * NCOL) + j * NCOL, NCOL)
                        for c in range(K2):
                            last = nc.tensor.matmul(PS[:, 2 + j, 0:NCOL], meanw[:, c, :], BIG[s[3]][:, c, cols], start=(c == 0), stop=(c == K2 - 1))
                        last.then_inc(var_in, 1)

                    def body(i, final):
                        mean(i, 1)
                        variance(i, 0)
                        if not final:
                            mean(i + 1, 0)
                        variance(i, 1)

                    mean(0, 0)
                    body(0, False)
                    with pe.Fori(1, NGROUP // 2 - 1) as i:
                        body(i, False)
                    body(NGROUP // 2 - 1, True)
                elif s[0] == "table8":
                    weights_in(pe, n)
                    u = before(n, TR8) * BLOCKS
                    g0 = groups_before(n)
                    with pe.Fori(0, BLOCKS // TRS) as i:
                        for k in range(TRS):
                            pe.wait_ge(tr_in, i * TRS + (u + k + 1))
                            for q in range(4):
                                pe.wait_ge(mm_out, i * (4 * TRS) + (g0 + 4 * k + q + 1))
                                for c in range(K2):
                                    last = nc.tensor.matmul(PS[:, (4 * k + q) % 8, :], stage_in[:, k, c * P:(c + 1) * P],
                                                            wview["typ"][:, c, q * 512:(q + 1) * 512],
                                                            start=(c == 0), stop=(c == K2 - 1))
                                last.then_inc(mm_done, 1)
                            pe.wait_ge(mm_done, i * (4 * TRS) + (g0 + 4 * k + 4))
                            pe.sem_inc(tr_done, 1)
                elif s[0] == "fold":
                    begin(pe, n)
                    weights_in(pe, n)
                    for f, (a, b) in enumerate((("wq", "wk"), ("wv", "wp"))):
                        for c in range(K2):
                            for d in range(K2):
                                last = nc.tensor.matmul(PS[:, 2 * f + c, 0:D], wview[a][:, d, c * P:(c + 1) * P],
                                                        wview[b][:, d, :], start=(d == 0), stop=(d == K2 - 1))
                    last.then_inc(from_pe, 1)
                elif s[0] == "steps":
                    pe.wait_ge(to_pe, 1)
                    nc.tensor.matmul(PS[:, 0, 0:BLOCKS - 1], ones[:], counts[:, 0:BLOCKS - 1], start=True, stop=True).then_inc(from_pe, 1)
                    pe.wait_ge(to_pe, 2)
                    for a in range(2):
                        for c in range(CHUNKS):
                            last = nc.tensor.matmul(PS[:, 1 + a, c * P:(c + 1) * P], ones[:], diag[:, a, c * P:(c + 1) * P],
                                                    start=True, stop=True)
                    last.then_inc(from_pe, 1)
                    pe.wait_ge(to_pe, 3)
                    for bank, a in enumerate((0, 1, 4, 5, 6)):
                        for c in range(CHUNKS):
                            last = nc.tensor.matmul(PS[:, bank, :], attr[:, a, c * P:(c + 1) * P], pick[:, c, :],
                                                    start=(c == 0), stop=(c == CHUNKS - 1))
                    for bank, a in ((5, 2), (6, 3), (7, 0)):
                        for j in range(CHUNKS):
                            for c in range(CHUNKS):
                                last = nc.tensor.matmul(PS[:, bank, j * P:(j + 1) * P], pick[:, c, j * P:(j + 1) * P],
                                                        attr[:, a, c * P:(c + 1) * P], start=(c == 0), stop=(c == CHUNKS - 1))
                    last.then_inc(from_pe, 1)
                    pe.wait_ge(to_pe, 4)
                    for a in range(2):
                        for c in range(CHUNKS):
                            last = nc.tensor.transpose(PS[0:1, a, c * P:(c + 1) * P], has_col[:, a, c:c + 1], ident[:])
                    last.then_inc(from_pe, 1)
                elif s[0] == "softmax":
                    begin(pe, n)
                    t0, f0 = dve_hands(n), pe_hands(n)
                    for c in range(CHUNKS):
                        last = nc.tensor.transpose(PS[:, 0, c * P:(c + 1) * P], score[:, c * P:(c + 1) * P], ident[:])
                    last.then_inc(from_pe, 1)
                    for direction in range(2):
                        pe.wait_ge(to_pe, t0 + 2 * direction + 1)
                        for c in range(CHUNKS):
                            last = nc.tensor.transpose(PS[0:1, 1, c * P:(c + 1) * P], tail[:, c:c + 1], ident[:])
                        last.then_inc(from_pe, 1)
                        pe.wait_ge(to_pe, t0 + 2 * direction + 2)
                        for c in range(CHUNKS):
                            at = 2 * direction + c * P
                            last = nc.tensor.matmul(PS[:, 2, c:c + 1], carry[0:1, at:at + P], ones[0:1, 0:1], start=True, stop=True)
                        last.then_inc(from_pe, 1)
                    pe.wait_ge(to_pe, t0 + 5)
                    for c in range(CHUNKS):
                        last = nc.tensor.transpose(PS[:, 3, c * P:(c + 1) * P], sm_b[:, c, :], ident[:])
                    last.then_inc(from_pe, 1)
                elif s[0] == "maxpool":
                    begin(pe, n)
                    u = before(n, EDGE) * STEPS
                    g0 = before(n, GATHERS) * (STEPS // RING)
                    oh0 = before(n, EDGE) * (STEPS // 4)
                    m = before(n, ("maxpool",)) * STEPS
                    a0 = before(n, ("maxpool", "sum")) * STEPS

                    def to_features(i, h):
                        pe.wait_ge(win_max, i * QUADS + (m // 4 + h + 1))
                        for k4 in range(4):
                            k = 4 * h + k4
                            pe.wait_ge(gathered[k], i * 16 + 16 * (g0 + 1))
                            for c in range(K2):
                                last = nc.tensor.transpose(PS[:, 2 * (h % 2) + c, k4 * P:(k4 + 1) * P],
                                                           slot(k)[:, c * P:(c + 1) * P], ident[:])
                            last.then_inc(slot_free, 1)

                    def to_edges(i, k):
                        pe.wait_ge(back_in, i * RING + (m + k + 1))
                        for c in range(K2):
                            last = nc.tensor.transpose(PS[:, 4 + k % 2, c * P:(c + 1) * P],
                                                       window(k // 4 % 2, c)[:, (k % 4) * P:(k % 4 + 1) * P], ident[:])
                        last.then_inc(back_tr, 1)

                    def to_nodes(i, k):
                        pe.wait_ge(back_in, i * RING + (m + k + 1 + 2))
                        pe.wait_ge(added, i * RING + (a0 + k + 1))
                        nc.tensor.matmul(PS[:, 6 + k % 2, 0:D], ohot[:, k % OHS, :], back[:, k % 2, :],
                                         start=True, stop=True).then_inc(summed, 1)

                    def body(i, final):
                        for h in range(QUADS):
                            if h < QUADS - 1:
                                to_features(i, h + 1)
                            elif not final:
                                to_features(i + 1, 0)
                            pe.wait_ge(win_max, i * QUADS + (m // 4 + h + 1 + 2))
                            pe.wait_ge(oh_made, i * QUADS + (oh0 + h + 1))
                            to_edges(i, 4 * h)
                            for k in range(4 * h, 4 * h + 4):
                                if k % 4 < 3:
                                    to_edges(i, k + 1)
                                to_nodes(i, k)

                    to_features(0, 0)
                    with pe.Fori(0, STEPS // RING - 1) as i:
                        body(i, False)
                    body(STEPS // RING - 1, True)
                elif s[0] == "score":
                    begin(pe, n)
                    u = before(n, EDGE) * STEPS
                    oh0 = before(n, EDGE) * (STEPS // 4)
                    q = before(n, ("score",)) * STEPS

                    def turn(i, k):
                        if k % 4 == 0:
                            pe.wait_ge(oh_made, i * QUADS + (oh0 + k // 4 + 1))
                        pe.wait_ge(oht_in, i * RING + (q + k + 1))
                        nc.tensor.transpose(PSB[:, k % 2, 0:P], ohot_bf[:, k % OHS, :], identb[:]).then_inc(oh_tr, 1)

                    def body(i, final):
                        blocks = block_regs(pe, i * RING)
                        for k in range(RING):
                            if k < RING - 1:
                                turn(i, k + 1)
                            elif not final:
                                turn(i + 1, 0)
                            pe.wait_ge(oht_in, i * RING + (q + k + 1 + 2))
                            pe.wait_ge(slot_free, i * RING + (u + k + 1 - 4 + RING))
                            for part in range(3):
                                rows = G[:, bass.ds(blocks[k], 1), part, :].rearrange("p o d -> p (o d)")
                                last = nc.tensor.matmul(PS[:, 2 + k % 4, 0:D], ohT[:, k % 2, :], rhs=rows,
                                                        start=(part == 0), stop=(part == 2))
                            last.then_inc(expanded, 1)

                    turn(0, 0)
                    with pe.Fori(0, STEPS // RING - 1) as i:
                        body(i, False)
                    body(STEPS // RING - 1, True)
                elif s[0] in ("sum", "attend"):
                    begin(pe, n)
                    e0 = before(n, ("attend",)) * (STEPS // 2)
                    g0 = before(n, ("attend",) if s[0] == "attend" else GATHERS) * (STEPS // RING)
                    oh0 = before(n, EDGE) * (STEPS // 4)
                    a0 = before(n, ("maxpool", "sum")) * STEPS
                    with pe.Fori(0, STEPS // RING) as i:
                        for k in range(RING):
                            if k % 4 == 0:
                                pe.wait_ge(oh_made, i * QUADS + (oh0 + k // 4 + 1))
                            if s[0] == "sum":
                                pe.wait_ge(gathered[k], i * 16 + 16 * (g0 + 1))
                            elif k % 2 == 0:
                                pe.wait_ge(reloaded[k // 2], i * 16 + 16 * (g0 + 1))
                            if s[0] == "sum":
                                pe.wait_ge(added, i * RING + (a0 + k + 1 - 4 + 2))
                            else:
                                pe.wait_ge(odd_out if k % 2 else even_added, i * (RING // 2) + (e0 + k // 2 + 1))
                            nc.tensor.matmul(PS[:, k % 4, 0:ROW], ohot[:, k % OHS, :], slot(k) if s[0] == "sum" else ring_h[:, k, :],
                                             start=True, stop=True).then_inc(slot_free, 1)

        @block.vector
        def _(dve):
            done = [0]

            def link(ins):
                done[0] += 1
                ins.then_inc(vec, 1)
                dve.wait_ge(vec, done[0])

            V = nc.vector
            V.memset(ring[:, :, D:ROW], 1.0).then_inc(slot_free, RING)
            V.memset(rcol[:], 0.0).then_inc(mm_out, 4)
            for s_, c_ in ((tr_done, TRS), (tr_out, TRS), (win_max, 2), (back_tr, 8), (back_in, 2), (oh_tr, OHS),
                           (oht_in, 2), (expanded, 2), (summed, OHS), (low_made, TRS), (std_out, 2), (added, 2), (moved, 1), (even_added, 2),
                           (odd_out, 2), (odd_added, 2)):
                dve.sem_inc(s_, c_)

            def one_hots(i, h, loc, scale=None, bf=False):
                if scale is None:
                    to = (ohot_bf if bf else ohot)[:, 4 * h % OHS:4 * h % OHS + 4, :]
                    at = loc[:, bass.ds(i * RING + 4 * h, 4)].rearrange("p (k o) -> p k o", o=1).to_broadcast([P, 4, P])
                    row = iota_row[:].rearrange("p (o e) -> p o e", o=1).to_broadcast([P, 4, P])
                    V.tensor_tensor(to, row, at, ALU.is_equal).then_inc(oh_made, 1)
                else:
                    for k in range(4 * h, 4 * h + 4):
                        last = V.tensor_scalar(ohot[:, k % OHS, :], iota_row[:], loc[:, bass.ds(i * RING + k, 1)],
                                               scale[:, bass.ds(i * RING + k, 1)], ALU.is_equal, ALU.mult)
                    last.then_inc(oh_made, 1)

            for n, s in enumerate(PLAN):
                if s[0] == "steps":
                    dve.wait_ge(consts, 3)
                    dve.wait_ge(loaded, 16 * 8)
                    bi, hi = BIASES.index("bi"), BIASES.index("hi")
                    link(V.tensor_tensor(bias[:, bi:bi + 3, :], bias[:, bi:bi + 3, :], bias[:, hi:hi + 3, :], ALU.add))
                    flat = [edge_int[:, a].rearrange("p c e -> p (c e)") for a in range(6)]
                    link(V.tensor_copy(attr[:, 0, :], flat[0]))
                    link(V.tensor_tensor(attr[:, 2, :], flat[0], flat[1], ALU.not_equal))
                    link(V.tensor_tensor(attr[:, 3, :], flat[0], flat[2], ALU.not_equal))
                    link(V.scalar_tensor_tensor(attr[:, 1, :], attr[:, 0, :], FAR, attr[:, 3, :], ALU.add, ALU.mult))
                    link(V.tensor_scalar(attr[:, 1, :], attr[:, 1, :], -FAR, None, ALU.add))
                    link(V.tensor_copy(attr[:, 4, :], flat[3]))
                    link(V.scalar_tensor_tensor(attr[:, 5, :], flat[4], float(NODES), flat[3], ALU.mult, ALU.add))
                    link(V.scalar_tensor_tensor(attr[:, 6, :], flat[3], float(REL8), flat[5], ALU.mult, ALU.add))
                    for b in range(1, BLOCKS):
                        link(V.tensor_scalar(scratch, attr[:, 0, :], float(b * P), 0.0, ALU.is_lt, ALU.add,
                                             accum_out=counts[:, b - 1:b]))
                    dve.sem_inc(to_pe, 1)
                    link(V.memset(bound[:, 0:1], 0.0))
                    link(V.memset(bound[:, BLOCKS:BLOCKS + 1], float(E)))
                    dve.wait_ge(from_pe, 1)
                    link(V.tensor_copy(bound[:, 1:BLOCKS], PS[:, 0, 0:BLOCKS - 1]))
                    link(V.tensor_copy(bound_i[:, 0, :], bound))
                    link(V.tensor_scalar(bound_i[:, 1, 0:BLOCKS], bound_i[:, 0, 1:BLOCKS + 1], -1.0, None, ALU.add))
                    link(V.tensor_scalar(bound_i[:, 0, :], bound_i[:, 0, :], 7, None, ALU.arith_shift_right))
                    link(V.tensor_scalar(bound_i[:, 1, 0:BLOCKS], bound_i[:, 1, 0:BLOCKS], 7, None, ALU.arith_shift_right))
                    first, cnt, cum, shift, step_d, ge = (small[:, j, 0:BLOCKS] for j in range(6))
                    link(V.tensor_copy(first, bound_i[:, 0, 0:BLOCKS]))
                    link(V.tensor_copy(cnt, bound_i[:, 1, 0:BLOCKS]))
                    link(V.scalar_tensor_tensor(cnt, cnt, 1.0, first, ALU.add, ALU.subtract))
                    link(V.tensor_tensor(ge, bound[:, 1:BLOCKS + 1], bound[:, 0:BLOCKS], ALU.is_gt))
                    link(V.tensor_tensor(cnt, cnt, ge, ALU.mult))
                    link(V.memset(ge, 1.0))
                    link(V.tensor_tensor_scan(cum, ge, cnt, 0.0, ALU.mult, ALU.add))
                    link(V.tensor_tensor(shift, first, cum, ALU.subtract))
                    link(V.tensor_tensor(shift, shift, cnt, ALU.add))
                    link(V.memset(step_d, 0.0))
                    link(V.tensor_tensor(step_d[:, 0:BLOCKS - 1], shift[:, 1:BLOCKS], shift[:, 0:BLOCKS - 1], ALU.subtract))
                    for c in range(CHUNKS):
                        link(V.tensor_scalar(ge, cum, tail[:, c:c + 1], 0.0, ALU.is_le, ALU.add, accum_out=where[:, 1, c:c + 1]))
                        link(V.tensor_tensor_reduce(ge2, ge, step_d, 1.0, 0.0, ALU.mult, ALU.add, where[:, 0, c:c + 1]))
                    link(V.tensor_tensor(where[:, 0, :], where[:, 0, :], tail[:], ALU.add))
                    link(V.tensor_scalar(where[:, 0, :], where[:, 0, :], float(TILES - 1), None, ALU.min))
                    for a in range(2):
                        for c in range(CHUNKS):
                            last = V.tensor_scalar(diag[:, a, c * P:(c + 1) * P], ident[:], where[:, a, c:c + 1], None, ALU.mult)
                    last.then_inc(to_pe, 1)
                    dve.wait_ge(from_pe, 2)
                    link(V.tensor_scalar(row128, PS[:, 2, :], float(P), None, ALU.mult))
                    link(V.tensor_scalar(blk[0:1, :], PS[0:1, 2, :], float(BLOCKS - 1), None, ALU.min))
                    for c in range(CHUNKS):
                        last = V.tensor_scalar(pick[:, c, :], PS[:, 1, :], tail[:, c:c + 1], None, ALU.is_equal)
                    last.then_inc(to_pe, 1)
                    dve.wait_ge(from_pe, 3)
                    link(V.tensor_tensor(dloc[:], PS[:, 0, :], row128, ALU.subtract))
                    link(V.tensor_tensor(eloc[:], PS[:, 1, :], row128, ALU.subtract))
                    for bank, name in ((2, "src"), (3, "rel"), (4, "typ")):
                        link(V.tensor_copy(idx[name][:], PS[:, bank, :]))
                    link(V.tensor_scalar(flat_of(rst_row), PS[:, 5, :], RESET, None, ALU.mult))
                    link(V.tensor_scalar(flat_of(end_row), PS[:, 6, :], RESET, None, ALU.mult))
                    link(V.tensor_scalar(where[:, 1, :], where[:, 1, :], float(P), None, ALU.mult))
                    link(V.tensor_scalar(reset_flat, PS[:, 5, :], RESET, None, ALU.mult))
                    dve.sem_inc(rows_ready, 1)
                    for c in range(CHUNKS):
                        last = V.tensor_scalar(val_row[:, c, :], PS[:, 7, c * P:(c + 1) * P], where[:, 1, c:c + 1], None, ALU.subtract)
                    link(last)
                    link(V.tensor_scalar(flat_of(sm_c), flat_of(val_row), 0.0, None, ALU.is_ge))
                    link(V.scalar_tensor_tensor(flat_of(val_row), flat_of(val_row), float(P), flat_of(sm_c), ALU.is_lt, ALU.mult))
                    link(V.tensor_reduce(has_col[:, 0, :], rst_row[:], AX_X, ALU.min))
                    V.tensor_reduce(has_col[:, 1, :], end_row[:], AX_X, ALU.min).then_inc(to_pe, 1)
                    dve.wait_ge(from_pe, 4)
                    V.tensor_copy(rowhas[0:1, :, :], PS[0:1, 0:2, :]).then_inc(rows_ready, 1)
                elif s[0] == "norm":
                    c0 = before(n, ("norm",)) * NGROUP
                    _, src, mid, _, dst, how = s

                    def wide_row(row):
                        return row.rearrange("p (o e) -> p o e", o=1).to_broadcast([P, K2, NCOL])

                    def centre(i, j):
                        dve.wait_ge(mean_in, i * 2 + (c0 + j + 1))
                        cols = bass.ds(i * (2 * NCOL) + j * NCOL, NCOL)
                        V.tensor_tensor(BIG[mid][:, :, cols], BIG[src][:, :, cols], wide_row(PS[:, j, 0:NCOL]), ALU.subtract)\
                         .then_inc(centred, 1)

                    def scale(i, j):
                        dve.wait_ge(std_out, i * 2 + (c0 + j + 1 + 2))
                        cols = bass.ds(i * (2 * NCOL) + j * NCOL, NCOL)
                        V.reciprocal(M[:, 0, cols], M[:, 0, cols]).then_inc(inverted, 1)
                        dve.wait_ge(inverted, i * 2 + (c0 + j + 1))
                        if how == "relu":
                            V.scalar_tensor_tensor(BIG[dst][:, :, cols], BIG[mid][:, :, cols], 0.0, wide_row(M[:, 0, cols]),
                                                   ALU.max, ALU.mult).then_inc(scaled, 1)
                        else:
                            for c in range(K2):
                                last = V.scalar_tensor_tensor(BIG[dst][:, c, cols], BIG[mid][:, c, cols], bias_of(how + "_g", c),
                                                              M[:, 0, cols], ALU.mult, ALU.mult)
                            last.then_inc(scaled, 1)

                    def body(i, final):
                        centre(i, 1)
                        scale(i, 0)
                        if not final:
                            centre(i + 1, 0)
                        scale(i, 1)

                    centre(0, 0)
                    with dve.Fori(0, NGROUP // 2 - 1) as i:
                        body(i, False)
                    body(NGROUP // 2 - 1, True)
                    dve.wait_ge(scaled, c0 + NGROUP)
                    if how != "relu":
                        for c in range(K2):
                            last = V.tensor_scalar(BIG[dst][:, c, :], BIG[dst][:, c, :], bias_of(how + "_b", c), None, ALU.add)
                        last.then_inc(stage_done, 1)
                    else:
                        dve.sem_inc(stage_done, 1)
                elif s[0] in ("add", "mul"):
                    begin(dve, n)
                    V.tensor_tensor(BIG[s[1]][:, :, :], BIG[s[1]][:, :, :], BIG[s[2]][:, :, :], ALU.add if s[0] == "add" else ALU.mult)\
                     .then_inc(stage_done, 1)
                elif s[0] == "add_relu":
                    begin(dve, n)
                    link(V.tensor_tensor(BIG[s[1]][:, :, :], BIG[s[1]][:, :, :], BIG[s[2]][:, :, :], ALU.add))
                    V.tensor_scalar(BIG[s[1]][:, :, :], BIG[s[1]][:, :, :], 0.0, None, ALU.max).then_inc(stage_done, 1)
                elif s[0] in TR:
                    u = before(n, TR8) * BLOCKS
                    v = before(n, TR) * BLOCKS
                    p0 = before(n, ("project",)) * BLOCKS

                    def low(i, k):
                        dve.wait_ge(mid_made, i * TRS + (p0 + k + 1))
                        V.tensor_tensor(part(i * TRS + k, 2), stage_out[:, k, :], part(i * TRS + k, 1), ALU.subtract).then_inc(low_made, 1)

                    with dve.Fori(0, BLOCKS // TRS) as i:
                        for k in range(TRS):
                            if s[0] == "project":
                                dve.wait_ge(high_made, i * TRS + (p0 + k + 1))
                                dve.wait_ge(low_made, i * TRS + (p0 + k + 1))
                                V.tensor_tensor(stage_out[:, k, :], PS[:, k, 0:D], part(i * TRS + k, 0), ALU.subtract).then_inc(tr_out, 1)
                                if k:
                                    low(i, k - 1)
                                continue
                            dve.wait_ge(tr_done, i * TRS + (u + k + 1 + TRS))
                            if s[0] == "table":
                                V.tensor_copy(A[:, bass.ds(i * TRS + k, 1), 0:D].rearrange("p o d -> p (o d)"), PS[:, k, 0:D]).then_inc(tr_out, 1)
                            else:
                                V.tensor_copy(BIG[s[2]][:, :, bass.ds(i * (TRS * P) + k * P, P)],
                                              PS[:, k, 0:D].rearrange("p (c e) -> p c e", c=K2)).then_inc(tr_out, 1)
                        if s[0] == "project":
                            low(i, TRS - 1)
                    if s[0] == "untranspose":
                        dve.wait_ge(tr_out, v + BLOCKS + TRS)
                        dve.sem_inc(stage_done, 1)
                    elif s[0] == "project":
                        dve.wait_ge(low_made, p0 + BLOCKS + TRS)
                        dve.sem_inc(stage_done, 1)
                elif s[0] == "table8":
                    begin(dve, n)
                    u = before(n, TR8) * BLOCKS
                    with dve.Fori(0, BLOCKS // TRS) as i:
                        for k in range(TRS):
                            dve.wait_ge(tr_done, i * TRS + (u + k + 1))
                            V.tensor_copy(stage_in[:, k, :].rearrange("p (c e) -> p c e", c=K2),
                                          H[:, :, bass.ds(i * (TRS * P) + k * P, P)]).then_inc(tr_in, 1)
                elif s[0] == "maxpool":
                    begin(dve, n)
                    u = before(n, EDGE) * STEPS
                    m = before(n, ("maxpool",)) * STEPS
                    a0 = before(n, ("maxpool", "sum")) * STEPS
                    link(V.memset(A, 0.0))

                    def scans(i, h):
                        dve.wait_ge(win_max, i * QUADS + (m // 4 + h + 2))
                        dve.wait_ge(back_tr, i * RING + (m + 4 * h + 4))
                        dve.wait_ge(slot_free, i * RING + (u + 4 * h + 4 + RING))
                        dve.wait_ge(reset_in[h % 2], i * 32 + 16 * (m // 8 + h // 2 + 1))
                        for c in range(K2):
                            last = V.tensor_tensor_scan(window(h % 2, c), resetw[:, h % 2, :], PS[:, 2 * (h % 2) + c, :],
                                                        window(1 - h % 2, c)[:, 4 * P - 1:4 * P], ALU.add, ALU.max)
                        last.then_inc(win_max, 1)
                        one_hots(i, h, eloc)

                    def body(i, final):
                        for h in range(QUADS):
                            if h < QUADS - 1:
                                scans(i, h + 1)
                            elif not final:
                                scans(i + 1, 0)
                            if h == 0:
                                blocks = block_regs(dve, i * RING)
                            for k in range(4 * h, 4 * h + 4):
                                dve.wait_ge(summed, i * RING + (m + k + 1 + OHS))
                                dve.wait_ge(added, i * RING + (a0 + k + 2))
                                to = A[:, bass.ds(blocks[k], 1), 0:D].rearrange("p o d -> p (o d)")
                                V.tensor_tensor(to, to, PS[:, 6 + k % 2, 0:D], ALU.add).then_inc(added, 1)

                    scans(0, 0)
                    with dve.Fori(0, STEPS // RING - 1) as i:
                        body(i, False)
                    body(STEPS // RING - 1, True)
                    dve.wait_ge(added, a0 + STEPS + 2)
                    dve.sem_inc(stage_done, 1)
                elif s[0] == "score":
                    begin(dve, n)
                    u = before(n, EDGE) * STEPS
                    g0 = before(n, GATHERS) * (STEPS // RING)
                    q = before(n, ("score",)) * STEPS

                    def body(i, final):
                        dve.wait_ge(moved, i + (q // RING + 1))
                        for h in range(QUADS):
                            for k in range(4 * h, 4 * h + 4):
                                dve.wait_ge(expanded, i * RING + (q + k + 1 + 2))
                                dve.wait_ge(gathered[k], i * 16 + 16 * (g0 + 1))
                                dve.wait_ge(slot_free, i * RING + (u + k + RING))
                                V.tensor_tensor_reduce(junk, PS[:, 2 + k % 4, 0:D], slot(k)[:, 0:D], 1.0, 0.0,
                                                       ALU.mult, ALU.add, score8[:, k:k + 1]).then_inc(slot_free, 1)
                            if h < QUADS - 2:
                                one_hots(i, h + 2, dloc, bf=True)
                            elif not final:
                                one_hots(i + 1, h + 2 - QUADS, dloc, bf=True)
                        dve.wait_ge(slot_free, i * RING + (u + RING + RING))
                        V.tensor_copy(score[:, bass.ds(i * RING, RING)], score8[:]).then_inc(moved, 1)

                    for h in range(2):
                        one_hots(0, h, dloc, bf=True)
                    with dve.Fori(0, STEPS // RING - 1) as i:
                        body(i, False)
                    body(STEPS // RING - 1, True)
                elif s[0] in ("sum", "attend"):
                    begin(dve, n)
                    u = before(n, EDGE) * STEPS
                    a0 = before(n, ("maxpool", "sum")) * STEPS
                    e0 = before(n, ("attend",)) * (STEPS // 2)
                    link(V.memset(A, 0.0))
                    scale = score if s[0] == "attend" else None
                    link(V.memset((ring_c if scale is None else ring_h)[:, :, D:ROW], 1.0))

                    def body(i, final):
                        blocks = block_regs(dve, i * RING)
                        for h in range(QUADS):
                            for k in range(4 * h, 4 * h + 4):
                                if s[0] == "attend" and k % 2:
                                    continue
                                dve.wait_ge(slot_free, i * RING + (u + k + 1 + RING))
                                to = A[:, bass.ds(blocks[k], 1), :].rearrange("p o d -> p (o d)")
                                if s[0] == "attend":
                                    dve.wait_ge(even_added, i * (RING // 2) + (e0 + k // 2 + 2))
                                    V.tensor_tensor(to, to, PS[:, k % 4, 0:ROW], ALU.add).then_inc(even_added, 1)
                                else:
                                    dve.wait_ge(added, i * RING + (a0 + k + 2))
                                    V.tensor_tensor(to, to, PS[:, k % 4, 0:ROW], ALU.add).then_inc(added, 1)
                            dve.wait_ge(slot_free, i * RING + (u + 4 * h + 4 + RING))
                            if h < QUADS - 2:
                                one_hots(i, h + 2, dloc, scale)
                            elif not final:
                                one_hots(i + 1, h + 2 - QUADS, dloc, scale)

                    for h in range(2):
                        one_hots(0, h, dloc, scale)
                    with dve.Fori(0, STEPS // RING - 1) as i:
                        body(i, False)
                    body(STEPS // RING - 1, True)
                    if s[0] == "attend":
                        dve.wait_ge(even_added, e0 + STEPS // 2 + 2)
                        dve.wait_ge(odd_added, e0 + STEPS // 2 + 2)
                        link(V.tensor_tensor(A, A, A2, ALU.add))
                    else:
                        dve.wait_ge(added, a0 + STEPS + 2)
                    total = A[:, :, D:ROW].rearrange("p b o -> p (b o)")
                    if s[0] == "attend":
                        link(V.tensor_scalar(rcol[:], total, SM_EPS, None, ALU.add))
                    else:
                        link(V.tensor_scalar(rcol[:], total, 1.0, None, ALU.max))
                    V.reciprocal(rcol[:], rcol[:]).then_inc(stage_done, 1)
                elif s[0] == "softmax":
                    f0 = pe_hands(n)
                    dve.wait_ge(from_pe, f0 + 1)
                    link(V.tensor_scalar(flat_of(sm_c), flat_of(val_row), -1.0, -LOW, ALU.add, ALU.mult))
                    link(V.tensor_tensor(flat_of(sm_b), PS[:, 0, :], flat_of(sm_c), ALU.add))
                    for c in range(CHUNKS):
                        last = V.tensor_tensor_scan(sm_a[:, c, :], rst_row[:, c, :], sm_b[:, c, :], LOW, ALU.add, ALU.max)
                    link(last)
                    V.tensor_copy(tail[:], sm_a[:, :, P - 1]).then_inc(to_pe, 1)
                    dve.wait_ge(from_pe, f0 + 2)
                    V.tensor_tensor_scan(carry[0:1, 1:SPAD + 1], rowhas[0:1, 0, :], PS[0:1, 1, :], LOW, ALU.add, ALU.max).then_inc(to_pe, 1)
                    dve.wait_ge(from_pe, f0 + 3)
                    link(V.tensor_copy(carry_col[:], PS[:, 2, 0:CHUNKS]))
                    for c in range(CHUNKS):
                        last = V.tensor_tensor_scan(sm_a[:, c, :], rst_row[:, c, :], sm_b[:, c, :], carry_col[:, c:c + 1], ALU.add, ALU.max)
                    link(last)
                    for c in range(CHUNKS):
                        last = V.tensor_tensor_scan(sm_c[:, c, ::-1], end_row[:, c, ::-1], sm_a[:, c, ::-1], LOW, ALU.add, ALU.max)
                    link(last)
                    V.tensor_copy(tail[:], sm_c[:, :, 0]).then_inc(to_pe, 1)
                    dve.wait_ge(from_pe, f0 + 4)
                    V.tensor_tensor_scan(carry[0:1, SPAD:0:-1], rowhas[0:1, 1, ::-1], PS[0:1, 1, ::-1], LOW, ALU.add, ALU.max).then_inc(to_pe, 1)
                    dve.wait_ge(from_pe, f0 + 5)
                    link(V.tensor_copy(carry_col[:], PS[:, 2, 0:CHUNKS]))
                    for c in range(CHUNKS):
                        last = V.tensor_tensor_scan(sm_c[:, c, ::-1], end_row[:, c, ::-1], sm_a[:, c, ::-1], carry_col[:, c:c + 1], ALU.add, ALU.max)
                    link(last)
                    link(V.tensor_tensor(flat_of(sm_c), flat_of(sm_b), flat_of(sm_c), ALU.subtract))
                    V.tensor_scalar(flat_of(sm_c), flat_of(sm_c), 50.0, -50.0, ALU.min, ALU.max).then_inc(arg_ready, 1)
                    dve.wait_ge(exp_done, before(n, ("softmax",)) + 1)
                    link(V.tensor_tensor(flat_of(sm_b), flat_of(sm_a), flat_of(val_row), ALU.mult))
                    V.tensor_scalar(flat_of(sm_b), flat_of(sm_b), 0.0, None, ALU.max).then_inc(to_pe, 1)
                    dve.wait_ge(from_pe, f0 + 6)
                    V.tensor_copy(score[:], PS[:, 3, :]).then_inc(stage_done, 1)


def edge_rows(src, dst, type2, type8):
    import numpy as np

    pad = SPAD * P - E
    d = np.concatenate([np.full(1, -1, np.int32), dst, np.full(pad + 1, 9999, np.int32)])
    zero = np.zeros(pad, np.int32)
    rest = [np.concatenate([a, zero]) for a in (src, type2, type8)]
    return np.stack([d[1:-1], d[:-2], d[2:], *rest])


def kernel(**inputs):
    import numpy as np
    import concourse.bacc as bacc
    from concourse.bass_utils import run_bass_kernel_spmd

    a = {k: np.asarray(v) for k, v in inputs.items()}

    def halves(w):
        return w.reshape(w.shape[0] // P, P, w.shape[1]).transpose(1, 0, 2)

    def group(ws):
        return np.concatenate([halves(w).reshape(P, -1) for w in ws], axis=1)

    x = a["x"]
    xT = np.zeros((D, NODES), x.dtype)
    xT[:, :N] = x.T
    xT = np.ascontiguousarray(halves(xT))
    ih = a["L2_gnn_W_ih"]
    w = [
        group([a["L0_gnn_Wp1"].T, a["L0_gnn_Wm1"].T, a["L0_gnn_Wm2"].T, a["L0_gnn_Wm3"].T,
               a["L1_gnn_w_in"]])[None],
        np.stack([group([a["L1_gnn_wq"][i].T, a["L1_gnn_wk"][i].T, a["L1_gnn_wv"][i].T, a["L1_gnn_wp"][i]]) for i in range(LAYERS)]),
        group([a["L2_gnn_W_rel"][0].T, a["L2_gnn_W_rel"][1].T, ih[0:D].T, ih[2 * D:3 * D].T, ih[3 * D:4 * D].T,
               a["L2_gnn_W1"].T, a["L2_gnn_W2"].T, a["L2_gnn_W3"].T])[None],
        group([a["L3_gnn_weight"].transpose(1, 0, 2).reshape(D, REL8 * D), a["L3_gnn_sl_w"].T])[None],
    ]
    bih, bhh = a["L2_gnn_b_ih"], a["L2_gnn_b_hh"]
    b = [a["L0_gnn_bp1"], a["L0_gnn_bm1"], a["L0_gnn_bm2"], a["L0_gnn_bm3"], a["L0_gnn_ln2_g"], a["L0_gnn_ln2_b"],
         a["L0_gnn_ln3_g"], a["L0_gnn_ln3_b"], a["L1_gnn_b_in"], *a["L1_gnn_bp"], *a["L2_gnn_b_rel"],
         bih[0:D], bih[2 * D:3 * D], bih[3 * D:], bhh[0:D], bhh[2 * D:3 * D], bhh[3 * D:],
         a["L2_gnn_b1"], a["L2_gnn_b2"], a["L2_gnn_b3"], a["L3_gnn_sl_b"]]
    bias = np.zeros((len(b), D), x.dtype)
    for i, v in enumerate(b):
        bias[i, :len(v)] = v
    bias = np.ascontiguousarray(bias.reshape(len(b), K2, P).transpose(2, 0, 1))

    nc = bacc.Bacc("TRN2", target_bir_lowering=False, num_devices=1)
    arrays = {}

    def put(name, v):
        arrays[name] = np.ascontiguousarray(v)
        return nc.dram_tensor(name, v.shape, mybir.dt.from_np(v.dtype), kind="ExternalInput").ap()

    e = put("edges", edge_rows(a["src"], a["dst"], a["edge_type_2"], a["edge_type_8"]))
    args = [e, put("xT", xT), [put(f"w{i}", v) for i, v in enumerate(w)], put("bias_in", bias)]
    args.append(nc.dram_tensor("outT", (P, K2, N), F32, kind="ExternalOutput").ap())
    for name, shape, dt in (("table", (NODES, D), F32), ("table_rel", (REL2 * NODES, D), F32),
                            ("table_typ", (REL8 * NODES, D), F32), ("spill", (STEPS, P, D), F32), ("resets", (SPAD, P), BF16)):
        args.append(nc.dram_tensor(name, shape, dt, kind="Internal").ap())
    gnn_kernel(nc, *args)
    r = run_bass_kernel_spmd(nc, [arrays], core_ids=[0])
    got = r.results[0]["outT"]
    return np.ascontiguousarray(got.transpose(2, 1, 0).reshape(N, D))
```

```python
from contextlib import ExitStack

import concourse.bass as bass
from concourse import mybir

F32 = mybir.dt.float32
BF16 = mybir.dt.bfloat16
I32 = mybir.dt.int32
ALU = mybir.AluOpType
ACT = mybir.ActivationFunctionType
AX_X = mybir.AxisListType.X

P = 128
N = 3125
E = 50000
D = 256
K2 = D // P
TILES = -(-E // P)
BLOCKS = -(-N // P)
NODES = BLOCKS * P
RING = 16
HALF = RING // 2
QUADS = RING // 4
UNROLL = 2 * RING
OHS = 8
SIDE = range(1, 16, 2)
MAIN = [k for k in range(RING) if k not in SIDE]
STEPS = -(-(TILES + BLOCKS - 1) // UNROLL) * UNROLL
SPAD = 512
CHUNKS = SPAD // P
assert TILES <= SPAD and STEPS <= SPAD
NCOL = 400
NGROUP = NODES // NCOL
TRS = 5
ROW = D + 1
EPS = 1e-5
RESET = -2e38
LOW = -1e30
SM_EPS = 1e-9
LAYERS = 3
FAR = 1e6
FUNCS = {"Relu": ACT.Relu, "Identity": ACT.Identity,
         "Sigmoid": ACT.Sigmoid, "Tanh": ACT.Tanh}
REL2, REL8 = 2, 8

GROUPS = [
    [("Wp1", 2, 256), ("Wm1", 4, 256), ("Wm2", 4, 256), ("Wm3", 4, 256), ("w_in", 2, 256)],
    [("wq", 2, 256), ("wk", 2, 256), ("wv", 2, 256), ("wp", 2, 256)],
    [("rel0", 2, 256), ("rel1", 2, 256), ("ih_i", 2, 256), ("ih_g", 2, 256), ("ih_o", 2, 256),
     ("W1", 2, 128), ("W2", 1, 128), ("W3", 1, 256)],
    [("typ", 2, REL8 * 256), ("self", 2, 256)],
]
BIASES = ["bp1", "bm1", "bm2", "bm3", "ln2_g", "ln2_b", "ln3_g", "ln3_b", "b_in", "bp_0", "bp_1", "bp_2",
          "br_0", "br_1", "bi", "bg", "bo", "hi", "hg", "ho", "b1", "b2", "b3", "slb"]


def plan():
    pool_layer = [("maxpool",), ("untranspose", None, "C")]
    s = [("steps",), ("norm", "X", "B", "C", "H", "relu")]
    s += [("dense", "Wp1", ["H"], "B", "Relu", "bp1"), ("table", "B"), *pool_layer]
    s += [("dense", "Wm1", ["H", "C"], "B", "Relu", "bm1"), ("table", "B"), *pool_layer]
    s += [("dense", "Wm2", ["B", "C"], "H", "Relu", "bm2", ("H", "B"))]
    s += [("norm", "H", "B", "C", "B", "ln2"), ("table", "B"), *pool_layer]
    s += [("dense", "Wm3", ["B", "C"], "H", "Relu", "bm3", ("H", "B")), ("load", 1, 0)]
    s += [("norm", "H", "B", "C", "B", "ln3"), ("add", "X", "B"), ("norm", "X", "B", "C", "H", "relu")]
    s += [("dense", "w_in", ["H"], "B", "Relu", "b_in"), ("table", "B")]
    for layer in range(LAYERS):
        s += [("fold",), ("load", 1, layer + 1) if layer < LAYERS - 1 else ("load", 2, 0)]
        s += [("project", "B"), ("score",), ("softmax",), ("attend",), ("untranspose", "ssum", "C")]
        s += [("dense", "Wvp", ["C"], "H", "Identity", f"bp_{layer}", ("B", "H", "relu"))]
        if layer < LAYERS - 1:
            s += [("table", "B")]
    s += [("add", "X", "B"), ("norm", "X", "B", "C", "H", "relu")]
    for r in range(REL2):
        s += [("dense", f"rel{r}", ["H"], "B", "Relu", f"br_{r}"), ("dense", f"rel{r}", ["B"], "C", "Relu", f"br_{r}"),
              ("table", "C", "rel", r)]
    s += [("sum", "rel"), ("untranspose", None, "C")]
    s += [("dense", "ih_i", ["C"], "B", "Sigmoid", "bi"), ("dense", "ih_g", ["C"], "H", "Tanh", "bg", ("B", "H", "mul"))]
    s += [("tanh", "B"), ("dense", "ih_o", ["C"], "H", "Sigmoid", "bo", ("H", "B", "mul"))]
    s += [("dense", "W1", ["H"], "B", "Relu", "b1"), ("dense", "W2", ["B"], "C", "Relu", "b2"),
          ("dense", "W3", ["C"], "B", "Identity", "b3", ("X", "B")), ("load", 3, 0)]
    s += [("norm", "X", "B", "C", "H", "relu"), ("table8", "H"), ("dense", "self", ["H"], "B", "Identity", "slb", ("X", "B"))]
    s += [("sum", "typ"), ("untranspose", "deg", "C"), ("add", "X", "C"), ("store",)]
    return s


def gnn_kernel(nc, edges, xT, weights, biases, out, table, table_rel, table_typ, spill, resets):
    PLAN = plan()
    FIRST = {kind: [n for n, s in enumerate(PLAN) if s[0] == kind][0] for kind in {s[0] for s in PLAN}}
    with ExitStack() as ctx:
        def sb(name, shape, dt=F32):
            return ctx.enter_context(nc.sbuf_tensor(name, shape, dt))

        def sem(name):
            return ctx.enter_context(nc.semaphore(name))

        X = sb("X", [P, K2, NODES])
        HC = sb("HC", [P, 2 * K2 * NODES])
        H = HC[:, 0:K2 * NODES].rearrange("p (c n) -> p c n", c=K2)
        C = HC[:, K2 * NODES:].rearrange("p (c n) -> p c n", c=K2)
        B = sb("B", [P, K2, NODES])
        AM = sb("AM", [P, BLOCKS * ROW + NODES])
        A = AM[:, 0:BLOCKS * ROW].rearrange("p (b r) -> p b r", r=ROW)
        A2 = HC[:, 2 * K2 * NODES - BLOCKS * ROW:].rearrange("p (b r) -> p b r", r=ROW)
        M = AM[:, BLOCKS * ROW:].rearrange("p (o n) -> p o n", o=1)
        G = AM[:, 0:BLOCKS * 3 * D // 2].bitcast(BF16).rearrange("p (b s d) -> p b s d", s=3, d=D)
        BIG = {"X": X, "H": H, "B": B, "C": C, "M": M}
        def window(h, c):
            return C[:, c, h * 4 * P:(h + 1) * 4 * P]

        W = sb("W", [P, max(sum(k * m for _, k, m in g) for g in GROUPS)])
        Wfold = sb("Wfold", [P, 2, K2, D])
        bias = sb("bias", [P, len(BIASES), K2])
        ring = sb("ring", [P, HALF, ROW])
        ring_c = C[:, 0, 8 * P:8 * P + HALF * ROW].rearrange("p (k r) -> p k r", r=ROW)
        ring_h = HC[:, 0:RING * ROW].rearrange("p (k r) -> p k r", r=ROW)

        def slot(k):
            return ring[:, k, :] if k < HALF else ring_c[:, k - HALF, :]

        work = sb("work", [P, 2 * TRS * D])
        stage_in = work[:, 0:TRS * D].rearrange("p (k d) -> p k d", d=D)
        stage_out = work[:, TRS * D:].rearrange("p (k d) -> p k d", d=D)
        ohot = work[:, 0:OHS * P].rearrange("p (k e) -> p k e", e=P)
        ohot_bf = work[:, 0:OHS * P // 2].bitcast(BF16).rearrange("p (k e) -> p k e", e=P)
        back = work[:, 1024:2048].rearrange("p (a d) -> p a d", a=2)
        junk = work[:, 1536:1792]
        side_rows = work[:, 0:len(SIDE) * ROW].rearrange("p (k r) -> p k r", r=ROW)
        weighted_hot = ring[:].rearrange("p k r -> p (k r)")[:, 0:RING * P].rearrange("p (k e) -> p k e", e=P)
        resetw = work[:, 2048:2560].bitcast(BF16).rearrange("p (h e) -> p h e", h=2)
        ohT = work[:, 2304:2432].bitcast(BF16).rearrange("p (k e) -> p k e", e=P)
        ident = sb("ident", [P, P])
        identb = sb("identb", [P, P], BF16)
        ones = sb("ones", [P, P])
        meanw = sb("meanw", [P, K2, P])
        epsc = sb("epsc", [P, 1])
        iota_row = sb("iota_row", [P, P])
        idx = {n: sb(f"idx_{n}", [P, SPAD], I32) for n in ("src", "rel", "typ")}
        idx_now = sb("idx_now", [P, 2, RING], I32)
        dloc = sb("dloc", [P, SPAD])
        eloc = sb("eloc", [P, SPAD])
        score = sb("score", [P, SPAD])
        score8 = sb("score8", [P, RING])
        rst_row = sb("rst_row", [P, CHUNKS, P])
        end_row = sb("end_row", [P, CHUNKS, P])
        val_row = sb("val_row", [P, CHUNKS, P])
        blk = sb("blk", [1, SPAD], I32)
        rowhas = sb("rowhas", [1, 2, SPAD])
        carry = sb("carry", [1, SPAD + 2])
        carry_col = sb("carry_col", [P, CHUNKS])
        tail = sb("tail", [P, CHUNKS])
        rcol = sb("rcol", [P, BLOCKS])
        sm_a = stage_in[:, 0:2, :].rearrange("p a d -> p (a d)").rearrange("p (c e) -> p c e", e=P)
        sm_b = stage_in[:, 2:4, :].rearrange("p a d -> p (a d)").rearrange("p (c e) -> p c e", e=P)
        sm_c = stage_out[:, 0:2, :].rearrange("p a d -> p (a d)").rearrange("p (c e) -> p c e", e=P)
        PS = ctx.enter_context(nc.psum_tensor("PS", [P, 8, 512], F32))
        PSB = PS[:].rearrange("p b e -> p (b e)").bitcast(BF16).rearrange("p (b e) -> p b e", b=8)


        flatB = B[:].rearrange("p c n -> p (c n)")
        flatC = HC[:, K2 * NODES:]
        flatH = HC[:, 0:K2 * NODES]
        edge_int = flatB[:, 0:6 * SPAD].bitcast(I32).rearrange("p (a c e) -> p a c e", a=6, e=P)
        scratch = flatB[:, 6 * SPAD:7 * SPAD]
        counts = flatB[:, 7 * SPAD:7 * SPAD + 32]
        small = flatB[:, 7 * SPAD + 32:7 * SPAD + 224].rearrange("p (j b) -> p j b", b=32)
        bound = flatB[:, 7 * SPAD + 224:7 * SPAD + 224 + BLOCKS + 1]
        ge2 = flatB[:, 7 * SPAD + 256:7 * SPAD + 256 + BLOCKS]
        bound_i = flatB[:, 7 * SPAD + 288:7 * SPAD + 288 + 2 * (BLOCKS + 1)].bitcast(I32).rearrange("p (a b) -> p a b", a=2)
        where = flatB[:, 7 * SPAD + 352:7 * SPAD + 352 + 2 * CHUNKS].rearrange("p (a c) -> p a c", a=2)
        has_col = flatB[:, 7 * SPAD + 368:7 * SPAD + 368 + 2 * CHUNKS].rearrange("p (a c) -> p a c", a=2)
        attr = flatC[:, 0:7 * SPAD].rearrange("p (a s) -> p a s", a=7)
        diag = flatH[:, 0:2 * SPAD].rearrange("p (a s) -> p a s", a=2)
        row128 = flatH[:, 2 * SPAD:3 * SPAD]
        pick = flatH[:, 3 * SPAD:7 * SPAD].rearrange("p (c s) -> p c s", c=CHUNKS)
        reset_flat = flatH[:, 7 * SPAD:7 * SPAD + SPAD // 2].bitcast(BF16)
        reset_bf = reset_flat.rearrange("p (c e) -> p c e", e=P)

        def flat_of(rows):
            return rows[:, :, :].rearrange("p c e -> p (c e)")

        def wide(k):
            base, at = (flatB, k) if k < 3 else (flatC, k - 3)
            return base[:, at * REL8 * D:(at + 1) * REL8 * D]

        wview = {}
        for g in GROUPS:
            at = 0
            for name, k, m in g:
                wview[name] = W[:, at:at + k * m].rearrange("p (k m) -> p k m", k=k)
                at += k * m
        wview["Wqk"] = Wfold[:, 0]
        wview["Wvp"] = Wfold[:, 1]
        wview["mean"] = meanw

        def bias_of(name, c):
            return bias[:, BIASES.index(name), c:c + 1]

        stage_done = sem("stage_done")
        consts = sem("consts")
        vec = sem("vec")
        loaded = sem("loaded")
        weighted = sem("weighted")
        to_pe = sem("to_pe")
        from_pe = sem("from_pe")
        rows_ready = sem("rows_ready")
        arg_ready = sem("arg_ready")
        exp_done = sem("exp_done")
        half_ready = sem("half_ready")
        mm_done = sem("mm_done")
        mm_out = sem("mm_out")
        joined = sem("joined")
        clipped = sem("clipped")
        tr_in = sem("tr_in")
        tr_done = sem("tr_done")
        tr_out = sem("tr_out")
        tabled = sem("tabled")
        wided = [sem(f"wided{k}") for k in range(TRS)]
        mean_in = sem("mean_in")
        centred = sem("centred")
        squared = sem("squared")
        var_in = sem("var_in")
        std_out = sem("std_out")
        inverted = sem("inverted")
        scaled = sem("scaled")
        high_made = sem("high_made")
        mid_made = sem("mid_made")
        low_made = sem("low_made")
        gathered = [sem(f"gathered{k}") for k in range(RING)]
        reloaded = [sem(f"reloaded{k}") for k in range(HALF)]
        slot_free = sem("slot_free")
        spilled = [sem(f"spilled{k}") for k in range(RING)]
        passed = sem("passed")
        staged = sem("staged")
        reset_in = [sem(f"reset_in{h}") for h in range(2)]
        win_max = sem("win_max")
        back_tr = sem("back_tr")
        back_in = sem("back_in")
        oh_made = sem("oh_made")
        oh_tr = sem("oh_tr")
        oht_in = sem("oht_in")
        expanded = sem("expanded")
        summed = sem("summed")
        added = sem("added")
        main_added = sem("main_added")
        side_out = sem("side_out")
        side_added = sem("side_added")
        cleared = sem("cleared")
        moved = sem("moved")
        stored = sem("stored")

        block = ctx.enter_context(nc.Block())

        def before(n, kinds):
            return sum(1 for s in PLAN[:n] if s[0] in kinds)

        def groups_before(n):
            return (sum(NGROUP * halves_out(s) for s in PLAN[:n] if s[0] == "dense")
                    + 4 * BLOCKS * before(n, ("table8",)))

        def halves_out(s):
            return 1 if s[1] in ("mean", "W1", "W2") else 2

        TR = ("table", "untranspose", "project")
        TR8 = TR + ("table8",)
        EDGE = ("maxpool", "score", "attend", "sum")
        GATHERS = ("maxpool", "score", "sum")

        def pe_hands(n):
            return 4 * before(n, ("steps",)) + before(n, ("fold",)) + 6 * before(n, ("softmax",))

        def dve_hands(n):
            return 4 * before(n, ("steps",)) + 5 * before(n, ("softmax",))

        def one(rows, at):
            return rows[bass.ds(at, 1)].rearrange("o p d -> (o p) d")

        def begin(eng, n):
            ended = sum(1 for s in PLAN[:n] if s[0] != "load")
            if ended:
                eng.wait_ge(stage_done, ended)

        def weights_in(eng, n):
            eng.wait_ge(weighted, 16 * (1 + before(n, ("load",))))

        def part(b, a):
            return G[:, bass.ds(b, 1), a, :].rearrange("p o d -> p (o d)")

        def block_regs(eng, s, count=RING):
            regs = nc.values_load_multi_w_load_instructions(
                blk[0:1, bass.ds(s, count)], engines=(eng.engine,), min_val=0, max_val=BLOCKS - 1,
                skip_runtime_bounds_check_because="the table is cut to the last block")[1]
            return regs

        @block.gpsimd
        def _(pool):
            pool.memset(ones[:], 1.0)
            pool.memset(meanw[:], 1.0 / D)
            pool.memset(epsc[:], EPS)
            pool.memset(score[:], 0.0)
            pool.memset(carry[:], LOW)
            pool.memset(ident[:], 0.0).then_inc(consts, 1)
            pool.iota(iota_row[:], pattern=[[1, P]], base=0, channel_multiplier=0,
                      allow_small_or_imprecise_dtypes=True)
            pool.iota(tail[:], pattern=[[P, CHUNKS]], base=0, channel_multiplier=1,
                      allow_small_or_imprecise_dtypes=True)
            pool.wait_ge(consts, 1)
            pool.affine_select(out=ident[:], in_=ident[:], compare_op=ALU.not_equal, fill=1.0, base=0,
                               pattern=[[-1, P]], channel_multiplier=1).then_inc(consts, 1)
            pool.wait_ge(consts, 2)
            pool.tensor_copy(identb[:], ident[:]).then_inc(consts, 1)
            for n, s in enumerate(PLAN):
                if s[0] == "project":
                    p0 = before(n, ("project",)) * BLOCKS
                    with pool.Fori(0, BLOCKS // TRS) as i:
                        for k in range(TRS):
                            pool.wait_ge(tr_out, i * TRS + (before(n, TR) * BLOCKS + k + 1 + TRS))
                            pool.sem_inc(passed, 1)
                            pool.tensor_copy(part(i * TRS + k, 1), stage_out[:, k, :]).then_inc(mid_made, 1)
                if s[0] == "softmax":
                    begin(pool, n)
                    pool.memset(A2, 0.0)
                    pool.memset(A, 0.0)
                    pool.memset(ring_h[:, :, D:ROW], 1.0).then_inc(cleared, 1)
                if s[0] == "attend":
                    begin(pool, n)
                    bodies = before(n, ("attend",)) * (STEPS // RING)
                    pool.wait_ge(cleared, before(n, ("attend",)) + 1)
                    with pool.Fori(0, STEPS // RING) as i:
                        blocks = block_regs(pool, i * RING)
                        for j, k in enumerate(SIDE):
                            pool.wait_ge(side_out, i * len(SIDE) + (bodies * len(SIDE) + j + 1 + RING))
                            pool.wait_ge(side_added, i * len(SIDE) + (bodies * len(SIDE) + j + RING))
                            pool.sem_inc(passed, 1)
                            to = A2[:, bass.ds(blocks[k], 1), :].rearrange("p o d -> p (o d)")
                            pool.tensor_tensor(to, to, side_rows[:, j, :], ALU.add).then_inc(side_added, 1)
                if s[0] not in ("maxpool", "score", "sum"):
                    continue
                begin(pool, n)
                gathers = before(n, ("maxpool", "score", "sum")) * STEPS
                uses = before(n, EDGE) * STEPS
                spills = 1 + before(n, ("score",)) * (STEPS // RING)
                src = {"rel": table_rel, "typ": table_typ}.get(s[-1], table)
                ids = idx[s[-1]] if s[0] == "sum" else idx["src"]
                with pool.Fori(0, STEPS // UNROLL) as i:
                    for h in range(2):
                        pool.wait_ge(slot_free, i * UNROLL + (uses + h * RING + 1))
                        pool.tensor_copy(idx_now[:, h, :], ids[:, bass.ds(i * UNROLL + h * RING, RING)]).then_inc(staged, 1)
                        pool.wait_ge(staged, i * 2 + (gathers // RING + h + 1))
                        for k in range(RING):
                            pool.wait_ge(slot_free, i * UNROLL + (uses + h * RING + k + 1))
                            if s[0] == "score":
                                pool.wait_ge(spilled[k], i * 32 + 16 * (spills + h))
                            pool.sem_inc(passed, 1)
                            pool.indirect_dma_start(
                                slot(k)[:, 0:D], None, src,
                                bass.IndirectOffsetOnAxis(ap=idx_now[:, h, k:k + 1], axis=0)).then_inc(gathered[k], 16)

        @block.sync
        def _(sp):
            for n, s in enumerate(PLAN):
                if s[0] == "steps":
                    for a in range(6):
                        sp.dma_start(edge_int[:, a], edges[a].rearrange("(c p e) -> p c e", c=CHUNKS, e=P)).then_inc(loaded, 16)
                    sp.dma_start(bias[:], biases).then_inc(loaded, 16)
                    sp.dma_start(X[:], xT).then_inc(loaded, 16)
                    sp.dma_start(W[:, 0:sum(k * m for _, k, m in GROUPS[0])], weights[0][0]).then_inc(weighted, 16)
                    for k in range(TRS):
                        sp.dma_start(spill[0, k:k + 1, 0:1], biases[0:1, 0, 0:1]).then_inc(wided[k], 16)
                    for k in range(RING):
                        sp.dma_start(spill[1, k:k + 1, 0:1], biases[0:1, 0, 0:1]).then_inc(spilled[k], 16)
                    for credit in wided + spilled:
                        sp.wait_ge(credit, 16)
                    sp.wait_ge(loaded, 16 * 8)
                    sp.wait_ge(rows_ready, 1)
                    sp.dma_start(resets.rearrange("(c q) e -> q c e", q=P), reset_bf).then_inc(stored, 16)
                    sp.wait_ge(stored, 16)
                    sp.wait_ge(rows_ready, 2)
                    sp.sem_inc(stage_done, 1)
                elif s[0] == "load":
                    begin(sp, n)
                    width = sum(k * m for _, k, m in GROUPS[s[1]])
                    sp.dma_start(W[:, 0:width], weights[s[1]][s[2]]).then_inc(weighted, 16)
                elif s[0] == "table":
                    begin(sp, n)
                    u = before(n, TR) * BLOCKS
                    t = before(n, ("table",))
                    to = table if len(s) == 2 else table_rel[s[3] * NODES:(s[3] + 1) * NODES, :]
                    rows = to.rearrange("(b p) d -> p b d", p=P)
                    with sp.Fori(0, BLOCKS // TRS) as i:
                        sp.wait_ge(tr_out, i * TRS + (u + TRS + TRS))
                        sp.dma_start(rows[:, bass.ds(i * TRS, TRS), :], A[:, bass.ds(i * TRS, TRS), 0:D]).then_inc(tabled, 16)
                    sp.wait_ge(tabled, 16 * (t + 1) * (BLOCKS // TRS))
                    sp.sem_inc(stage_done, 1)
                elif s[0] == "table8":
                    begin(sp, n)
                    g0 = groups_before(n)
                    rows = table_typ.rearrange("(b p r) d -> b p (r d)", p=P, r=REL8)
                    with sp.Fori(0, BLOCKS // TRS) as i:
                        for k in range(TRS):
                            sp.wait_ge(mm_out, i * (4 * TRS) + (g0 + 4 * k + 4 + 4))
                            sp.dma_start(one(rows, i * TRS + k), wide(k)).then_inc(wided[k], 16)
                    for k in range(TRS):
                        sp.wait_ge(wided[k], 16 * (1 + BLOCKS // TRS))
                    sp.sem_inc(stage_done, 1)
                elif s[0] == "maxpool":
                    begin(sp, n)
                    m = before(n, ("maxpool",)) * (STEPS // 4)
                    rows = resets.rearrange("(g a) e -> g (a e)", a=4)
                    with sp.Fori(0, STEPS // 8) as i:
                        for h in range(2):
                            sp.wait_ge(win_max, i * 2 + (m + h + 1))
                            sp.dma_start(resetw[:, h, :], rows[bass.ds(i * 2 + h, 1), :].to_broadcast([P, 4 * P]))\
                              .then_inc(reset_in[h], 16)
                elif s[0] == "score":
                    begin(sp, n)
                    g0 = before(n, GATHERS) * (STEPS // RING)
                    with sp.Fori(0, STEPS // RING) as i:
                        for k in range(RING):
                            sp.wait_ge(gathered[k], i * 16 + 16 * (g0 + 1))
                            sp.dma_start(one(spill, i * RING + k), slot(k)[:, 0:D]).then_inc(spilled[k], 16)
                    for k in range(RING):
                        sp.wait_ge(spilled[k], 16 * (1 + (before(n, ("score",)) + 1) * (STEPS // RING)))
                    sp.wait_ge(moved, (before(n, ("score",)) + 1) * (STEPS // RING) + 1)
                    sp.sem_inc(stage_done, 1)
                elif s[0] == "attend":
                    begin(sp, n - 1)
                    u = before(n, EDGE) * STEPS
                    rows = spill.rearrange("s p d -> p s d")
                    with sp.Fori(0, STEPS // RING) as i:
                        for k in range(0, RING, 2):
                            sp.wait_ge(slot_free, i * RING + (u + k + 2))
                            sp.dma_start(ring_h[:, k:k + 2, 0:D], rows[:, bass.ds(i * RING + k, 2), :]).then_inc(reloaded[k // 2], 16)
                elif s[0] == "store":
                    begin(sp, n)
                    sp.dma_start(out, X[:, :, 0:N]).then_inc(stored, 16)
                    sp.wait_ge(stored, 32)

        @block.scalar
        def _(act):
            for n, s in enumerate(PLAN):
                if s[0] == "dense":
                    w, ins, to, func, b = s[1:6]
                    halves = halves_out(s)
                    g0 = groups_before(n)
                    dst = BIG[to]
                    with act.Fori(0, NGROUP // 2) as i:
                        for j in range(2 * halves):
                            cols = bass.ds(i * (2 * NCOL) + (j // halves) * NCOL, NCOL)
                            act.wait_ge(mm_done, i * (2 * halves) + (g0 + j + 1))
                            more = {}
                            if b:
                                more["bias"] = bias_of(b, j % halves)
                            fn = FUNCS[func]
                            nc.scalar.activation(dst[:, j % halves, cols], PS[:, j, 0:NCOL], fn, **more).then_inc(mm_out, 1)
                    if len(s) == 6:
                        act.wait_ge(mm_out, g0 + NGROUP * halves + 4)
                        act.sem_inc(stage_done, 1)
                elif s[0] in TR:
                    begin(act, n)
                    u = before(n, TR8) * BLOCKS
                    p0 = before(n, ("project",)) * BLOCKS

                    def copy_in(i, k):
                        act.wait_ge(tr_done, i * TRS + (u + k + 1))
                        dst = stage_in[:, k, :]
                        if s[0] == "untranspose":
                            src = A[:, bass.ds(i * TRS + k, 1), 0:D].rearrange("p o d -> p (o d)")
                            more = {"scale": rcol[:, bass.ds(i * TRS + k, 1)]} if s[1] else {}
                            nc.scalar.activation(dst, src, ACT.Copy, **more).then_inc(tr_in, 1)
                        else:
                            src = BIG[s[1]][:, :, bass.ds(i * (TRS * P) + k * P, P)]
                            nc.scalar.activation(dst.rearrange("p (c e) -> p c e", c=K2), src, ACT.Copy).then_inc(tr_in, 1)

                    with act.Fori(0, BLOCKS // TRS) as i:
                        for k in range(TRS):
                            if k == 0 or s[0] != "project":
                                copy_in(i, k)
                            if s[0] == "project":
                                if k < TRS - 1:
                                    copy_in(i, k + 1)
                                act.wait_ge(tr_done, i * TRS + (u + k + 1 + TRS))
                                nc.scalar.activation(part(i * TRS + k, 0), PS[:, k, 0:D], ACT.Copy).then_inc(high_made, 1)
                elif s[0] == "norm":
                    c0 = before(n, ("norm",)) * NGROUP

                    def square(i, j):
                        act.wait_ge(centred, i * 2 + (c0 + j + 1))
                        cols = bass.ds(i * (2 * NCOL) + j * NCOL, NCOL)
                        nc.scalar.activation(BIG[s[3]][:, :, cols], BIG[s[2]][:, :, cols], ACT.Square).then_inc(squared, 1)

                    def root(i, j):
                        act.wait_ge(var_in, i * 2 + (c0 + j + 1))
                        nc.scalar.activation(M[:, 0, bass.ds(i * (2 * NCOL) + j * NCOL, NCOL)], PS[:, 2 + j, 0:NCOL],
                                             ACT.Sqrt, bias=epsc[:]).then_inc(std_out, 1)

                    def body(i, final):
                        for j in range(2):
                            root(i, j)
                            if not final:
                                square(i + 1, j)

                    square(0, 0)
                    square(0, 1)
                    with act.Fori(0, NGROUP // 2 - 1) as i:
                        body(i, False)
                    body(NGROUP // 2 - 1, True)
                elif s[0] == "tanh":
                    begin(act, n)
                    nc.scalar.activation(BIG[s[1]][:, :, :], BIG[s[1]][:, :, :], ACT.Tanh).then_inc(stage_done, 1)
                elif s[0] == "table8":
                    g0 = groups_before(n)
                    with act.Fori(0, BLOCKS // TRS) as i:
                        for k in range(TRS):
                            act.wait_ge(wided[k], i * 16 + 16)
                            for q in range(4):
                                act.wait_ge(mm_done, i * (4 * TRS) + (g0 + 4 * k + q + 1))
                                nc.scalar.activation(wide(k)[:, q * 512:(q + 1) * 512], PS[:, (4 * k + q) % 8, :],
                                                     ACT.Copy).then_inc(mm_out, 1)
                elif s[0] == "fold":
                    act.wait_ge(from_pe, pe_hands(n) + 1)
                    for f in range(2):
                        for c in range(K2):
                            last = nc.scalar.activation(Wfold[:, f, c, :], PS[:, 2 * f + c, 0:D], ACT.Copy,
                                                        scale=float(D) ** -0.5 if f == 0 else 1.0)
                    last.then_inc(stage_done, 1)
                elif s[0] == "maxpool":
                    m = before(n, ("maxpool",)) * STEPS
                    with act.Fori(0, STEPS // RING) as i:
                        for k in range(0, RING, 2):
                            act.wait_ge(back_tr, i * RING + (m + k + 2 + 8))
                            act.wait_ge(summed, i * RING + (m + k - 2 + OHS))
                            nc.scalar.activation(back[:, k // 2 % 2, :], PS[:, 4 + k // 2 % 2, :], ACT.Copy).then_inc(back_in, 2)
                elif s[0] == "score":
                    q = before(n, ("score",)) * STEPS
                    with act.Fori(0, STEPS // RING) as i:
                        for k in range(RING):
                            act.wait_ge(oh_tr, i * RING + (q + k + 1 + OHS))
                            act.wait_ge(expanded, i * RING + (q + k + 1))
                            nc.scalar.activation(ohT[:, k % 2, :], PSB[:, k % 2, 0:P], ACT.Copy).then_inc(oht_in, 1)
                elif s[0] == "attend":
                    begin(act, n)
                    u = before(n, EDGE) * STEPS
                    bodies = before(n, ("attend",)) * (STEPS // RING)
                    with act.Fori(0, STEPS // RING) as i:
                        for j, k in enumerate(SIDE):
                            act.wait_ge(slot_free, i * RING + (u + k + 1 + RING))
                            act.wait_ge(side_added, i * len(SIDE) + ((bodies - 1) * len(SIDE) + j + 1 + RING))
                            nc.scalar.activation(side_rows[:, j, :], PS[:, k % 8, 0:ROW], ACT.Copy).then_inc(side_out, 1)
                elif s[0] == "softmax":
                    act.wait_ge(arg_ready, before(n, ("softmax",)) + 1)
                    nc.scalar.activation(sm_a, sm_c, ACT.Exp).then_inc(exp_done, 1)

        @block.tensor
        def _(pe):
            pe.wait_ge(consts, 3)
            for n, s in enumerate(PLAN):
                if s[0] == "dense":
                    w, ins, to, func, b = s[1:6]
                    begin(pe, n)
                    weights_in(pe, n)
                    halves = halves_out(s)
                    g0 = groups_before(n)
                    wt = wview[w]
                    ks = [(BIG[x], c) for x in ins for c in range(K2)][:wt.shape[1]]
                    with pe.Fori(0, NGROUP // 2) as i:
                        for j in range(2 * halves):
                            cols = bass.ds(i * (2 * NCOL) + (j // halves) * NCOL, NCOL)
                            c = j % halves
                            pe.wait_ge(mm_out, i * (2 * halves) + (g0 + j + 1 + (4 - 2 * halves)))
                            for q, (x, xc) in enumerate(ks):
                                last = nc.tensor.matmul(PS[:, j, 0:NCOL], wt[:, q, c * P:(c + 1) * P], x[:, xc, cols],
                                                        start=(q == 0), stop=(q == len(ks) - 1))
                            last.then_inc(mm_done, 1)
                elif s[0] in TR:
                    u = before(n, TR8) * BLOCKS
                    v = before(n, TR) * BLOCKS
                    if s[0] == "project":
                        begin(pe, n)
                    with pe.Fori(0, BLOCKS // TRS) as i:
                        for k in range(TRS):
                            pe.wait_ge(tr_in, i * TRS + (u + k + 1))
                            pe.wait_ge(tr_out, i * TRS + (v + k + 1))
                            for c in range(K2):
                                half = stage_in[:, k, c * P:(c + 1) * P]
                                if s[0] == "project":
                                    last = nc.tensor.matmul(PS[:, k, 0:D], half, wview["Wqk"][:, c, :], start=(c == 0), stop=(c == K2 - 1))
                                else:
                                    last = nc.tensor.transpose(PS[:, k, c * P:(c + 1) * P], half, ident[:])
                            last.then_inc(tr_done, 1)
                elif s[0] == "norm":
                    begin(pe, n)
                    c0 = before(n, ("norm",)) * NGROUP

                    def mean(i, j):
                        if not (isinstance(i, int) and i == 0):
                            pe.wait_ge(centred, i * 2 + (c0 + j - 1))
                        cols = bass.ds(i * (2 * NCOL) + j * NCOL, NCOL)
                        for c in range(K2):
                            last = nc.tensor.matmul(PS[:, j, 0:NCOL], meanw[:, c, :], BIG[s[1]][:, c, cols], start=(c == 0), stop=(c == K2 - 1))
                        last.then_inc(mean_in, 1)

                    def variance(i, j):
                        pe.wait_ge(squared, i * 2 + (c0 + j + 1))
                        pe.wait_ge(std_out, i * 2 + (c0 + j + 1))
                        cols = bass.ds(i * (2 * NCOL) + j * NCOL, NCOL)
                        for c in range(K2):
                            last = nc.tensor.matmul(PS[:, 2 + j, 0:NCOL], meanw[:, c, :], BIG[s[3]][:, c, cols], start=(c == 0), stop=(c == K2 - 1))
                        last.then_inc(var_in, 1)

                    def body(i, final):
                        for j in range(2):
                            if not final:
                                mean(i + 1, j)
                            variance(i, j)

                    mean(0, 0)
                    mean(0, 1)
                    with pe.Fori(0, NGROUP // 2 - 1) as i:
                        body(i, False)
                    body(NGROUP // 2 - 1, True)
                elif s[0] == "table8":
                    weights_in(pe, n)
                    u = before(n, TR8) * BLOCKS
                    g0 = groups_before(n)
                    with pe.Fori(0, BLOCKS // TRS) as i:
                        for k in range(TRS):
                            pe.wait_ge(tr_in, i * TRS + (u + k + 1))
                            for q in range(4):
                                pe.wait_ge(mm_out, i * (4 * TRS) + (g0 + 4 * k + q + 1))
                                for c in range(K2):
                                    last = nc.tensor.matmul(PS[:, (4 * k + q) % 8, :], stage_in[:, k, c * P:(c + 1) * P],
                                                            wview["typ"][:, c, q * 512:(q + 1) * 512],
                                                            start=(c == 0), stop=(c == K2 - 1))
                                last.then_inc(mm_done, 1)
                            pe.wait_ge(mm_done, i * (4 * TRS) + (g0 + 4 * k + 4))
                            pe.sem_inc(tr_done, 1)
                elif s[0] == "fold":
                    begin(pe, n)
                    weights_in(pe, n)
                    for f, (a, b) in enumerate((("wq", "wk"), ("wv", "wp"))):
                        for c in range(K2):
                            for d in range(K2):
                                last = nc.tensor.matmul(PS[:, 2 * f + c, 0:D], wview[a][:, d, c * P:(c + 1) * P],
                                                        wview[b][:, d, :], start=(d == 0), stop=(d == K2 - 1))
                    last.then_inc(from_pe, 1)
                elif s[0] == "steps":
                    pe.wait_ge(to_pe, 1)
                    nc.tensor.matmul(PS[:, 0, 0:BLOCKS - 1], ones[:], counts[:, 0:BLOCKS - 1], start=True, stop=True).then_inc(from_pe, 1)
                    pe.wait_ge(to_pe, 2)
                    for a in range(2):
                        for c in range(CHUNKS):
                            last = nc.tensor.matmul(PS[:, 1 + a, c * P:(c + 1) * P], ones[:], diag[:, a, c * P:(c + 1) * P],
                                                    start=True, stop=True)
                    last.then_inc(from_pe, 1)
                    pe.wait_ge(to_pe, 3)
                    for bank, a in enumerate((0, 1, 4, 5, 6)):
                        for c in range(CHUNKS):
                            last = nc.tensor.matmul(PS[:, bank, :], attr[:, a, c * P:(c + 1) * P], pick[:, c, :],
                                                    start=(c == 0), stop=(c == CHUNKS - 1))
                    for bank, a in ((5, 2), (6, 3), (7, 0)):
                        for j in range(CHUNKS):
                            for c in range(CHUNKS):
                                last = nc.tensor.matmul(PS[:, bank, j * P:(j + 1) * P], pick[:, c, j * P:(j + 1) * P],
                                                        attr[:, a, c * P:(c + 1) * P], start=(c == 0), stop=(c == CHUNKS - 1))
                    last.then_inc(from_pe, 1)
                    pe.wait_ge(to_pe, 4)
                    for a in range(2):
                        for c in range(CHUNKS):
                            last = nc.tensor.transpose(PS[0:1, a, c * P:(c + 1) * P], has_col[:, a, c:c + 1], ident[:])
                    last.then_inc(from_pe, 1)
                elif s[0] == "softmax":
                    begin(pe, n)
                    t0, f0 = dve_hands(n), pe_hands(n)
                    for c in range(CHUNKS):
                        last = nc.tensor.transpose(PS[:, 0, c * P:(c + 1) * P], score[:, c * P:(c + 1) * P], ident[:])
                    last.then_inc(from_pe, 1)
                    for direction in range(2):
                        pe.wait_ge(to_pe, t0 + 2 * direction + 1)
                        for c in range(CHUNKS):
                            last = nc.tensor.transpose(PS[0:1, 1, c * P:(c + 1) * P], tail[:, c:c + 1], ident[:])
                        last.then_inc(from_pe, 1)
                        pe.wait_ge(to_pe, t0 + 2 * direction + 2)
                        for c in range(CHUNKS):
                            at = 2 * direction + c * P
                            last = nc.tensor.matmul(PS[:, 2, c:c + 1], carry[0:1, at:at + P], ones[0:1, 0:1], start=True, stop=True)
                        last.then_inc(from_pe, 1)
                    pe.wait_ge(to_pe, t0 + 5)
                    for c in range(CHUNKS):
                        last = nc.tensor.transpose(PS[:, 3, c * P:(c + 1) * P], sm_b[:, c, :], ident[:])
                    last.then_inc(from_pe, 1)
                elif s[0] == "maxpool":
                    begin(pe, n)
                    u = before(n, EDGE) * STEPS
                    g0 = before(n, GATHERS) * (STEPS // RING)
                    oh0 = before(n, EDGE) * (STEPS // 4)
                    m = before(n, ("maxpool",)) * STEPS
                    a0 = before(n, ("maxpool", "sum")) * STEPS

                    def to_features(i, h):
                        pe.wait_ge(win_max, i * QUADS + (m // 4 + h + 1))
                        for k4 in range(4):
                            k = 4 * h + k4
                            pe.wait_ge(gathered[k], i * 16 + 16 * (g0 + 1))
                            for c in range(K2):
                                last = nc.tensor.transpose(PS[:, 2 * (h % 2) + c, k4 * P:(k4 + 1) * P],
                                                           slot(k)[:, c * P:(c + 1) * P], ident[:])
                            last.then_inc(slot_free, 1)

                    def to_edges(i, k):
                        pe.wait_ge(back_in, i * RING + (m + k // 2 * 2 - 2 + 4))
                        for c in range(K2):
                            last = nc.tensor.transpose(PS[:, 4 + k // 2 % 2, k % 2 * D + c * P:k % 2 * D + (c + 1) * P],
                                                       window(k // 4 % 2, c)[:, (k % 4) * P:(k % 4 + 1) * P], ident[:])
                        last.then_inc(back_tr, 1)

                    def to_nodes(i, k):
                        pe.wait_ge(back_in, i * RING + (m + k // 2 * 2 + 2 + 4))
                        pe.wait_ge(added, i * RING + (a0 + k // 2 * 2 - 2 + 8))
                        nc.tensor.matmul(PS[:, 6 + k // 2 % 2, k % 2 * D:(k % 2 + 1) * D], ohot[:, k % OHS, :], back[:, k // 2 % 2, k % 2 * D:(k % 2 + 1) * D],
                                         start=True, stop=True).then_inc(summed, 1)

                    def body(i, final):
                        for h in range(QUADS):
                            pe.wait_ge(win_max, i * QUADS + (m // 4 + h + 1 + 2))
                            pe.wait_ge(oh_made, i * QUADS + (oh0 + h + 1))
                            for k in range(4 * h, 4 * h + 4):
                                to_edges(i, k)
                            if h < QUADS - 2:
                                to_features(i, h + 2)
                            elif not final:
                                to_features(i + 1, h + 2 - QUADS)
                            for k in range(4 * h, 4 * h + 4):
                                to_nodes(i, k)

                    to_features(0, 0)
                    to_features(0, 1)
                    with pe.Fori(0, STEPS // RING - 1) as i:
                        body(i, False)
                    body(STEPS // RING - 1, True)
                elif s[0] == "score":
                    begin(pe, n)
                    u = before(n, EDGE) * STEPS
                    oh0 = before(n, EDGE) * (STEPS // 4)
                    q = before(n, ("score",)) * STEPS

                    def turn(i, k):
                        if k % 4 == 0:
                            pe.wait_ge(oh_made, i * QUADS + (oh0 + k // 4 + 1))
                        pe.wait_ge(oht_in, i * RING + (q + k + 1))
                        nc.tensor.transpose(PSB[:, k % 2, 0:P], ohot_bf[:, k % OHS, :], identb[:]).then_inc(oh_tr, 1)

                    def body(i, final):
                        blocks = block_regs(pe, i * RING)
                        for k in range(RING):
                            if k < RING - 1:
                                turn(i, k + 1)
                            elif not final:
                                turn(i + 1, 0)
                            pe.wait_ge(oht_in, i * RING + (q + k + 1 + 2))
                            pe.wait_ge(slot_free, i * RING + (u + k + 1 - 4 + RING))
                            for part in range(3):
                                rows = G[:, bass.ds(blocks[k], 1), part, :].rearrange("p o d -> p (o d)")
                                last = nc.tensor.matmul(PS[:, 2 + k % 4, 0:D], ohT[:, k % 2, :], rhs=rows,
                                                        start=(part == 0), stop=(part == 2))
                            last.then_inc(expanded, 1)

                    turn(0, 0)
                    with pe.Fori(0, STEPS // RING - 1) as i:
                        body(i, False)
                    body(STEPS // RING - 1, True)
                elif s[0] in ("sum", "attend"):
                    begin(pe, n)
                    if s[0] == "attend":
                        pe.wait_ge(cleared, before(n, ("attend",)) + 1)
                    bodies = before(n, ("attend",)) * (STEPS // RING)
                    g0 = before(n, ("attend",) if s[0] == "attend" else GATHERS) * (STEPS // RING)
                    oh0 = before(n, EDGE) * (STEPS // 4)
                    a0 = before(n, ("maxpool", "sum")) * STEPS
                    with pe.Fori(0, STEPS // RING) as i:
                        for k in range(RING):
                            if k % 4 == 0:
                                pe.wait_ge(oh_made, i * QUADS + (oh0 + k // 4 + 1))
                            if s[0] == "sum":
                                pe.wait_ge(gathered[k], i * 16 + 16 * (g0 + 1))
                            elif k % 2 == 0:
                                pe.wait_ge(reloaded[k // 2], i * 16 + 16 * (g0 + 1))
                            if s[0] == "sum":
                                pe.wait_ge(added, i * RING + (a0 + k + 1 - 8 + 8))
                            else:
                                steps, taken = (SIDE, side_out) if (k - 8) % RING in SIDE else (MAIN, main_added)
                                pe.wait_ge(taken, i * len(steps) + ((bodies - (k < 8)) * len(steps)
                                                                    + list(steps).index((k - 8) % RING) + 1 + RING))
                            hot, rows = (ohot[:, k % OHS, :], slot(k)) if s[0] == "sum" else (weighted_hot[:, k, :], ring_h[:, k, :])
                            nc.tensor.matmul(PS[:, k % 8, 0:ROW], hot, rows, start=True, stop=True).then_inc(slot_free, 1)

        @block.vector
        def _(dve):
            done = [0]

            def link(ins):
                done[0] += 1
                ins.then_inc(vec, 1)
                dve.wait_ge(vec, done[0])

            V = nc.vector
            V.memset(ring[:, :, D:ROW], 1.0).then_inc(slot_free, RING)
            V.memset(rcol[:], 0.0).then_inc(mm_out, 4)
            for s_, c_ in ((tr_done, TRS), (tr_out, TRS), (win_max, 2), (back_tr, 8), (back_in, 4), (oh_tr, OHS),
                           (oht_in, 2), (expanded, 2), (summed, OHS), (low_made, TRS), (std_out, 2), (added, 8), (moved, 1), (main_added, RING),
                           (side_out, RING), (side_added, RING)):
                dve.sem_inc(s_, c_)

            def one_hots(i, h, loc, bf=False):
                to = (ohot_bf if bf else ohot)[:, 4 * h % OHS:4 * h % OHS + 4, :]
                at = loc[:, bass.ds(i * RING + 4 * h, 4)].rearrange("p (k o) -> p k o", o=1).to_broadcast([P, 4, P])
                row = iota_row[:].rearrange("p (o e) -> p o e", o=1).to_broadcast([P, 4, P])
                V.tensor_tensor(to, row, at, ALU.is_equal).then_inc(oh_made, 1)

            def weighted_one_hot(i, k):
                made = V.tensor_scalar(weighted_hot[:, k, :], iota_row[:], dloc[:, bass.ds(i * RING + k, 1)],
                                       score[:, bass.ds(i * RING + k, 1)], ALU.is_equal, ALU.mult)
                if k % 4 == 3:
                    made.then_inc(oh_made, 1)

            for n, s in enumerate(PLAN):
                if s[0] == "steps":
                    dve.wait_ge(consts, 3)
                    dve.wait_ge(loaded, 16 * 8)
                    bi, hi = BIASES.index("bi"), BIASES.index("hi")
                    link(V.tensor_tensor(bias[:, bi:bi + 3, :], bias[:, bi:bi + 3, :], bias[:, hi:hi + 3, :], ALU.add))
                    flat = [edge_int[:, a].rearrange("p c e -> p (c e)") for a in range(6)]
                    link(V.tensor_copy(attr[:, 0, :], flat[0]))
                    link(V.tensor_tensor(attr[:, 2, :], flat[0], flat[1], ALU.not_equal))
                    link(V.tensor_tensor(attr[:, 3, :], flat[0], flat[2], ALU.not_equal))
                    link(V.scalar_tensor_tensor(attr[:, 1, :], attr[:, 0, :], FAR, attr[:, 3, :], ALU.add, ALU.mult))
                    link(V.tensor_scalar(attr[:, 1, :], attr[:, 1, :], -FAR, None, ALU.add))
                    link(V.tensor_copy(attr[:, 4, :], flat[3]))
                    link(V.scalar_tensor_tensor(attr[:, 5, :], flat[4], float(NODES), flat[3], ALU.mult, ALU.add))
                    link(V.scalar_tensor_tensor(attr[:, 6, :], flat[3], float(REL8), flat[5], ALU.mult, ALU.add))
                    for b in range(1, BLOCKS):
                        link(V.tensor_scalar(scratch, attr[:, 0, :], float(b * P), 0.0, ALU.is_lt, ALU.add,
                                             accum_out=counts[:, b - 1:b]))
                    dve.sem_inc(to_pe, 1)
                    link(V.memset(bound[:, 0:1], 0.0))
                    link(V.memset(bound[:, BLOCKS:BLOCKS + 1], float(E)))
                    dve.wait_ge(from_pe, 1)
                    link(V.tensor_copy(bound[:, 1:BLOCKS], PS[:, 0, 0:BLOCKS - 1]))
                    link(V.tensor_copy(bound_i[:, 0, :], bound))
                    link(V.tensor_scalar(bound_i[:, 1, 0:BLOCKS], bound_i[:, 0, 1:BLOCKS + 1], -1.0, None, ALU.add))
                    link(V.tensor_scalar(bound_i[:, 0, :], bound_i[:, 0, :], 7, None, ALU.arith_shift_right))
                    link(V.tensor_scalar(bound_i[:, 1, 0:BLOCKS], bound_i[:, 1, 0:BLOCKS], 7, None, ALU.arith_shift_right))
                    first, cnt, cum, shift, step_d, ge = (small[:, j, 0:BLOCKS] for j in range(6))
                    link(V.tensor_copy(first, bound_i[:, 0, 0:BLOCKS]))
                    link(V.tensor_copy(cnt, bound_i[:, 1, 0:BLOCKS]))
                    link(V.scalar_tensor_tensor(cnt, cnt, 1.0, first, ALU.add, ALU.subtract))
                    link(V.tensor_tensor(ge, bound[:, 1:BLOCKS + 1], bound[:, 0:BLOCKS], ALU.is_gt))
                    link(V.tensor_tensor(cnt, cnt, ge, ALU.mult))
                    link(V.memset(ge, 1.0))
                    link(V.tensor_tensor_scan(cum, ge, cnt, 0.0, ALU.mult, ALU.add))
                    link(V.tensor_tensor(shift, first, cum, ALU.subtract))
                    link(V.tensor_tensor(shift, shift, cnt, ALU.add))
                    link(V.memset(step_d, 0.0))
                    link(V.tensor_tensor(step_d[:, 0:BLOCKS - 1], shift[:, 1:BLOCKS], shift[:, 0:BLOCKS - 1], ALU.subtract))
                    for c in range(CHUNKS):
                        link(V.tensor_scalar(ge, cum, tail[:, c:c + 1], 0.0, ALU.is_le, ALU.add, accum_out=where[:, 1, c:c + 1]))
                        link(V.tensor_tensor_reduce(ge2, ge, step_d, 1.0, 0.0, ALU.mult, ALU.add, where[:, 0, c:c + 1]))
                    link(V.tensor_tensor(where[:, 0, :], where[:, 0, :], tail[:], ALU.add))
                    link(V.tensor_scalar(where[:, 0, :], where[:, 0, :], float(TILES - 1), None, ALU.min))
                    for a in range(2):
                        for c in range(CHUNKS):
                            last = V.tensor_scalar(diag[:, a, c * P:(c + 1) * P], ident[:], where[:, a, c:c + 1], None, ALU.mult)
                    last.then_inc(to_pe, 1)
                    dve.wait_ge(from_pe, 2)
                    link(V.tensor_scalar(row128, PS[:, 2, :], float(P), None, ALU.mult))
                    link(V.tensor_scalar(blk[0:1, :], PS[0:1, 2, :], float(BLOCKS - 1), None, ALU.min))
                    for c in range(CHUNKS):
                        last = V.tensor_scalar(pick[:, c, :], PS[:, 1, :], tail[:, c:c + 1], None, ALU.is_equal)
                    last.then_inc(to_pe, 1)
                    dve.wait_ge(from_pe, 3)
                    link(V.tensor_tensor(dloc[:], PS[:, 0, :], row128, ALU.subtract))
                    link(V.tensor_tensor(eloc[:], PS[:, 1, :], row128, ALU.subtract))
                    for bank, name in ((2, "src"), (3, "rel"), (4, "typ")):
                        link(V.tensor_copy(idx[name][:], PS[:, bank, :]))
                    link(V.tensor_scalar(flat_of(rst_row), PS[:, 5, :], RESET, None, ALU.mult))
                    link(V.tensor_scalar(flat_of(end_row), PS[:, 6, :], RESET, None, ALU.mult))
                    link(V.tensor_scalar(where[:, 1, :], where[:, 1, :], float(P), None, ALU.mult))
                    link(V.tensor_scalar(reset_flat, PS[:, 5, :], RESET, None, ALU.mult))
                    dve.sem_inc(rows_ready, 1)
                    for c in range(CHUNKS):
                        last = V.tensor_scalar(val_row[:, c, :], PS[:, 7, c * P:(c + 1) * P], where[:, 1, c:c + 1], None, ALU.subtract)
                    link(last)
                    link(V.tensor_scalar(flat_of(sm_c), flat_of(val_row), 0.0, None, ALU.is_ge))
                    link(V.scalar_tensor_tensor(flat_of(val_row), flat_of(val_row), float(P), flat_of(sm_c), ALU.is_lt, ALU.mult))
                    link(V.tensor_reduce(has_col[:, 0, :], rst_row[:], AX_X, ALU.min))
                    V.tensor_reduce(has_col[:, 1, :], end_row[:], AX_X, ALU.min).then_inc(to_pe, 1)
                    dve.wait_ge(from_pe, 4)
                    V.tensor_copy(rowhas[0:1, :, :], PS[0:1, 0:2, :]).then_inc(rows_ready, 1)
                elif s[0] == "norm":
                    c0 = before(n, ("norm",)) * NGROUP
                    _, src, mid, _, dst, how = s

                    def wide_row(row):
                        return row.rearrange("p (o e) -> p o e", o=1).to_broadcast([P, K2, NCOL])

                    def centre(i, j):
                        dve.wait_ge(mean_in, i * 2 + (c0 + j + 1))
                        cols = bass.ds(i * (2 * NCOL) + j * NCOL, NCOL)
                        V.tensor_tensor(BIG[mid][:, :, cols], BIG[src][:, :, cols], wide_row(PS[:, j, 0:NCOL]), ALU.subtract)\
                         .then_inc(centred, 1)

                    def scale(i, j):
                        dve.wait_ge(std_out, i * 2 + (c0 + j + 1 + 2))
                        cols = bass.ds(i * (2 * NCOL) + j * NCOL, NCOL)
                        V.reciprocal(M[:, 0, cols], M[:, 0, cols]).then_inc(inverted, 1)
                        dve.wait_ge(inverted, i * 2 + (c0 + j + 1))
                        if how == "relu":
                            V.scalar_tensor_tensor(BIG[dst][:, :, cols], BIG[mid][:, :, cols], 0.0, wide_row(M[:, 0, cols]),
                                                   ALU.max, ALU.mult).then_inc(scaled, 1)
                        else:
                            for c in range(K2):
                                last = V.scalar_tensor_tensor(BIG[dst][:, c, cols], BIG[mid][:, c, cols], bias_of(how + "_g", c),
                                                              M[:, 0, cols], ALU.mult, ALU.mult)
                            last.then_inc(scaled, 1)

                    def body(i, final):
                        for j in range(2):
                            if not final:
                                centre(i + 1, j)
                            scale(i, j)

                    centre(0, 0)
                    centre(0, 1)
                    with dve.Fori(0, NGROUP // 2 - 1) as i:
                        body(i, False)
                    body(NGROUP // 2 - 1, True)
                    dve.wait_ge(scaled, c0 + NGROUP)
                    if how != "relu":
                        for c in range(K2):
                            last = V.tensor_scalar(BIG[dst][:, c, :], BIG[dst][:, c, :], bias_of(how + "_b", c), None, ALU.add)
                        last.then_inc(stage_done, 1)
                    else:
                        dve.sem_inc(stage_done, 1)
                elif s[0] == "add":
                    begin(dve, n)
                    V.tensor_tensor(BIG[s[1]][:, :, :], BIG[s[1]][:, :, :], BIG[s[2]][:, :, :], ALU.add).then_inc(stage_done, 1)
                elif s[0] == "dense" and len(s) == 7:
                    a, b, *how = s[6]
                    halves = halves_out(s)
                    g0 = groups_before(n)
                    j0 = sum(NGROUP for t in PLAN[:n] if t[0] == "dense" and len(t) == 7)
                    with dve.Fori(0, NGROUP // 2) as i:
                        for j in range(2):
                            cols = bass.ds(i * (2 * NCOL) + j * NCOL, NCOL)
                            dve.wait_ge(mm_out, i * (2 * halves) + (g0 + (j + 1) * halves + 4))
                            V.tensor_tensor(BIG[a][:, :, cols], BIG[a][:, :, cols], BIG[b][:, :, cols],
                                            ALU.mult if how == ["mul"] else ALU.add).then_inc(joined, 1)
                            if how == ["relu"]:
                                dve.wait_ge(joined, i * 2 + (j0 + j + 1))
                                V.tensor_scalar(BIG[a][:, :, cols], BIG[a][:, :, cols], 0.0, None, ALU.max).then_inc(clipped, 1)
                    if how == ["relu"]:
                        dve.wait_ge(clipped, (before(n, ("project",))) * NGROUP)
                    dve.wait_ge(joined, j0 + NGROUP)
                    dve.sem_inc(stage_done, 1)
                elif s[0] in TR:
                    u = before(n, TR8) * BLOCKS
                    v = before(n, TR) * BLOCKS
                    p0 = before(n, ("project",)) * BLOCKS

                    def low(i, k):
                        dve.wait_ge(mid_made, i * TRS + (p0 + k + 1))
                        V.tensor_tensor(part(i * TRS + k, 2), stage_out[:, k, :], part(i * TRS + k, 1), ALU.subtract).then_inc(low_made, 1)

                    with dve.Fori(0, BLOCKS // TRS) as i:
                        for k in range(TRS):
                            if s[0] == "project":
                                dve.wait_ge(high_made, i * TRS + (p0 + k + 1))
                                dve.wait_ge(low_made, i * TRS + (p0 + k + 1))
                                V.tensor_tensor(stage_out[:, k, :], PS[:, k, 0:D], part(i * TRS + k, 0), ALU.subtract).then_inc(tr_out, 1)
                                if k:
                                    low(i, k - 1)
                                continue
                            dve.wait_ge(tr_done, i * TRS + (u + k + 1 + TRS))
                            if s[0] == "table":
                                V.tensor_copy(A[:, bass.ds(i * TRS + k, 1), 0:D].rearrange("p o d -> p (o d)"), PS[:, k, 0:D]).then_inc(tr_out, 1)
                            else:
                                V.tensor_copy(BIG[s[2]][:, :, bass.ds(i * (TRS * P) + k * P, P)],
                                              PS[:, k, 0:D].rearrange("p (c e) -> p c e", c=K2)).then_inc(tr_out, 1)
                        if s[0] == "project":
                            low(i, TRS - 1)
                    if s[0] == "untranspose":
                        dve.wait_ge(tr_out, v + BLOCKS + TRS)
                        dve.sem_inc(stage_done, 1)
                    elif s[0] == "project":
                        dve.wait_ge(low_made, p0 + BLOCKS + TRS)
                        dve.sem_inc(stage_done, 1)
                elif s[0] == "table8":
                    begin(dve, n)
                    u = before(n, TR8) * BLOCKS
                    with dve.Fori(0, BLOCKS // TRS) as i:
                        for k in range(TRS):
                            dve.wait_ge(tr_done, i * TRS + (u + k + 1))
                            V.tensor_copy(stage_in[:, k, :].rearrange("p (c e) -> p c e", c=K2),
                                          H[:, :, bass.ds(i * (TRS * P) + k * P, P)]).then_inc(tr_in, 1)
                elif s[0] == "maxpool":
                    begin(dve, n)
                    u = before(n, EDGE) * STEPS
                    m = before(n, ("maxpool",)) * STEPS
                    a0 = before(n, ("maxpool", "sum")) * STEPS
                    link(V.memset(A, 0.0))

                    def scans(i, h):
                        dve.wait_ge(win_max, i * QUADS + (m // 4 + h + 2))
                        dve.wait_ge(back_tr, i * RING + (m + 4 * h + 4))
                        dve.wait_ge(slot_free, i * RING + (u + 4 * h + 4 + RING))
                        dve.wait_ge(reset_in[h % 2], i * 32 + 16 * (m // 8 + h // 2 + 1))
                        for c in range(K2):
                            last = V.tensor_tensor_scan(window(h % 2, c), resetw[:, h % 2, :], PS[:, 2 * (h % 2) + c, :],
                                                        window(1 - h % 2, c)[:, 4 * P - 1:4 * P], ALU.add, ALU.max)
                        last.then_inc(win_max, 1)
                        one_hots(i, h, eloc)

                    def body(i, final):
                        for h in range(QUADS):
                            if h < QUADS - 1:
                                scans(i, h + 1)
                            elif not final:
                                scans(i + 1, 0)
                            if h == 0:
                                blocks = block_regs(dve, i * RING)
                            for k in range(4 * h, 4 * h + 4):
                                dve.wait_ge(summed, i * RING + (m + k // 2 * 2 + 2 + OHS))
                                dve.wait_ge(added, i * RING + (a0 + k + 8))
                                to = A[:, bass.ds(blocks[k], 1), 0:D].rearrange("p o d -> p (o d)")
                                V.tensor_tensor(to, to, PS[:, 6 + k // 2 % 2, k % 2 * D:(k % 2 + 1) * D], ALU.add).then_inc(added, 1)

                    scans(0, 0)
                    with dve.Fori(0, STEPS // RING - 1) as i:
                        body(i, False)
                    body(STEPS // RING - 1, True)
                    dve.wait_ge(added, a0 + STEPS + 8)
                    dve.sem_inc(stage_done, 1)
                elif s[0] == "score":
                    begin(dve, n)
                    u = before(n, EDGE) * STEPS
                    g0 = before(n, GATHERS) * (STEPS // RING)
                    q = before(n, ("score",)) * STEPS

                    def body(i, final):
                        dve.wait_ge(moved, i + (q // RING + 1))
                        for h in range(QUADS):
                            for k in range(4 * h, 4 * h + 4):
                                dve.wait_ge(expanded, i * RING + (q + k + 1 + 2))
                                dve.wait_ge(gathered[k], i * 16 + 16 * (g0 + 1))
                                dve.wait_ge(slot_free, i * RING + (u + k + RING))
                                V.tensor_tensor_reduce(junk, PS[:, 2 + k % 4, 0:D], slot(k)[:, 0:D], 1.0, 0.0,
                                                       ALU.mult, ALU.add, score8[:, k:k + 1]).then_inc(slot_free, 1)
                            if h < QUADS - 2:
                                one_hots(i, h + 2, dloc, bf=True)
                            elif not final:
                                one_hots(i + 1, h + 2 - QUADS, dloc, bf=True)
                        dve.wait_ge(slot_free, i * RING + (u + RING + RING))
                        V.tensor_copy(score[:, bass.ds(i * RING, RING)], score8[:]).then_inc(moved, 1)

                    for h in range(2):
                        one_hots(0, h, dloc, bf=True)
                    with dve.Fori(0, STEPS // RING - 1) as i:
                        body(i, False)
                    body(STEPS // RING - 1, True)
                elif s[0] in ("sum", "attend"):
                    begin(dve, n)
                    u = before(n, EDGE) * STEPS
                    a0 = before(n, ("maxpool", "sum")) * STEPS
                    bodies = before(n, ("attend",)) * (STEPS // RING)
                    if s[0] == "sum":
                        link(V.memset(A, 0.0))
                        link(V.memset(ring[:, :, D:ROW], 1.0))
                        link(V.memset(ring_c[:, :, D:ROW], 1.0))
                    else:
                        dve.wait_ge(cleared, before(n, ("attend",)) + 1)

                    def body(i, final):
                        blocks = block_regs(dve, i * RING)
                        for k in range(RING):
                            to = A[:, bass.ds(blocks[k], 1), :].rearrange("p o d -> p (o d)")
                            if s[0] == "sum" or k in MAIN:
                                dve.wait_ge(slot_free, i * RING + (u + k + 1 + RING))
                            if s[0] == "sum":
                                dve.wait_ge(added, i * RING + (a0 + k + 8))
                                V.tensor_tensor(to, to, PS[:, k % 8, 0:ROW], ALU.add).then_inc(added, 1)
                                if k % 4 == 3 and k // 4 < QUADS - 2:
                                    one_hots(i, k // 4 + 2, dloc)
                                elif k % 4 == 3 and not final:
                                    one_hots(i + 1, k // 4 + 2 - QUADS, dloc)
                                continue
                            if k in MAIN:
                                dve.wait_ge(main_added, i * len(MAIN) + (bodies * len(MAIN) + MAIN.index(k) + RING))
                                V.tensor_tensor(to, to, PS[:, k % 8, 0:ROW], ALU.add).then_inc(main_added, 1)
                            if k < 4 or not final:
                                dve.wait_ge(slot_free, i * RING + (u + k - 4 + 1 + RING))
                                weighted_one_hot(i if k < 4 else i + 1, (k + 12) % RING)

                    if s[0] == "sum":
                        for h in range(2):
                            one_hots(0, h, dloc)
                    else:
                        for k in range(12):
                            weighted_one_hot(0, k)
                    with dve.Fori(0, STEPS // RING - 1) as i:
                        body(i, False)
                    body(STEPS // RING - 1, True)
                    if s[0] == "attend":
                        dve.wait_ge(main_added, (bodies + STEPS // RING) * len(MAIN) + RING)
                        dve.wait_ge(side_added, (bodies + STEPS // RING) * len(SIDE) + RING)
                        link(V.tensor_tensor(A, A, A2, ALU.add))
                    else:
                        dve.wait_ge(added, a0 + STEPS + 8)
                    total = A[:, :, D:ROW].rearrange("p b o -> p (b o)")
                    if s[0] == "attend":
                        link(V.tensor_scalar(rcol[:], total, SM_EPS, None, ALU.add))
                    else:
                        link(V.tensor_scalar(rcol[:], total, 1.0, None, ALU.max))
                    V.reciprocal(rcol[:], rcol[:]).then_inc(stage_done, 1)
                elif s[0] == "softmax":
                    f0 = pe_hands(n)
                    dve.wait_ge(from_pe, f0 + 1)
                    link(V.tensor_scalar(flat_of(sm_c), flat_of(val_row), -1.0, -LOW, ALU.add, ALU.mult))
                    link(V.tensor_tensor(flat_of(sm_b), PS[:, 0, :], flat_of(sm_c), ALU.add))
                    for c in range(CHUNKS):
                        last = V.tensor_tensor_scan(sm_a[:, c, :], rst_row[:, c, :], sm_b[:, c, :], LOW, ALU.add, ALU.max)
                    link(last)
                    V.tensor_copy(tail[:], sm_a[:, :, P - 1]).then_inc(to_pe, 1)
                    dve.wait_ge(from_pe, f0 + 2)
                    V.tensor_tensor_scan(carry[0:1, 1:SPAD + 1], rowhas[0:1, 0, :], PS[0:1, 1, :], LOW, ALU.add, ALU.max).then_inc(to_pe, 1)
                    dve.wait_ge(from_pe, f0 + 3)
                    link(V.tensor_copy(carry_col[:], PS[:, 2, 0:CHUNKS]))
                    for c in range(CHUNKS):
                        last = V.tensor_tensor_scan(sm_a[:, c, :], rst_row[:, c, :], sm_b[:, c, :], carry_col[:, c:c + 1], ALU.add, ALU.max)
                    link(last)
                    for c in range(CHUNKS):
                        last = V.tensor_tensor_scan(sm_c[:, c, ::-1], end_row[:, c, ::-1], sm_a[:, c, ::-1], LOW, ALU.add, ALU.max)
                    link(last)
                    V.tensor_copy(tail[:], sm_c[:, :, 0]).then_inc(to_pe, 1)
                    dve.wait_ge(from_pe, f0 + 4)
                    V.tensor_tensor_scan(carry[0:1, SPAD:0:-1], rowhas[0:1, 1, ::-1], PS[0:1, 1, ::-1], LOW, ALU.add, ALU.max).then_inc(to_pe, 1)
                    dve.wait_ge(from_pe, f0 + 5)
                    link(V.tensor_copy(carry_col[:], PS[:, 2, 0:CHUNKS]))
                    for c in range(CHUNKS):
                        last = V.tensor_tensor_scan(sm_c[:, c, ::-1], end_row[:, c, ::-1], sm_a[:, c, ::-1], carry_col[:, c:c + 1], ALU.add, ALU.max)
                    link(last)
                    link(V.tensor_tensor(flat_of(sm_c), flat_of(sm_b), flat_of(sm_c), ALU.subtract))
                    V.tensor_scalar(flat_of(sm_c), flat_of(sm_c), 50.0, -50.0, ALU.min, ALU.max).then_inc(arg_ready, 1)
                    dve.wait_ge(exp_done, before(n, ("softmax",)) + 1)
                    link(V.tensor_tensor(flat_of(sm_b), flat_of(sm_a), flat_of(val_row), ALU.mult))
                    V.tensor_scalar(flat_of(sm_b), flat_of(sm_b), 0.0, None, ALU.max).then_inc(to_pe, 1)
                    dve.wait_ge(from_pe, f0 + 6)
                    V.tensor_copy(score[:], PS[:, 3, :]).then_inc(stage_done, 1)


def edge_rows(src, dst, type2, type8):
    import numpy as np

    pad = SPAD * P - E
    d = np.concatenate([np.full(1, -1, np.int32), dst, np.full(pad + 1, 9999, np.int32)])
    zero = np.zeros(pad, np.int32)
    rest = [np.concatenate([a, zero]) for a in (src, type2, type8)]
    return np.stack([d[1:-1], d[:-2], d[2:], *rest])


def kernel(**inputs):
    import numpy as np
    import concourse.bacc as bacc
    from concourse.bass_utils import run_bass_kernel_spmd

    a = {k: np.asarray(v) for k, v in inputs.items()}

    def halves(w):
        return w.reshape(w.shape[0] // P, P, w.shape[1]).transpose(1, 0, 2)

    def group(ws):
        return np.concatenate([halves(w).reshape(P, -1) for w in ws], axis=1)

    x = a["x"]
    xT = np.zeros((D, NODES), x.dtype)
    xT[:, :N] = x.T
    xT = np.ascontiguousarray(halves(xT))
    ih = a["L2_gnn_W_ih"]
    w = [
        group([a["L0_gnn_Wp1"].T, a["L0_gnn_Wm1"].T, a["L0_gnn_Wm2"].T, a["L0_gnn_Wm3"].T,
               a["L1_gnn_w_in"]])[None],
        np.stack([group([a["L1_gnn_wq"][i].T, a["L1_gnn_wk"][i].T, a["L1_gnn_wv"][i].T, a["L1_gnn_wp"][i]]) for i in range(LAYERS)]),
        group([a["L2_gnn_W_rel"][0].T, a["L2_gnn_W_rel"][1].T, ih[0:D].T, ih[2 * D:3 * D].T, ih[3 * D:4 * D].T,
               a["L2_gnn_W1"].T, a["L2_gnn_W2"].T, a["L2_gnn_W3"].T])[None],
        group([a["L3_gnn_weight"].transpose(1, 0, 2).reshape(D, REL8 * D), a["L3_gnn_sl_w"].T])[None],
    ]
    bih, bhh = a["L2_gnn_b_ih"], a["L2_gnn_b_hh"]
    b = [a["L0_gnn_bp1"], a["L0_gnn_bm1"], a["L0_gnn_bm2"], a["L0_gnn_bm3"], a["L0_gnn_ln2_g"], a["L0_gnn_ln2_b"],
         a["L0_gnn_ln3_g"], a["L0_gnn_ln3_b"], a["L1_gnn_b_in"], *a["L1_gnn_bp"], *a["L2_gnn_b_rel"],
         bih[0:D], bih[2 * D:3 * D], bih[3 * D:], bhh[0:D], bhh[2 * D:3 * D], bhh[3 * D:],
         a["L2_gnn_b1"], a["L2_gnn_b2"], a["L2_gnn_b3"], a["L3_gnn_sl_b"]]
    bias = np.zeros((len(b), D), x.dtype)
    for i, v in enumerate(b):
        bias[i, :len(v)] = v
    bias = np.ascontiguousarray(bias.reshape(len(b), K2, P).transpose(2, 0, 1))

    nc = bacc.Bacc("TRN2", target_bir_lowering=False, num_devices=1)
    arrays = {}

    def put(name, v):
        arrays[name] = np.ascontiguousarray(v)
        return nc.dram_tensor(name, v.shape, mybir.dt.from_np(v.dtype), kind="ExternalInput").ap()

    e = put("edges", edge_rows(a["src"], a["dst"], a["edge_type_2"], a["edge_type_8"]))
    args = [e, put("xT", xT), [put(f"w{i}", v) for i, v in enumerate(w)], put("bias_in", bias)]
    args.append(nc.dram_tensor("outT", (P, K2, N), F32, kind="ExternalOutput").ap())
    for name, shape, dt in (("table", (NODES, D), F32), ("table_rel", (REL2 * NODES, D), F32),
                            ("table_typ", (REL8 * NODES, D), F32), ("spill", (STEPS, P, D), F32), ("resets", (SPAD, P), BF16)):
        args.append(nc.dram_tensor(name, shape, dt, kind="Internal").ap())
    gnn_kernel(nc, *args)
    r = run_bass_kernel_spmd(nc, [arrays], core_ids=[0])
    got = r.results[0]["outT"]
    return np.ascontiguousarray(got.transpose(2, 1, 0).reshape(N, D))
```
